# Optimizing a Trainium2 kernel written in Bass

```python
import numpy as np
import jax
import jax.numpy as jnp

def _softmax(x, axis=-1):
    return jax.nn.softmax(x, axis=axis)

def _gelu(x):
    return jax.nn.gelu(x, approximate=True)

def _silu(x):
    return jax.nn.silu(x)

def _sigmoid(x):
    return jax.nn.sigmoid(x)

def _layernorm(x, axis=-1, eps=1e-05):
    m = jnp.mean(x, axis=axis, keepdims=True)
    v = jnp.var(x, axis=axis, keepdims=True)
    return (x - m) / jnp.sqrt(v + eps)

def _scatter_add(tgt, idx, src, axis=0):
    return tgt.at[idx].add(src)

def _segment_sum(src, seg, n):
    return jax.ops.segment_sum(src, seg, n)
kernel_name = 'mk_gnn_ffn_d1_gnn_r8_7f435f'

def setup_inputs(seed: int=0):
    np.random.seed(seed)
    _w = jnp.asarray

    def _rec_inputs():
        import jax
        import jax.numpy as jnp
        _gk = jax.random.key(seed)
        x = -0.0006008 + 1.001 * jax.random.normal(jax.random.fold_in(_gk, 1), (6250, 256), jnp.float32)
        _s = jax.random.randint(jax.random.fold_in(_gk, 2), (50000,), 0, 6250, jnp.int32)
        _d = jax.random.randint(jax.random.fold_in(_gk, 3), (50000,), 0, 6250, jnp.int32)
        _loop = jnp.arange(6250, dtype=jnp.int32)
        src = jnp.concatenate([_s, _d, _loop])
        dst = jnp.concatenate([_d, _s, _loop])
        _o = jnp.argsort(dst, stable=True)
        src = src[_o]
        dst = dst[_o]
        return (x, src, dst)
    x, src, dst = _rec_inputs()

    def _L0_gnn_setup():
        import jax, jax.numpy as jnp
        import numpy as np
        N_NODES = 1250
        N_EDGES = 20000
        D = 256
        P = 2.0
        key = jax.random.key(seed)
        k1, k2, k3, k4 = jax.random.split(key, 4)
        X = jax.random.normal(k1, (N_NODES, D), dtype=jnp.float32)
        edge_index = jax.random.randint(k2, (2, N_EDGES), 0, N_NODES, dtype=jnp.int64)
        scale = 1.0 / np.sqrt(D)
        W_root = jax.random.normal(k3, (D, D), dtype=jnp.float32) * scale
        W_neigh = jax.random.normal(k4, (D, D), dtype=jnp.float32) * scale
        b = jnp.zeros((D,), dtype=jnp.float32)
        return {'X': X, 'edge_index': edge_index, 'W_root': W_root, 'W_neigh': W_neigh, 'b': b}
    _L0_gnn_all = _L0_gnn_setup()
    _L0_gnn_in = {k: v for k, v in _L0_gnn_all.items() if k in ('W_root', 'W_neigh', 'b')}
    del _L0_gnn_all

    def _L0_ffn_setup():
        import jax, jax.numpy as jnp
        import numpy as np
        NUM_EXPERTS = 8
        TOP_K = 2
        B, S, D = (8, 1024, 256)

        def _moe(tokens, router_w, w1, b1, w2, b2):
            N = tokens.shape[0]
            E = router_w.shape[0]
            logits = tokens.astype(jnp.float32) @ router_w.astype(jnp.float32).T
            probs = jax.nn.softmax(logits, axis=-1)
            rw, re = jax.lax.top_k(probs, TOP_K)
            if TOP_K > 1:
                rw = rw / jnp.maximum(rw.sum(-1, keepdims=True), 1e-12)
            rw = rw.astype(tokens.dtype)
            combine = jnp.zeros((N, E), tokens.dtype).at[jnp.arange(N)[:, None], re].set(rw)
            out = tokens
            for e in range(E):
                h = jax.nn.gelu(tokens @ w1[e] + b1[e], approximate=False)
                y = h @ w2[e] + b2[e]
                out = out + combine[:, e:e + 1] * y
            return out
        key = jax.random.key(seed)
        ks = jax.random.split(key, 4)
        scale = 1.0 / np.sqrt(D).astype(np.float32)
        return {'input_embeddings': jax.random.normal(ks[0], (B, S, D), jnp.float32), 'router_w': jax.random.normal(ks[1], (NUM_EXPERTS, D), jnp.float32) * scale, 'w1': jax.random.normal(ks[2], (NUM_EXPERTS, D, D), jnp.float32) * scale, 'b1': jnp.zeros((NUM_EXPERTS, D), jnp.float32), 'w2': jax.random.normal(ks[3], (NUM_EXPERTS, D, D), jnp.float32) * scale, 'b2': jnp.zeros((NUM_EXPERTS, D), jnp.float32)}
    _L0_ffn_all = _L0_ffn_setup()
    _L0_ffn_in = {k: v for k, v in _L0_ffn_all.items() if k in ('router_w', 'w1', 'b1', 'w2', 'b2')}
    del _L0_ffn_all
    return {'x': x, 'src': src, 'dst': dst, 'L0_gnn_W_root': _L0_gnn_in['W_root'], 'L0_gnn_W_neigh': _L0_gnn_in['W_neigh'], 'L0_gnn_b': _L0_gnn_in['b'], 'L0_ffn_router_w': _L0_ffn_in['router_w'], 'L0_ffn_w1': _L0_ffn_in['w1'], 'L0_ffn_b1': _L0_ffn_in['b1'], 'L0_ffn_w2': _L0_ffn_in['w2'], 'L0_ffn_b2': _L0_ffn_in['b2']}

def reference(x, src, dst, L0_gnn_W_root, L0_gnn_W_neigh, L0_gnn_b, L0_ffn_router_w, L0_ffn_w1, L0_ffn_b1, L0_ffn_w2, L0_ffn_b2):
    import jax
    import jax.numpy as jnp

    def _L0_gnn_ref(X, edge_index, W_root, W_neigh, b):
        import jax, jax.numpy as jnp
        import numpy as np
        N_NODES = 1250
        N_EDGES = 20000
        D = 256
        P = 2.0
        n = X.shape[0]
        row, col = (edge_index[0], edge_index[1])
        ones = jnp.ones((row.shape[0],), dtype=X.dtype)
        deg = jax.ops.segment_sum(ones, row, num_segments=n)
        denom = jnp.maximum(deg, 1.0)[:, None]
        neigh_sum = jax.ops.segment_sum(X[col], row, num_segments=n)
        neigh_mean = neigh_sum / denom
        H = jax.nn.relu(X @ W_root + neigh_mean @ W_neigh + b)
        diffs = jnp.abs(H[row] - H[col]) ** P
        gg = jax.ops.segment_sum(diffs, row, num_segments=n) / denom
        return jnp.tanh(gg)

    def _L0_ffn_ref(input_embeddings, router_w, w1, b1, w2, b2):
        import jax, jax.numpy as jnp
        import numpy as np
        NUM_EXPERTS = 8
        TOP_K = 2
        B, S, D = (8, 1024, 256)

        def _moe(tokens, router_w, w1, b1, w2, b2):
            N = tokens.shape[0]
            E = router_w.shape[0]
            logits = tokens.astype(jnp.float32) @ router_w.astype(jnp.float32).T
            probs = jax.nn.softmax(logits, axis=-1)
            rw, re = jax.lax.top_k(probs, TOP_K)
            if TOP_K > 1:
                rw = rw / jnp.maximum(rw.sum(-1, keepdims=True), 1e-12)
            rw = rw.astype(tokens.dtype)
            combine = jnp.zeros((N, E), tokens.dtype).at[jnp.arange(N)[:, None], re].set(rw)
            out = tokens
            for e in range(E):
                h = jax.nn.gelu(tokens @ w1[e] + b1[e], approximate=False)
                y = h @ w2[e] + b2[e]
                out = out + combine[:, e:e + 1] * y
            return out
        b, s, d = input_embeddings.shape
        tokens = input_embeddings.reshape(b * s, d)
        return _moe(tokens, router_w, w1, b1, w2, b2).reshape(b, s, d)
    edge_index = jnp.stack([src, dst])
    x = x + _L0_gnn_ref(_layernorm(x, axis=-1), edge_index, L0_gnn_W_root, L0_gnn_W_neigh, L0_gnn_b)
    x = x + _L0_ffn_ref(_layernorm(x, axis=-1)[None], L0_ffn_router_w, L0_ffn_w1, L0_ffn_b1, L0_ffn_w2, L0_ffn_b2)[0]
    return x

_drawn_inputs = setup_inputs


def setup_inputs(seed=0):
    import zlib

    import numpy as np

    out = dict(_drawn_inputs(seed))
    spreads = {'L0_gnn_b': (0.0, 0.1), 'L0_ffn_b1': (0.0, 0.338), 'L0_ffn_b2': (0.0, 0.1)}
    factors = {}
    for name, (base, spread) in spreads.items():
        noise = np.random.default_rng([zlib.crc32(name.encode()), seed]).standard_normal(out[name].shape)
        drawn = base * np.exp(spread * noise) if base else spread * noise
        out[name] = jnp.asarray(drawn.astype(out[name].dtype))
    for name, factor in factors.items():
        out[name] = (out[name] * factor).astype(out[name].dtype)
    return out
```

```python
import concourse.bass as bass
from concourse import mybir
from concourse.alu_op_type import AluOpType as ALU
from contextlib import ExitStack

P = 128
N_NODES = 6250
D = 256
N_EDGES = 106250
N_EXP = 8
EPS = 1e-5
BLOCKS = -(-N_NODES // P)
LAST_ROWS = N_NODES - (BLOCKS - 1) * P
EDGE_COLS = N_EDGES // P
EDGE_REST = N_EDGES - EDGE_COLS * P
IN_UNROLL = 4
IN_COLS = -(-(EDGE_COLS + 1) // IN_UNROLL) * IN_UNROLL
POOL_COLS = 352
GROUP = 8
MAX_CHUNKS = -(-N_EDGES // P) + BLOCKS - 1
TURN = 2 * GROUP
CHUNKS = -(-MAX_CHUNKS // TURN) * TURN
HALF = CHUNKS // 2
NOWHERE = 1 << 18
COL_BIAS = 0x3000
BLK_COLS = -(-(CHUNKS + GROUP) // P) * P
TBLK = 7
TGRP = BLOCKS // TBLK
TOK = TBLK * P // 2
ACC_BUFS = 4
assert BLOCKS % TBLK == 0 and HALF <= 512 and TOK <= 512


def gnn_moe(nc, x, src, dst, w_root, w_neigh, gnn_b, router_w, w1, b1, w2, b2, out):
    f32, i32, u8 = mybir.dt.float32, mybir.dt.int32, mybir.dt.uint8
    bf16, f16, u32 = mybir.dt.bfloat16, mybir.dt.float16, mybir.dt.uint32
    ACT, AX = mybir.ActivationFunctionType, mybir.AxisListType
    ds = bass.ds

    ctx = ExitStack()
    with ctx:
        def sb(name, shape, dt):
            return ctx.enter_context(nc.sbuf_tensor(name, shape, dt))

        def pb(name, shape, dt):
            return ctx.enter_context(nc.psum_tensor(name, shape, dt))

        def sem(name):
            return ctx.enter_context(nc.semaphore(name))

        xn_dram = nc.dram_tensor("xn_rows", (BLOCKS * P, D), f32).ap()
        h_dram = nc.dram_tensor("h_rows", (BLOCKS * P, D), f32).ap()
        pair_dram = nc.dram_tensor("sorted_pairs", (P * CHUNKS, 2), f32).ap()
        blk_dram = nc.dram_tensor("chunk_block", (BLK_COLS,), i32).ap()

        rows = sb("rows", [P, BLOCKS, 2 * D + 1], f32)
        big = sb("big", [P, BLOCKS * IN_COLS // 4], f32)
        masks = big[:, :].bitcast(u8).rearrange("p (b c) -> p b c", b=BLOCKS)
        wsize = N_EXP * 2 * D
        w1_sb = big[:, 0:wsize].rearrange("p (e k f) -> p e k f", e=N_EXP, k=2)
        w2_sb = big[:, wsize:2 * wsize].rearrange("p (e k f) -> p e k f", e=N_EXP, k=2)
        wr_sb = sb("wr_sb", [P, 2, D], f32)
        wn_sb = sb("wn_sb", [P, 2, D], f32)
        gb_sb = sb("gb_sb", [1, D], f32)
        rw_sb = sb("rw_sb", [P, 2, N_EXP], f32)
        b1_sb = sb("b1_sb", [P, N_EXP, 2], f32)
        b2_sb = sb("b2_sb", [N_EXP, D], f32)

        iota_h = sb("iota_h", [P, CHUNKS], f16)
        iota1_f = sb("iota1_f", [P, P], f32)
        iota8_f = sb("iota8_f", [P, N_EXP], f32)
        kpos_i = sb("kpos_i", [P, BLK_COLS // P], i32)
        kpos_f = sb("kpos_f", [P, BLK_COLS // P], f32)
        ident = sb("ident", [P, P], f32)
        upper = sb("upper", [P, P], f32)
        ones = sb("ones", [P, P], f32)
        zero_bf = sb("zero_bf", [P, HALF], bf16)
        eps_t = sb("eps_t", [P, 1], f32)

        ring = sb("ring", [P, TURN, 2 * D], f32)
        rflat = ring[:, :, :].rearrange("p a b -> p (a b)")
        o = 0
        dst_i = rflat[:, o:o + IN_COLS].bitcast(i32); o += IN_COLS
        hi_f = rflat[:, o:o + IN_COLS]; o += IN_COLS
        lo_f = rflat[:, o:o + IN_COLS]; o += IN_COLS
        rowlo_f = rflat[:, o:o + IN_COLS]; o += IN_COLS
        colbits = rflat[:, o:o + IN_COLS]; o += IN_COLS
        pos_f = rflat[:, o:o + IN_COLS]; o += IN_COLS
        tmp_i = rflat[:, o:o + IN_COLS].bitcast(i32); o += IN_COLS
        pair_f = rflat[:, o:o + 2 * POOL_COLS].rearrange("p (c w) -> p c w", w=2)
        src_i = rflat[:, o:o + IN_COLS].bitcast(i32); o += IN_COLS
        blk_f = rflat[:, o:o + IN_COLS]; o += IN_COLS
        place_i = tmp_i
        assert o <= TURN * 2 * D
        onehot = sb("onehot", [P, 2, GROUP, P], f32)
        oflat = onehot[:, :, :, :].rearrange("p a b c -> p (a b c)").bitcast(bf16)
        hi_oh = sb("hi_oh", [P, IN_UNROLL, CHUNKS], bf16)
        lo_col = oflat[:, 0:IN_UNROLL * P].rearrange("p (a b) -> p a b", a=IN_UNROLL)
        lo_row = oflat[:, IN_UNROLL * P:2 * IN_UNROLL * P].rearrange("p (a b) -> p a b", a=IN_UNROLL)

        idx_i = sb("idx_i", [P, CHUNKS], i32)
        erow = sb("erow", [P, CHUNKS + TURN], f32)
        blk_row = big[0:1, 2 * wsize:2 * wsize + BLK_COLS].bitcast(i32)
        stage = sb("stage", [P, 2, GROUP], i32)
        pair_stage = sb("pair_stage", [P, 2, GROUP, 2], f32)
        merged = big[:, 0:2 * CHUNKS].rearrange("p (c w) -> p c w", w=2)

        iota_i = idx_i
        hflat = hi_oh[:, :, :].rearrange("p a b -> p (a b)").bitcast(f32)
        qb = BLK_COLS // P * BLOCKS
        cmp_f = hflat[:, D:D + qb].rearrange("p (q b) -> p q b", b=BLOCKS)
        picked = onehot[:, :, :, :].rearrange("p a b c -> p (a b c)")[:, 0:2 * IN_COLS].rearrange("p (a c) -> p a c", a=2)
        operand = rflat[:, 0:4 * D].rearrange("p (a d) -> p a d", a=2)
        tr_sb = rflat[:, 4 * D:4 * D + 8 * P].rearrange("p (a k r) -> p a k r", a=2, k=4)
        counts = sb("counts", [P, BLOCKS], f32)
        tot_i = sb("tot_i", [P, BLOCKS], i32)
        nch_f = sb("nch_f", [P, BLOCKS], f32)
        start_f = sb("start_f", [P, BLOCKS + 1], f32)
        off_f = sb("off_f", [P, BLOCKS], f32)
        blk_cf = sb("blk_cf", [P, BLK_COLS // P], f32)
        blk_ci = sb("blk_ci", [P, BLK_COLS // P], i32)

        G7 = TBLK * D
        xg = rflat[:, 0:G7].rearrange("p (j d) -> p j d", j=TBLK)
        hg = rflat[:, G7:2 * G7].rearrange("p (j d) -> p j d", j=TBLK)
        ug = rflat[:, 2 * G7:3 * G7].rearrange("p (j d) -> p j d", j=TBLK)
        xT = rflat[:, 3 * G7:4 * G7].rearrange("p (k t) -> p k t", k=2)
        xT_flat = rflat[:, 3 * G7:4 * G7]
        combT = rflat[0:N_EXP, 4 * G7:4 * G7 + TBLK * P]
        hT = [onehot[:, :, :, :].rearrange("p a b c -> p (a b c)")[:, 0:G7].rearrange("p (k t) -> p k t", k=2),
              big[:, 2 * wsize:2 * wsize + G7].rearrange("p (k t) -> p k t", k=2)]
        bn6 = sb("bn6", [P, TBLK, 6], f32)
        mv = sb("mv", [P, TBLK, 2], f32)
        t7 = sb("t7", [P, 8, TBLK], f32)
        lg = sb("lg", [P, 2, TBLK, N_EXP], f32)
        top8 = sb("top8", [P, TBLK, 8], f32)
        idx8 = sb("idx8", [P, TBLK, 8], u32)
        idx8f = sb("idx8f", [P, 2, TBLK], f32)
        comb = sb("comb", [P, TBLK, N_EXP], f32)

        sums = sb("sums", [P, BLOCKS], f32)
        nmean = sb("nmean", [P, BLOCKS], f32)
        ssq = sb("ssq", [P, BLOCKS], f32)
        std = sb("std", [P, BLOCKS], f32)
        rstd = sb("rstd", [P, BLOCKS], f32)
        nmr = sb("nmr", [P, BLOCKS], f32)
        deg = sb("deg", [P, BLOCKS], f32)
        rden = sb("rden", [P, BLOCKS], f32)

        ps = pb("ps", [P, 8 * 512], f32)
        bank = [ps[:, 512 * i:512 * (i + 1)] for i in range(8)]

        pairs_zero, pairs_ready, pairs_staged = sem("pairs_zero"), sem("pairs_ready"), sem("pairs_staged")
        pairs_loaded = sem("pairs_loaded")
        scattered = [sem(f"scattered{i}") for i in range(2 * GROUP)]
        tail_turn = sem("tail_turn")
        tail_step = sem("tail_step")
        placed, pos_ready = sem("placed"), sem("pos_ready")
        pad_set = sem("pad_set")
        s_edges, s_x, s_w = sem("s_edges"), sem("s_x"), sem("s_w")
        pool_step, consts = sem("pool_step"), sem("consts")
        dve_step = sem("dve_step")
        sums_done, ssq_done, std_done = sem("sums_done"), sem("ssq_done"), sem("std_done")
        rstd_ready, xn_done, xn_stored = sem("rstd_ready"), sem("xn_done"), sem("xn_stored")
        act_step = sem("act_step")
        mask_done, scan_done, pick_done = sem("mask_done"), sem("scan_done"), sem("pick_done")
        counts_ready, totals_done = sem("counts_ready"), sem("totals_done")
        oh_ready, sorted_cols = sem("oh_ready"), sem("sorted_cols")
        blk_ready, blk_stored, blk_loaded = sem("blk_ready"), sem("blk_stored"), sem("blk_loaded")
        sort_ready = sem("sort_ready")
        rows_zero, oh_made, mult_done, added = sem("rows_zero"), sem("oh_made"), sem("mult_done"), sem("added")
        gathered = [sem(f"gathered{i}") for i in range(TURN)]
        staged, squared, pool_turn = sem("staged"), sem("squared"), sem("pool_turn")
        deg_ready, mean_made, tr_done, tr_copied = sem("deg_ready"), sem("mean_made"), sem("tr_done"), sem("tr_copied")
        hmm_done, h_made, w_gnn = sem("hmm_done"), sem("h_made"), sem("w_gnn")
        h_stored = [sem(f"h_stored{i}") for i in range(TGRP)]
        h_all = sem("h_all")
        rows_clear = sem("rows_clear")
        w_ffn = sem("w_ffn")
        x_loaded, h_loaded, out_stored = sem("x_loaded"), sem("h_loaded"), sem("out_stored")
        h_free, x_free, grp_done = sem("h_free"), sem("x_free"), sem("grp_done")
        u_ready, th_ready, var_ready, sd_ready = sem("u_ready"), sem("th_ready"), sem("var_ready"), sem("sd_ready")
        x2_ready, xt_done, xt_copied = sem("x2_ready"), sem("xt_done"), sem("xt_copied")
        lg_done, lsub_ready, ex_ready, comb_ready = sem("lg_done"), sem("lsub_ready"), sem("ex_ready"), sem("comb_ready")
        ct_done, ct_copied = sem("ct_done"), sem("ct_copied")
        h_ready, gelu_done, y_ready, y_used = sem("h_ready"), sem("gelu_done"), sem("y_ready"), sem("y_used")

        block = ctx.enter_context(nc.Block())

        def blocked(ap):
            return ap.rearrange("(t p) d -> p t d", p=P)

        @block.sync
        def _(sp):
            full = EDGE_COLS * P
            for t, a in ((src_i, src), (dst_i, dst)):
                sp.dma_start(t[:, 0:EDGE_COLS], a[0:full].rearrange("(p n) -> p n", p=P)).then_inc(s_edges, 16)
            sp.wait_ge(pad_set, 4)
            zeros = zero_bf[:, :].bitcast(f32)
            sp.dma_start(pair_dram.rearrange("(p a c) w -> p a (c w)", p=P, a=8),
                         zeros.unsqueeze(1).to_broadcast([P, 8, HALF // 2])).then_inc(pairs_zero, 16)
            for t, a in ((src_i, src), (dst_i, dst)):
                with nc.allow_non_contiguous_dma(reason="ten single edges"):
                    sp.dma_start(t[0:EDGE_REST, EDGE_COLS:EDGE_COLS + 1],
                                 a[full:N_EDGES].rearrange("(p n) -> p n", n=1)).then_inc(s_edges, 16)
            sp.dma_start(rows[:, 0:BLOCKS - 1, 0:D], blocked(x[0:(BLOCKS - 1) * P, :])).then_inc(s_x, 16)
            sp.dma_start(rows[0:LAST_ROWS, BLOCKS - 1, 0:D], x[(BLOCKS - 1) * P:N_NODES, :]).then_inc(s_x, 16)
            sp.wait_ge(blk_ready, 1)
            with nc.allow_non_contiguous_dma(reason="small table"):
                sp.dma_start(blk_dram.rearrange("(q p) -> p q", p=P), blk_ci[:, :]).then_inc(blk_stored, 16)
            sp.wait_ge(blk_stored, 16)
            sp.wait_ge(pick_done, BLOCKS)
            sp.dma_start(blk_row[:, :], blk_dram.rearrange("(a n) -> a n", a=1)).then_inc(blk_loaded, 16)
            sp.wait_ge(xn_done, BLOCKS)
            sp.dma_start(blocked(xn_dram), rows[:, :, 0:D]).then_inc(xn_stored, 16)
            sp.wait_ge(xn_stored, 16)
            sp.wait_ge(blk_loaded, 16)
            for u in range(2 * GROUP):
                sp.wait_ge(scattered[u], 16 * (POOL_COLS // (2 * GROUP)))
            sp.dma_start(big[:, 0:2 * CHUNKS], pair_dram.rearrange("(p c) w -> p (c w)", p=P)).then_inc(pairs_loaded, 16)
            for k in range(2):
                sp.dma_start(wr_sb[:, k, :], w_root[k * P:(k + 1) * P, :]).then_inc(w_gnn, 16)
                sp.dma_start(wn_sb[:, k, :], w_neigh[k * P:(k + 1) * P, :]).then_inc(w_gnn, 16)
            sp.dma_start(gb_sb[:, :], gnn_b.rearrange("(a n) -> a n", a=1)).then_inc(w_gnn, 16)
            sp.wait_ge(sort_ready, 2)
            for k in range(2):
                sp.dma_start(w1_sb[:, :, k, :], w1[:, k * P:(k + 1) * P, :].rearrange("e p f -> p e f")).then_inc(w_ffn, 16)
                sp.dma_start(w2_sb[:, :, k, :], w2[:, k * P:(k + 1) * P, :].rearrange("e p f -> p e f")).then_inc(w_ffn, 16)
            sp.dma_start(b2_sb[:, :], b2).then_inc(w_ffn, 16)
            with nc.allow_non_contiguous_dma(reason="small transposed weights"):
                for k in range(2):
                    sp.dma_start(rw_sb[:, k, :], router_w[:, k * P:(k + 1) * P].rearrange("e p -> p e")).then_inc(w_ffn, 16)
                    sp.dma_start(b1_sb[:, :, k], b1[:, k * P:(k + 1) * P].rearrange("e p -> p e")).then_inc(w_ffn, 16)
            for g in range(TGRP):
                sp.wait_ge(h_made, TBLK * (g + 1))
                sp.dma_start(blocked(h_dram[g * TBLK * P:(g + 1) * TBLK * P, :]),
                             rows[:, g * TBLK:(g + 1) * TBLK, 0:D]).then_inc(h_stored[g], 16)

            def load_h(g):
                sp.dma_start(hg, blocked(h_dram[ds(g * TBLK * P, TBLK * P), :])).then_inc(h_loaded, 16)

            def load_x(g):
                first = g * TBLK * P
                whole = (TBLK - 1) * P
                tail_rows = LAST_ROWS if g is TGRP - 1 else P
                sp.dma_start(xg[:, 0:TBLK - 1, :], blocked(x[ds(first, whole), :])).then_inc(x_loaded, 16)
                sp.dma_start(xg[0:tail_rows, TBLK - 1, :], x[ds(first + whole, tail_rows), :]).then_inc(x_loaded, 16)

            def store(g):
                first = g * TBLK * P
                whole = (TBLK - 1) * P
                tail_rows = LAST_ROWS if g is TGRP - 1 else P
                sp.dma_start(blocked(out[ds(first, whole), :]),
                             rows[:, ds(g * TBLK, TBLK - 1), 0:D]).then_inc(out_stored, 16)
                sp.dma_start(out[ds(first + whole, tail_rows), :],
                             rows[0:tail_rows, ds(g * TBLK + TBLK - 1, 1), 0:D].rearrange("p a d -> p (a d)"))\
                    .then_inc(out_stored, 16)

            def group_io(g, nxt, first=False):
                sp.wait_ge(h_free, g + 1)
                load_h(nxt)
                if not first:
                    sp.wait_ge(grp_done, g)
                    store(g - 1)
                sp.wait_ge(x_free, g + 1)
                load_x(nxt)

            sp.wait_ge(added, 2 * CHUNKS)
            load_h(0)
            load_x(0)
            group_io(0, 1, first=True)
            with sp.Fori(1, TGRP - 2) as g:
                group_io(g, g + 1)
            group_io(TGRP - 2, TGRP - 1)
            for g in (TGRP - 2, TGRP - 1):
                sp.wait_ge(grp_done, g + 1)
                store(g)
            sp.wait_ge(out_stored, 32 * TGRP)

        @block.gpsimd
        def _(pool):
            n = [0]

            def step(ins):
                n[0] += 1
                ins.then_inc(pool_step, 1)
                pool.wait_ge(pool_step, n[0])

            step(pool.memset(ones[:, :], 1.0))
            pool.memset(rows[:, BLOCKS - 1, 0:D], 0.0).then_inc(pad_set, 1)
            step(pool.iota(iota_i[:, :], [[1, CHUNKS]], base=0, channel_multiplier=0))
            step(pool.iota(kpos_i[:, :], [[P, BLK_COLS // P]], base=0, channel_multiplier=1))
            step(pool.memset(eps_t[:, :], EPS))
            step(pool.affine_select(out=upper[:, :], in_=ones[:, :], compare_op=ALU.is_gt, fill=0.0, base=0,
                                    pattern=[[1, P]], channel_multiplier=-1))
            pool.affine_select(out=ident[:, :], in_=ones[:, :], compare_op=ALU.is_equal, fill=0.0, base=0,
                               pattern=[[1, P]], channel_multiplier=-1).then_inc(consts, 1)
            pool.wait_ge(pos_ready, 1)

            def add_places(b, par, first=False):
                if not first:
                    pool.wait_ge(pick_done, b)
                pool.wait_ge(placed, b + 1)
                pool.tensor_tensor(pos_f, pos_f, picked[:, par, :], ALU.add).then_inc(pick_done, 1)

            add_places(0, 0, True)
            with pool.Fori(0, BLOCKS // 2) as i:
                add_places(2 * i + 1, 1)
                add_places(2 * i + 2, 0)

            pool.wait_ge(pairs_zero, 16)

            def scatter(i):
                for h in range(2):
                    pool.wait_ge(pairs_staged, 2 * i + h + 1)
                    pool.sem_inc(pool_turn, 1)
                    for c in range(GROUP):
                        pool.indirect_dma_start(pair_dram, bass.IndirectOffsetOnAxis(ap=stage[:, h, c:c + 1], axis=0),
                                                pair_stage[:, h, c, :], None).then_inc(scattered[GROUP * h + c], 16)

            with pool.Fori(0, POOL_COLS // (2 * GROUP)) as i:
                scatter(i)
            pool.wait_ge(ssq_done, BLOCKS)
            pool.memset(rows[:, :, D:2 * D + 1], 0.0).then_inc(rows_zero, 1)

            def gather_turn(table, base, i, first):
                for h in range(2):
                    for_half = base + TURN * i + GROUP * h
                    pool.wait_ge(staged, 2 * (base // TURN) + 2 * i + h + 1)
                    if not first:
                        pool.wait_ge(mult_done, for_half - TURN + GROUP)
                    pool.sem_inc(pool_turn, 1)
                    for c in range(GROUP):
                        slot = GROUP * h + c
                        pool.indirect_dma_start(ring[:, slot, 0:D], None, table,
                                                bass.IndirectOffsetOnAxis(ap=stage[:, h, c:c + 1], axis=0))\
                            .then_inc(gathered[slot], 16)

            def gather_pass(table, base):
                gather_turn(table, base, 0, True)
                with pool.Fori(1, CHUNKS // TURN) as i:
                    gather_turn(table, base, i, False)

            pool.wait_ge(xn_stored, 16)
            gather_pass(xn_dram, 0)
            for g in range(TGRP):
                pool.wait_ge(h_stored[g], 16)
                pool.memset(rows[:, g * TBLK:(g + 1) * TBLK, 0:2 * D], 0.0).then_inc(rows_clear, 1)
            gather_pass(h_dram, CHUNKS)

        @block.scalar
        def _(act):
            act.wait_ge(s_x, 32)

            def total(t):
                row = rows[:, ds(t, 1), 0:D].rearrange("p a d -> p (a d)")
                act.activation(row, row, ACT.Identity, accum_out=sums[:, ds(t, 1)]).then_inc(sums_done, 1)

            total(0)
            with act.Fori(1, BLOCKS) as t:
                total(t)
            act.wait_ge(sums_done, BLOCKS)
            act.mul(nmean[:, :], sums[:, :], -1.0 / D).then_inc(act_step, 1)
            act.wait_ge(act_step, 1)
            with act.Fori(0, BLOCKS) as t:
                act.activation(rows[:, ds(t, 1), D:2 * D].rearrange("p a d -> p (a d)"),
                               rows[:, ds(t, 1), 0:D].rearrange("p a d -> p (a d)"), ACT.Square,
                               bias=nmean[:, ds(t, 1)], accum_out=ssq[:, ds(t, 1)]).then_inc(ssq_done, 1)
            act.wait_ge(ssq_done, BLOCKS)
            act.wait_ge(consts, 1)
            act.activation(std[:, :], ssq[:, :], ACT.Sqrt, bias=eps_t[:, :], scale=1.0 / D).then_inc(std_done, 1)
            act.wait_ge(rstd_ready, 1)
            with act.Fori(0, BLOCKS) as t:
                row = rows[:, ds(t, 1), 0:D].rearrange("p a d -> p (a d)")
                act.activation(row, row, ACT.Identity, bias=nmr[:, ds(t, 1)], scale=rstd[:, ds(t, 1)]).then_inc(xn_done, 1)


            def put_pairs(i, h, first):
                if not first:
                    for c in range(GROUP):
                        act.wait_ge(scattered[GROUP * h + c], 16 * i)
                at = 2 * GROUP * i + GROUP * h
                act.copy(pair_stage[:, h, :, :], pair_f[:, ds(at, GROUP), :])
                act.copy(stage[:, h, :], place_i[:, ds(at, GROUP)]).then_inc(pairs_staged, 1)

            act.wait_ge(pairs_ready, 1)
            put_pairs(0, 0, True)
            put_pairs(0, 1, True)
            with act.Fori(1, POOL_COLS // (2 * GROUP)) as i:
                put_pairs(i, 0, False)
                put_pairs(i, 1, False)

            def put(i, h):
                act.copy(stage[:, h, :], idx_i[:, ds(TURN * i + GROUP * h, GROUP)]).then_inc(staged, 1)

            def stage_pass(base, squares):
                turns = base // TURN

                def half(i, h, last):
                    for c in range(GROUP):
                        slot = GROUP * h + c
                        act.wait_ge(gathered[slot], 16 * (turns + i + 1))
                        if squares:
                            act.activation(ring[:, slot, D:2 * D], ring[:, slot, 0:D], ACT.Square).then_inc(squared, 1)
                    if not last:
                        put(i + 1, h)

                put(0, 0)
                put(0, 1)
                with act.Fori(0, CHUNKS // TURN - 1) as i:
                    half(i, 0, False)
                    half(i, 1, False)
                half(CHUNKS // TURN - 1, 0, True)
                half(CHUNKS // TURN - 1, 1, True)

            act.wait_ge(sort_ready, 2)
            stage_pass(0, False)

            def copy_tr(t, par, early=False):
                act.wait_ge(tr_done, t + 1)
                if not early:
                    act.wait_ge(hmm_done, t - 1)
                act.copy(tr_sb[:, par, :, :].rearrange("p k r -> p (k r)"), bank[4 + par]).then_inc(tr_copied, 1)

            def relu(t, par):
                act.wait_ge(hmm_done, t + 1)
                act.activation(rows[:, ds(t, 1), 0:D].rearrange("p a d -> p (a d)"), bank[6 + par][:, 0:D],
                               ACT.Relu).then_inc(h_made, 1)

            copy_tr(0, 0, True)
            copy_tr(1, 1, True)
            relu(0, 0)
            with act.Fori(1, BLOCKS // 2) as i:
                copy_tr(2 * i, 0)
                relu(2 * i - 1, 1)
                copy_tr(2 * i + 1, 1)
                relu(2 * i, 0)
            copy_tr(BLOCKS - 1, 0)
            relu(BLOCKS - 2, 1)
            relu(BLOCKS - 1, 0)
            act.wait_ge(h_made, BLOCKS)
            stage_pass(CHUNKS, True)

            def tanhs(g):
                act.wait_ge(u_ready, g + 1)
                for j in range(TBLK):
                    act.activation(ug[:, j, :], ug[:, j, :], ACT.Tanh, scale=rden[:, ds(g * TBLK + j, 1)]).then_inc(th_ready, 1)

            def stds(g):
                act.wait_ge(var_ready, g + 1)
                act.activation(t7[:, 1, :], t7[:, 0, :], ACT.Sqrt).then_inc(sd_ready, 1)

            def copy_xt(g):
                for r in range(4):
                    n = 2 * TBLK * P - 512 * r if r == 3 else 512
                    act.wait_ge(xt_done, 4 * g + r + 1)
                    act.copy(xT_flat[:, 512 * r:512 * r + n], bank[4][:, 0:n]).then_inc(xt_copied, 1)

            def exps(g):
                act.wait_ge(lsub_ready, g + 1)
                act.activation(lg[:, 1, :, :], lg[:, 0, :, :], ACT.Exp).then_inc(ex_ready, 1)

            def copy_ct(g):
                act.wait_ge(ct_done, g + 1)
                act.copy(combT[:, 0:512], bank[4][0:N_EXP, :]).then_inc(ct_copied, 1)
                act.copy(combT[:, 512:TBLK * P], bank[5][0:N_EXP, 0:TBLK * P - 512]).then_inc(ct_copied, 1)

            def gelus(g, e, early=False):
                if not early:
                    act.wait_ge(y_ready, (1 + N_EXP) * TBLK * g + TBLK * e)
                for q in range(4):
                    act.wait_ge(h_ready, 4 * (N_EXP * g + e) + q + 1)
                    act.activation(hT[e % 2][:, q // 2, TOK * (q % 2):TOK * (q % 2 + 1)], bank[q][:, 0:TOK], ACT.Gelu,
                                   bias=b1_sb[:, e, q // 2:q // 2 + 1]).then_inc(gelu_done, 1)

            def group(g, more):
                for e in range(N_EXP):
                    if e + 1 < N_EXP:
                        gelus(g, e + 1)
                    if more and e == 3:
                        tanhs(g + 1)
                    if more and e == 4:
                        stds(g + 1)
                    if more and e == 6:
                        copy_xt(g + 1)
                if more:
                    exps(g + 1)
                    gelus(g + 1, 0)
                    copy_ct(g + 1)

            act.wait_ge(w_ffn, 16 * 9)
            tanhs(0)
            stds(0)
            copy_xt(0)
            exps(0)
            gelus(0, 0, True)
            copy_ct(0)
            with act.Fori(0, TGRP - 1) as g:
                group(g, True)
            group(TGRP - 1, False)

        @block.vector
        def _(dve):
            n = [0]

            def step(ins):
                n[0] += 1
                ins.then_inc(dve_step, 1)
                dve.wait_ge(dve_step, n[0])

            v = nc.vector
            v.memset(src_i[:, EDGE_COLS:IN_COLS], BLOCKS * P).then_inc(pad_set, 1)
            v.memset(dst_i[:, EDGE_COLS:IN_COLS], 0).then_inc(pad_set, 1)
            step(v.memset(zero_bf[:, :], 0.0))
            v.sem_inc(pad_set, 1)
            dve.wait_ge(consts, 1)
            step(v.tensor_copy(iota_h[:, :], iota_i[:, :]))
            step(v.tensor_copy(kpos_f[:, :], kpos_i[:, :]))
            step(v.tensor_scalar(iota1_f[:, :], iota_i[:, 0:P], 1.0, None, ALU.add))
            step(v.tensor_copy(iota8_f[:, :], iota_i[:, 0:N_EXP]))
            dve.wait_ge(s_edges, 64)
            step(v.tensor_scalar(tmp_i, src_i, 7, None, ALU.arith_shift_right))
            step(v.tensor_scalar(blk_f, tmp_i, 1.0, None, ALU.add))
            step(v.tensor_scalar(tmp_i, src_i, P - 1, None, ALU.bitwise_and))
            step(v.tensor_scalar(rowlo_f, tmp_i, 1.0, None, ALU.add))
            step(v.tensor_scalar(tmp_i, dst_i, float(COL_BIAS), None, ALU.add))
            step(v.tensor_scalar(colbits.bitcast(i32), tmp_i, 16, None, ALU.logical_shift_left))
            step(v.tensor_scalar(pos_f, blk_f, float(BLOCKS), float(NOWHERE), ALU.is_gt, ALU.mult))
            v.sem_inc(pos_ready, 1)
            with dve.Fori(0, BLOCKS) as b:
                v.tensor_scalar(masks[:, ds(b, 1), :].rearrange("p a c -> p (a c)"), blk_f, iota1_f[:, ds(b, 1)],
                                0.0, ALU.is_equal, ALU.add, accum_out=counts[:, ds(b, 1)]).then_inc(mask_done, 1)
            dve.wait_ge(mask_done, BLOCKS)
            step(v.tensor_copy(off_f[:, :], counts[:, :]))
            v.sem_inc(counts_ready, 1)
            dve.wait_ge(totals_done, 1)
            step(v.tensor_scalar(tot_i[:, :], bank[1][:, 0:BLOCKS], float(P - 1), None, ALU.add))
            step(v.tensor_scalar(tot_i[:, :], tot_i[:, :], 7, None, ALU.arith_shift_right))
            step(v.tensor_copy(nch_f[:, :], tot_i[:, :]))
            step(v.memset(start_f[:, 0:1], 0.0))
            step(v.tensor_tensor_scan(start_f[:, 1:BLOCKS + 1], nch_f[:, :], nch_f[:, :], 0.0, ALU.add, ALU.max))
            step(v.scalar_tensor_tensor(off_f[:, :], start_f[:, 0:BLOCKS], float(P), bank[0][:, 0:BLOCKS],
                                        ALU.mult, ALU.add))
            q = BLK_COLS // P
            step(v.tensor_tensor(cmp_f[:, :, :], kpos_f[:, :].unsqueeze(2).to_broadcast([P, q, BLOCKS]),
                                 start_f[:, 0:BLOCKS].unsqueeze(1).to_broadcast([P, q, BLOCKS]), ALU.is_ge))
            step(v.tensor_reduce(blk_cf[:, :], cmp_f[:, :, :], AX.X, ALU.add))
            v.tensor_scalar(blk_ci[:, :], blk_cf[:, :], -1.0, float(BLOCKS - 1), ALU.add, ALU.min).then_inc(blk_ready, 1)
            def places(b, par, first):
                m = masks[:, ds(b, 1), :].rearrange("p a c -> p (a c)")
                running = ps[:, 1024 * (1 + par):1024 * (1 + par) + IN_COLS]
                if not first:
                    dve.wait_ge(pick_done, b - 1)
                v.tensor_tensor_scan(running, m, m, off_f[:, ds(b, 1)], ALU.add, ALU.max).then_inc(scan_done, 1)
                dve.wait_ge(scan_done, b + 1)
                v.tensor_tensor(picked[:, par, :], running, m, ALU.mult).then_inc(placed, 1)

            places(0, 0, True)
            places(1, 1, True)
            places(2, 0, False)
            with dve.Fori(1, BLOCKS // 4) as i:
                places(2 * i + 1, 1, False)
                places(2 * i + 2, 0, False)
            dve.wait_ge(std_done, 1)
            step(v.reciprocal(rstd[:, :], std[:, :]))
            v.tensor_tensor(nmr[:, :], nmean[:, :], rstd[:, :], ALU.mult).then_inc(rstd_ready, 1)
            with dve.Fori(BLOCKS // 4, BLOCKS // 2) as i:
                places(2 * i + 1, 1, False)
                places(2 * i + 2, 0, False)
            dve.wait_ge(pick_done, BLOCKS)
            step(v.tensor_scalar(tmp_i, pos_f, -1.0, None, ALU.add))
            step(v.tensor_scalar(src_i, tmp_i, 7, None, ALU.arith_shift_right))
            step(v.tensor_copy(hi_f, src_i))
            step(v.tensor_scalar(src_i, tmp_i, P - 1, None, ALU.bitwise_and))
            step(v.tensor_copy(lo_f, src_i))
            step(v.scalar_tensor_tensor(place_i, lo_f, float(CHUNKS), hi_f, ALU.mult, ALU.add))
            step(v.tensor_copy(pair_f[:, :, 0], dst_i[:, 0:POOL_COLS]))
            step(v.tensor_copy(pair_f[:, :, 1], rowlo_f[:, 0:POOL_COLS]))
            v.sem_inc(pairs_ready, 1)
            def one_hots(i, first):
                for u in range(IN_UNROLL):
                    j = POOL_COLS + i * IN_UNROLL + u
                    if not first:
                        dve.wait_ge(sorted_cols, (i - 1) * IN_UNROLL + u + 1)
                    v.tensor_scalar(hi_oh[:, u, :], iota_h[:, :], hi_f[:, ds(j, 1)], None, ALU.is_equal)
                    v.tensor_scalar(lo_col[:, u, :], iota_h[:, 0:P], lo_f[:, ds(j, 1)], colbits[:, ds(j, 1)],
                                    ALU.is_equal, ALU.mult)
                    v.tensor_scalar(lo_row[:, u, :], iota_h[:, 0:P], lo_f[:, ds(j, 1)], rowlo_f[:, ds(j, 1)],
                                    ALU.is_equal, ALU.mult).then_inc(oh_ready, 1)

            one_hots(0, True)
            with dve.Fori(1, (IN_COLS - POOL_COLS) // IN_UNROLL) as i:
                one_hots(i, False)
            dve.wait_ge(sorted_cols, IN_COLS - POOL_COLS + 1)
            bits = rflat[:, 0:CHUNKS]
            for half in range(2):
                v.tensor_copy(bits[:, half * HALF:(half + 1) * HALF], bank[half][:, 0:HALF])
                v.tensor_copy(erow[:, half * HALF:(half + 1) * HALF], bank[2 + half][:, 0:HALF])
            step(v.memset(erow[:, CHUNKS:CHUNKS + TURN], 0.0))
            step(v.tensor_scalar(bits.bitcast(i32), bits.bitcast(i32), 16, None, ALU.logical_shift_right))
            step(v.tensor_scalar(idx_i[:, :], bits.bitcast(i32), float(-COL_BIAS), 0.0, ALU.add, ALU.max))
            dve.wait_ge(pairs_loaded, 16)
            step(v.tensor_tensor(erow[:, 0:CHUNKS], erow[:, 0:CHUNKS], merged[:, :, 1], ALU.add))
            v.tensor_tensor(idx_i[:, :], merged[:, :, 0], idx_i[:, :], ALU.add).then_inc(sort_ready, 2)


            def make_one_hot(k, slot):
                v.tensor_scalar(onehot[:, slot // GROUP, slot % GROUP, :], iota1_f[:, :], erow[:, ds(k, 1)], None,
                                ALU.is_equal).then_inc(oh_made, 1)

            def add_half(i, h, base, lo, width, first):
                k0 = TURN * i + GROUP * h
                _, blocks = nc.values_load_multi_w_load_instructions(
                    blk_row[0:1, ds(k0, GROUP)], engines=[mybir.EngineType.DVE], min_val=0, max_val=BLOCKS - 1,
                    skip_runtime_bounds_check_because="the table is clamped to 0..BLOCKS-1 when it is made")
                for c in range(GROUP):
                    k = base + k0 + c
                    row = rows[:, ds(blocks[c], 1), lo:lo + width].rearrange("p a d -> p (a d)")
                    if not (first and c == 0):
                        dve.wait_ge(added, k)
                    dve.wait_ge(mult_done, k + 1)
                    v.tensor_tensor(row, row, bank[(GROUP * h + c) % ACC_BUFS][:, 0:width], ALU.add).then_inc(added, 1)
                    make_one_hot(k0 + c + TURN, GROUP * h + c)

            def add_pass(base, lo, width):
                for k in range(TURN):
                    make_one_hot(k, k)

                def turn(i, first):
                    add_half(i, 0, base, lo, width, first)
                    add_half(i, 1, base, lo, width, False)

                turn(0, base == 0)
                with dve.Fori(1, CHUNKS // TURN) as i:
                    turn(i, False)

            dve.wait_ge(sort_ready, 2)
            step(v.memset(ring[:, :, D:D + 1], 1.0))
            dve.wait_ge(blk_loaded, 16)
            dve.wait_ge(rows_zero, 1)
            add_pass(0, D, D + 1)

            dve.wait_ge(added, CHUNKS)
            step(v.tensor_copy(deg[:, :], rows[:, :, 2 * D]))
            step(v.tensor_scalar(rden[:, :], deg[:, :], 1.0, None, ALU.max))
            step(v.reciprocal(rden[:, :], rden[:, :]))

            def mean(t, par, early=False):
                if not early:
                    dve.wait_ge(tr_done, t - 1)
                v.tensor_copy(operand[:, par, 0:D], rows[:, ds(t, 1), 0:D].rearrange("p a d -> p (a d)"))
                v.tensor_scalar(operand[:, par, D:2 * D], rows[:, ds(t, 1), D:2 * D].rearrange("p a d -> p (a d)"),
                                rden[:, ds(t, 1)], None, ALU.mult).then_inc(mean_made, 1)

            mean(0, 0, True)
            mean(1, 1, True)
            with dve.Fori(1, BLOCKS // 2) as i:
                mean(2 * i, 0)
                mean(2 * i + 1, 1)
            mean(BLOCKS - 1, 0)

            dve.wait_ge(rows_clear, TGRP)
            add_pass(CHUNKS, 0, 2 * D)

            done = [0]

            def link(ins, g, per):
                done[0] += 1
                ins.then_inc(tail_step, 1)
                dve.wait_ge(tail_step, g * per + done[0])

            blocks7 = lambda g, lo: rows[:, ds(g * TBLK, TBLK), lo:lo + D]
            col7 = lambda r: t7[:, r, :]

            def p0(g):
                dve.wait_ge(h_loaded, 16 * (g + 1))
                for j in range(TBLK):
                    last = v.tensor_scalar(ug[:, j, :], hg[:, j, :], deg[:, ds(g * TBLK + j, 1)], None, ALU.mult)
                link(last, g, STEPS)
                link(v.scalar_tensor_tensor(ug, blocks7(g, 0), -2.0, ug, ALU.mult, ALU.add), g, STEPS)

            def p1(g):
                link(v.tensor_tensor(ug, ug, hg, ALU.mult), g, STEPS)
                v.sem_inc(h_free, 1)

            def p2(g):
                v.tensor_tensor(ug, ug, blocks7(g, D), ALU.add).then_inc(u_ready, 1)

            def p4(g):
                dve.wait_ge(x_loaded, 32 * (g + 1))
                dve.wait_ge(th_ready, TBLK * (g + 1))
                link(v.tensor_tensor(xg, xg, ug, ALU.add), g, STEPS)
                for j in range(TBLK):
                    last = v.bn_stats(bn6[:, j, :], xg[:, j, :])
                link(last, g, STEPS)
                v.sem_inc(tail_turn, 1)
                for j in range(TBLK):
                    last = v.bn_aggr(mv[:, j, :], bn6[:, j, :])
                link(last, g, STEPS)
                v.tensor_scalar(col7(0), mv[:, :, 1], EPS, None, ALU.add).then_inc(var_ready, 1)

            def p5(g):
                dve.wait_ge(sd_ready, g + 1)
                link(v.reciprocal(col7(2), col7(1)), g, STEPS)
                link(v.tensor_tensor(col7(3), col7(2), col7(2), ALU.mult), g, STEPS)
                link(v.tensor_tensor(col7(3), col7(3), col7(0), ALU.mult), g, STEPS)
                link(v.tensor_scalar(col7(3), col7(3), -0.5, 1.5, ALU.mult, ALU.add), g, STEPS)
                link(v.tensor_tensor(col7(2), col7(2), col7(3), ALU.mult), g, STEPS)
                for j in range(TBLK):
                    last = v.tensor_scalar(ug[:, j, :], xg[:, j, :], mv[:, j, 0:1], t7[:, 2, j:j + 1], ALU.subtract, ALU.mult)
                last.then_inc(x2_ready, 1)

            def wide(ap):
                return ap.unsqueeze(2).to_broadcast([P, TBLK, N_EXP])

            logits = bank[5][:, 0:TBLK * N_EXP].rearrange("p (j e) -> p j e", j=TBLK)

            def p7a(g):
                dve.wait_ge(lg_done, g + 1)
                link(v.tensor_reduce(col7(4), logits, AX.X, ALU.max), g, STEPS)
                v.tensor_tensor(lg[:, 0, :, :], logits, wide(col7(4)), ALU.subtract).then_inc(lsub_ready, 1)

            def p7b(g):
                dve.wait_ge(ex_ready, g + 1)
                ex = lg[:, 1, :, :]
                link(v.tensor_reduce(col7(4), ex, AX.X, ALU.add), g, STEPS)
                link(v.reciprocal(col7(4), col7(4)), g, STEPS)
                link(v.tensor_tensor(ex, ex, wide(col7(4)), ALU.mult), g, STEPS)
                v.sem_inc(tail_turn, 1)
                for j in range(TBLK):
                    last = v.max(top8[:, j, :], lg[:, 1, j, :])
                link(last, g, STEPS)
                v.sem_inc(tail_turn, 1)
                for j in range(TBLK):
                    last = v.max_index(idx8[:, j, :], top8[:, j, :], lg[:, 1, j, :])
                link(last, g, STEPS)
                link(v.tensor_tensor(col7(5), top8[:, :, 0], top8[:, :, 1], ALU.add), g, STEPS)
                link(v.tensor_scalar(col7(5), col7(5), 1e-12, None, ALU.max), g, STEPS)
                link(v.reciprocal(col7(5), col7(5)), g, STEPS)
                iota7 = iota8_f[:, :].unsqueeze(1).to_broadcast([P, TBLK, N_EXP])
                for r in range(2):
                    link(v.tensor_copy(idx8f[:, r, :], idx8[:, :, r]), g, STEPS)
                    link(v.tensor_tensor(col7(6 + r), top8[:, :, r], col7(5), ALU.mult), g, STEPS)
                    link(v.tensor_tensor(lg[:, r, :, :], iota7, wide(idx8f[:, r, :]), ALU.is_equal), g, STEPS)
                    link(v.tensor_tensor(lg[:, r, :, :], lg[:, r, :, :], wide(col7(6 + r)), ALU.mult), g, STEPS)
                v.tensor_tensor(comb[:, :, :], lg[:, 0, :, :], lg[:, 1, :, :], ALU.add).then_inc(comb_ready, 1)
                link(v.tensor_tensor(blocks7(g, 0), xg, ug, ALU.add), g, STEPS)
                v.sem_inc(x_free, 1)

            def combine(g, n0, e):
                for j in range(TBLK):
                    n = n0 + j
                    count = (1 + N_EXP) * TBLK * g + n
                    row = rows[:, ds(g * TBLK + j, 1), 0:D].rearrange("p a d -> p (a d)")
                    y = bank[6 + n % 2][:, 0:D]
                    if e is not None:
                        dve.wait_ge(y_used, count - TBLK + 1)
                    dve.wait_ge(y_ready, count + 1)
                    if e is None:
                        last = v.tensor_tensor(row, row, y, ALU.add)
                    else:
                        last = v.scalar_tensor_tensor(row, y, comb[:, j, e:e + 1], row, ALU.mult, ALU.add)
                    last.then_inc(y_used, 1)

            def prepare(g, e):
                done[0] = PIECES[e]
                if e < 7:
                    {0: p0, 1: p1, 2: p2, 4: p4, 5: p5}.get(e, lambda g: None)(g)

            PIECES = {0: 0, 1: 2, 2: 3, 3: 3, 4: 3, 5: 6, 6: 11, 7: 11, 8: 12}
            STEPS = 12 + 8 + 8 + 1

            def group(g, more):
                for e in range(N_EXP):
                    if more and e < 7:
                        prepare(g + 1, e)
                    if more and e == 7:
                        done[0] = PIECES[7]
                        p7a(g + 1)
                    combine(g, TBLK * (e + 1), e)
                dve.wait_ge(y_used, (1 + N_EXP) * TBLK * (g + 1))
                v.sem_inc(grp_done, 1)
                if more:
                    done[0] = PIECES[8]
                    p7b(g + 1)
                    combine(g + 1, 0, None)

            dve.wait_ge(added, 2 * CHUNKS)
            for e in range(7):
                prepare(0, e)
            done[0] = PIECES[7]
            p7a(0)
            p7b(0)
            assert done[0] == STEPS
            combine(0, 0, None)
            with dve.Fori(0, TGRP - 1) as g:
                group(g, True)
            group(TGRP - 1, False)

        @block.tensor
        def _(pe):
            mm = nc.tensor.matmul
            pe.wait_ge(consts, 1)
            pe.wait_ge(counts_ready, 1)
            mm(bank[0][:, 0:BLOCKS], upper[:, :], counts[:, :], start=True, stop=True)
            mm(bank[1][:, 0:BLOCKS], ones[:, :], counts[:, :], start=True, stop=True).then_inc(totals_done, 1)
            pe.wait_ge(pairs_ready, 1)

            def zero(start):
                for b in range(4):
                    last = mm(bank[b][:, 0:HALF], zero_bf[:, 0:P], zero_bf[:, :], start=start, stop=not start)
                return last

            zero(True)

            def sort(i):
                for u in range(IN_UNROLL):
                    pe.wait_ge(oh_ready, i * IN_UNROLL + u + 1)
                    for n, lo in enumerate((lo_col, lo_row)):
                        for half in range(2):
                            last = mm(bank[2 * n + half][:, 0:HALF], lo[:, u, :],
                                      hi_oh[:, u, half * HALF:(half + 1) * HALF], start=False, stop=False)
                    last.then_inc(sorted_cols, 1)

            sort(0)
            with pe.Fori(1, (IN_COLS - POOL_COLS) // IN_UNROLL) as i:
                sort(i)
            zero(False).then_inc(sorted_cols, 1)

            def multiply_turn(i, base, width, ready, first):
                for s in range(TURN):
                    k = base + TURN * i + s
                    pe.wait_ge(oh_made, made[0] + TURN * i + s + 1)
                    if not (first and s < ACC_BUFS):
                        pe.wait_ge(added, k - ACC_BUFS + 1)
                    if ready is None:
                        pe.wait_ge(gathered[s], 16 * (i + 1))
                    else:
                        pe.wait_ge(squared, TURN * i + s + 1)
                    mm(bank[s % ACC_BUFS][:, 0:width], onehot[:, s // GROUP, s % GROUP, :], ring[:, s, 0:width],
                       start=True, stop=True).then_inc(mult_done, 1)

            made = [0]

            def multiply_pass(base, width, ready):
                multiply_turn(0, base, width, ready, base == 0)
                with pe.Fori(1, CHUNKS // TURN) as i:
                    multiply_turn(i, base, width, ready, False)

            multiply_pass(0, D + 1, None)

            def transposes(t, par, early=False):
                pe.wait_ge(mean_made, t + 1)
                if not early:
                    pe.wait_ge(tr_copied, t - 1)
                for k in range(4):
                    last = nc.tensor.transpose(bank[4 + par][:, k * P:(k + 1) * P],
                                               operand[:, par, k * P:(k + 1) * P], ident[:, :])
                last.then_inc(tr_done, 1)

            def hidden(t, par, early=False):
                pe.wait_ge(tr_copied, t + 1)
                if not early:
                    pe.wait_ge(h_made, t - 1)
                o = bank[6 + par][:, 0:D]
                for k in range(4):
                    mm(o, tr_sb[:, par, k, :], (wr_sb if k < 2 else wn_sb)[:, k % 2, :], start=(k == 0), stop=False)
                mm(o, ones[0:1, :], gb_sb[:, :], start=False, stop=True).then_inc(hmm_done, 1)

            pe.wait_ge(w_gnn, 16 * 5)
            transposes(0, 0, True)
            transposes(1, 1, True)
            hidden(0, 0, True)
            hidden(1, 1, True)
            transposes(2, 0)
            with pe.Fori(1, BLOCKS // 2) as i:
                transposes(2 * i + 1, 1)
                hidden(2 * i, 0)
                transposes(2 * i + 2, 0)
                hidden(2 * i + 1, 1)
            hidden(BLOCKS - 1, 0)

            made[0] = CHUNKS + TURN
            multiply_pass(CHUNKS, 2 * D, squared)

            def transpose_x2(g):
                pe.wait_ge(x2_ready, g + 1)
                for r in range(4):
                    if r == 0:
                        pe.wait_ge(ct_copied, 2 * g)
                    else:
                        pe.wait_ge(xt_copied, 4 * g + r)
                    tiles = range(4 * r, min(4 * r + 4, 2 * TBLK))
                    for n in tiles:
                        k, j = n // TBLK, n % TBLK
                        last = nc.tensor.transpose(
                            bank[4][:, (n % 4) * P:(n % 4 + 1) * P],
                            ug[:, j, k * P:(k + 1) * P], ident[:, :])
                    last.then_inc(xt_done, 1)

            def route(g):
                pe.wait_ge(xt_copied, 4 * (g + 1))
                for j in range(TBLK):
                    for k in range(2):
                        last = mm(bank[5][:, j * N_EXP:(j + 1) * N_EXP], xT[:, k, j * P:(j + 1) * P], rw_sb[:, k, :],
                                  start=(k == 0), stop=(k == 1))
                last.then_inc(lg_done, 1)

            def transpose_comb(g):
                pe.wait_ge(comb_ready, g + 1)
                for j in range(TBLK):
                    last = mm(bank[4 + j // 4][0:N_EXP, (j % 4) * P:(j % 4 + 1) * P], comb[:, j, :], ident[:, :],
                              start=True, stop=True)
                last.then_inc(ct_done, 1)

            def y_bank(g, n, early=False):
                count = (1 + N_EXP) * TBLK * g + n
                if not (early and n < 2):
                    pe.wait_ge(y_used, count if n == 0 else count - 1)
                return bank[6 + n % 2][:, 0:D]

            def bias2(g, early=False):
                pe.wait_ge(ct_copied, 2 * (g + 1))
                for j in range(TBLK):
                    y = y_bank(g, j, early)
                    mm(y, combT[:, j * P:(j + 1) * P], b2_sb[:, :], start=True, stop=True).then_inc(y_ready, 1)

            def layer1(g, e, early=False):
                for q in range(4):
                    if not early:
                        pe.wait_ge(gelu_done, 4 * (N_EXP * g + e) - 3 + q)
                    f = q // 2
                    for k in range(2):
                        last = mm(bank[q][:, 0:TOK], w1_sb[:, e, k, f * P:(f + 1) * P],
                                  xT[:, k, TOK * (q % 2):TOK * (q % 2 + 1)], start=(k == 0), stop=(k == 1))
                    last.then_inc(h_ready, 1)

            def layer2(g, e):
                pe.wait_ge(gelu_done, 4 * (N_EXP * g + e + 1))
                for j in range(TBLK):
                    y = y_bank(g, TBLK * (e + 1) + j)
                    for k in range(2):
                        last = mm(y, hT[e % 2][:, k, j * P:(j + 1) * P], w2_sb[:, e, k, :], start=(k == 0), stop=(k == 1))
                    last.then_inc(y_ready, 1)

            def group(g, more):
                for e in range(N_EXP):
                    if e + 1 < N_EXP:
                        layer1(g, e + 1)
                    layer2(g, e)
                    if more and e == 6:
                        transpose_x2(g + 1)
                        route(g + 1)
                if more:
                    layer1(g + 1, 0)
                    transpose_comb(g + 1)
                    bias2(g + 1)

            pe.wait_ge(w_ffn, 16 * 9)
            transpose_x2(0)
            route(0)
            layer1(0, 0, True)
            transpose_comb(0)
            bias2(0, True)
            with pe.Fori(0, TGRP - 1) as g:
                group(g, True)
            group(TGRP - 1, False)


_INS = ['x', 'src', 'dst', 'L0_gnn_W_root', 'L0_gnn_W_neigh', 'L0_gnn_b', 'L0_ffn_router_w', 'L0_ffn_w1',
        'L0_ffn_b1', 'L0_ffn_w2', 'L0_ffn_b2']


def kernel(**inputs):
    import numpy as _np
    import concourse.bacc as _bacc
    from concourse import mybir as _mybir
    from concourse.bass_utils import run_bass_kernel_spmd as _run

    nc = _bacc.Bacc("TRN2", target_bir_lowering=False, num_devices=1)
    arrays, args = {}, []
    for name in _INS:
        a = _np.ascontiguousarray(inputs[name])
        arrays[f"in_{name}"] = a
        args.append(nc.dram_tensor(f"in_{name}", a.shape, _mybir.dt.from_np(a.dtype), kind="ExternalInput").ap())
    args.append(nc.dram_tensor("out_0", (N_NODES, D), _mybir.dt.float32, kind="ExternalOutput").ap())
    gnn_moe(nc, *args)
    r = _run(nc, [arrays], core_ids=[0])
    return r.results[0]["out_0"]
```

```python
import concourse.bass as bass
from concourse import mybir
from concourse.alu_op_type import AluOpType as ALU
from contextlib import ExitStack

P = 128
N_NODES = 6250
D = 256
N_EDGES = 106250
N_EXP = 8
EPS = 1e-5
BLOCKS = -(-N_NODES // P)
LAST_ROWS = N_NODES - (BLOCKS - 1) * P
EDGE_COLS = N_EDGES // P
EDGE_REST = N_EDGES - EDGE_COLS * P
IN_UNROLL = 4
IN_COLS = -(-(EDGE_COLS + 1) // IN_UNROLL) * IN_UNROLL
POOL_COLS = 352
GROUP = 8
MAX_CHUNKS = -(-N_EDGES // P) + BLOCKS - 1
NORM_STEPS = 3
TURN = 2 * GROUP
CHUNKS = -(-MAX_CHUNKS // TURN) * TURN
HALF = CHUNKS // 2
NOWHERE = 1 << 18
COL_BIAS = 0x3000
BLK_COLS = -(-(CHUNKS + GROUP) // P) * P
TBLK = 7
TGRP = BLOCKS // TBLK
TOP_K = 2
PICKS = TOP_K * BLOCKS
EXP_TURN = 4
EXP_CHUNKS = -(-(PICKS + N_EXP - 1) // EXP_TURN) * EXP_TURN
ACC_BUFS = 4
assert BLOCKS % TBLK == 0 and HALF <= 512 and EXP_CHUNKS <= P - EXP_TURN


def gnn_moe(nc, x, src, dst, w_root, w_neigh, gnn_b, router_w, w1, b1, w2, b2, out):
    f32, i32, u8 = mybir.dt.float32, mybir.dt.int32, mybir.dt.uint8
    bf16, f16, u32 = mybir.dt.bfloat16, mybir.dt.float16, mybir.dt.uint32
    ACT, AX = mybir.ActivationFunctionType, mybir.AxisListType
    ds = bass.ds

    ctx = ExitStack()
    with ctx:
        def sb(name, shape, dt):
            return ctx.enter_context(nc.sbuf_tensor(name, shape, dt))

        def pb(name, shape, dt):
            return ctx.enter_context(nc.psum_tensor(name, shape, dt))

        def sem(name):
            return ctx.enter_context(nc.semaphore(name))

        xn_dram = nc.dram_tensor("xn_rows", (BLOCKS * P, D), f32).ap()
        h_dram = nc.dram_tensor("h_rows", (BLOCKS * P, D), f32).ap()
        pair_dram = nc.dram_tensor("sorted_pairs", (P * CHUNKS, 2), f32).ap()
        x2_dram = nc.dram_tensor("x2_rows", (BLOCKS * P, D), f32).ap()
        y_dram = nc.dram_tensor("expert_rows", (EXP_CHUNKS * P, D), f32).ap()
        ct_dram = nc.dram_tensor("chunk_expert", (P,), i32).ap()
        blk_dram = nc.dram_tensor("chunk_block", (BLK_COLS,), i32).ap()

        rows = sb("rows", [P, BLOCKS, 2 * D + 1], f32)
        big = sb("big", [P, BLOCKS * IN_COLS // 4], f32)
        masks = big[:, :].bitcast(u8).rearrange("p (b c) -> p b c", b=BLOCKS)
        wsize = N_EXP * 2 * D
        w1_sb = big[:, 0:wsize].rearrange("p (e k f) -> p e k f", e=N_EXP, k=2)
        w2_sb = big[:, wsize:2 * wsize].rearrange("p (e k f) -> p e k f", e=N_EXP, k=2)
        wr_sb = sb("wr_sb", [P, 2, D], f32)
        wn_sb = sb("wn_sb", [P, 2, D], f32)
        gb_sb = sb("gb_sb", [1, D], f32)
        rw_sb = sb("rw_sb", [P, 2, N_EXP], f32)

        iota_h = sb("iota_h", [P, CHUNKS], f16)
        iota1_f = sb("iota1_f", [P, P], f32)
        iota8_f = sb("iota8_f", [P, N_EXP], f32)
        kpos_i = sb("kpos_i", [P, BLK_COLS // P], i32)
        kpos_f = sb("kpos_f", [P, BLK_COLS // P], f32)
        ident = sb("ident", [P, P], f32)
        upper = sb("upper", [P, P], f32)
        ones = sb("ones", [P, P], f32)
        zero_bf = sb("zero_bf", [P, HALF], bf16)
        eps_t = sb("eps_t", [P, 1], f32)

        ring = sb("ring", [P, TURN, 2 * D], f32)
        rflat = ring[:, :, :].rearrange("p a b -> p (a b)")
        o = 0
        dst_i = rflat[:, o:o + IN_COLS].bitcast(i32); o += IN_COLS
        hi_f = rflat[:, o:o + IN_COLS]; o += IN_COLS
        lo_f = rflat[:, o:o + IN_COLS]; o += IN_COLS
        rowlo_f = rflat[:, o:o + IN_COLS]; o += IN_COLS
        colbits = rflat[:, o:o + IN_COLS]; o += IN_COLS
        pos_f = rflat[:, o:o + IN_COLS]; o += IN_COLS
        tmp_i = rflat[:, o:o + IN_COLS].bitcast(i32); o += IN_COLS
        pair_f = rflat[:, o:o + 2 * POOL_COLS].rearrange("p (c w) -> p c w", w=2)
        src_i = rflat[:, o:o + IN_COLS].bitcast(i32); o += IN_COLS
        blk_f = rflat[:, o:o + IN_COLS]; o += IN_COLS
        place_i = tmp_i
        assert o <= TURN * 2 * D
        onehot = sb("onehot", [P, 2, GROUP, P], f32)
        oflat = onehot[:, :, :, :].rearrange("p a b c -> p (a b c)").bitcast(bf16)
        hi_oh = sb("hi_oh", [P, IN_UNROLL, CHUNKS], bf16)
        lo_col = oflat[:, 0:IN_UNROLL * P].rearrange("p (a b) -> p a b", a=IN_UNROLL)
        lo_row = oflat[:, IN_UNROLL * P:2 * IN_UNROLL * P].rearrange("p (a b) -> p a b", a=IN_UNROLL)

        idx_i = sb("idx_i", [P, CHUNKS], i32)
        erow = sb("erow", [P, CHUNKS + TURN], f32)
        blk_row = big[0:1, 2 * wsize:2 * wsize + BLK_COLS].bitcast(i32)
        stage = sb("stage", [P, 2, GROUP], i32)
        pair_stage = sb("pair_stage", [P, 2, GROUP, 2], f32)
        merged = big[:, 0:2 * CHUNKS].rearrange("p (c w) -> p c w", w=2)

        iota_i = idx_i
        hflat = hi_oh[:, :, :].rearrange("p a b -> p (a b)").bitcast(f32)
        qb = BLK_COLS // P * BLOCKS
        cmp_f = hflat[:, D:D + qb].rearrange("p (q b) -> p q b", b=BLOCKS)
        picked = onehot[:, :, :, :].rearrange("p a b c -> p (a b c)")[:, 0:2 * IN_COLS].rearrange("p (a c) -> p a c", a=2)
        operand = rflat[:, 0:4 * D].rearrange("p (a d) -> p a d", a=2)
        tr_sb = rflat[:, 4 * D:4 * D + 8 * P].rearrange("p (a k r) -> p a k r", a=2, k=4)
        counts = sb("counts", [P, BLOCKS], f32)
        tot_i = sb("tot_i", [P, BLOCKS], i32)
        nch_f = sb("nch_f", [P, BLOCKS], f32)
        start_f = sb("start_f", [P, BLOCKS + 1], f32)
        off_f = sb("off_f", [P, BLOCKS], f32)
        blk_cf = sb("blk_cf", [P, BLK_COLS // P], f32)
        blk_ci = sb("blk_ci", [P, BLK_COLS // P], i32)

        G7 = TBLK * D
        xg, hg, ug, x2g = [rflat[:, n * G7:(n + 1) * G7].rearrange("p (j d) -> p j d", j=TBLK) for n in range(4)]
        oh_flat = onehot[:, :, :, :].rearrange("p a b c -> p (a b c)")
        xT_flat = oh_flat[:, 0:G7]
        xT = xT_flat.rearrange("p (k t) -> p k t", k=2)
        spare = [2 * wsize + BLK_COLS]

        def small(*shape):
            n = 1
            for a in shape:
                n *= a
            flat = big[:, spare[0]:spare[0] + n]
            spare[0] += n
            assert spare[0] <= BLOCKS * IN_COLS // 4
            if len(shape) == 3:
                return flat.rearrange("p (a b c) -> p a b c", a=shape[0], b=shape[1])
            return flat.rearrange("p (a b) -> p a b", a=shape[0]) if len(shape) == 2 else flat

        bn6 = small(TBLK, 6)
        mv = sb("mv", [P, TBLK, 2], f32)
        t7 = sb("t7", [P, 6, TBLK], f32)
        lg = small(2, TBLK, N_EXP)
        top8 = small(TBLK, 8)
        idx8 = small(TBLK, 8).bitcast(u32)
        share = sb("share", [P, TOP_K, BLOCKS], f32)
        expert_f = sb("expert_f", [P, TOP_K, BLOCKS], f32)
        picks = TOP_K * BLOCKS
        pmask = oh_flat[:, 0:N_EXP * picks].rearrange("p (e c) -> p e c", e=N_EXP)
        pscan = hi_oh[:, :, :].rearrange("p a b -> p (a b)").bitcast(f32)[:, 0:N_EXP * picks]\
            .rearrange("p (e c) -> p e c", e=N_EXP)
        c8 = small(4, N_EXP + 1)
        c8_i = small(N_EXP).bitcast(i32)
        pick_pos = small(3, picks)
        pick_row = idx_i[:, 0:picks]
        pick_tmp = idx_i[:, picks:2 * picks]
        tok_bits = idx_i[:, 2 * picks:2 * picks + BLOCKS]
        tok_sorted = idx_i[:, 256:256 + EXP_CHUNKS]
        ct_f = sb("ct_f", [P, 1], f32)
        ct_i = sb("ct_i", [P, 1], i32)
        exp_row = erow[0:1, 0:EXP_TURN + P].bitcast(i32)
        pk_hi = erow[:, 256:256 + EXP_CHUNKS].bitcast(bf16).rearrange("p (a c) -> p a c", a=2)
        pk_lo = erow[:, 512:512 + P].bitcast(bf16).rearrange("p (a c) -> p a c", a=2)
        xc = rflat[:, 0:4 * D].rearrange("p (a d) -> p a d", a=4)
        xcT = rflat[:, 4 * D:6 * D].rearrange("p (a d) -> p a d", a=2)
        hid = rflat[:, 6 * D:8 * D].rearrange("p (a d) -> p a d", a=2)
        hidT = rflat[:, 8 * D:10 * D].rearrange("p (a d) -> p a d", a=2)
        yc = rflat[:, 10 * D:14 * D].rearrange("p (a d) -> p a d", a=4)
        yg = rflat[:, 14 * D:28 * D].rearrange("p (a d) -> p a d", a=2 * TBLK)

        sums = sb("sums", [P, BLOCKS], f32)
        nmean = sb("nmean", [P, BLOCKS], f32)
        ssq = sb("ssq", [P, BLOCKS], f32)
        std = sb("std", [P, BLOCKS], f32)
        rstd = sb("rstd", [P, BLOCKS], f32)
        nmr = sb("nmr", [P, BLOCKS], f32)
        deg = sb("deg", [P, BLOCKS], f32)
        rden = sb("rden", [P, BLOCKS], f32)

        ps = pb("ps", [P, 8 * 512], f32)
        bank = [ps[:, 512 * i:512 * (i + 1)] for i in range(8)]

        pairs_zero, pairs_ready, pairs_staged = sem("pairs_zero"), sem("pairs_ready"), sem("pairs_staged")
        pairs_loaded = sem("pairs_loaded")
        scattered = [sem(f"scattered{i}") for i in range(2 * GROUP)]
        tail_turn = sem("tail_turn")
        tail_step = sem("tail_step")
        placed, pos_ready = sem("placed"), sem("pos_ready")
        pad_set = sem("pad_set")
        s_edges, s_x, s_w = sem("s_edges"), sem("s_x"), sem("s_w")
        pool_step, consts = sem("pool_step"), sem("consts")
        dve_step = sem("dve_step")
        sums_done, ssq_done, std_done = sem("sums_done"), sem("ssq_done"), sem("std_done")
        rstd_ready, xn_done, xn_stored = sem("rstd_ready"), sem("xn_done"), sem("xn_stored")
        act_step = sem("act_step")
        mask_done, scan_done, pick_done = sem("mask_done"), sem("scan_done"), sem("pick_done")
        counts_ready, totals_done = sem("counts_ready"), sem("totals_done")
        oh_ready, sorted_cols = sem("oh_ready"), sem("sorted_cols")
        blk_ready, blk_stored, blk_loaded = sem("blk_ready"), sem("blk_stored"), sem("blk_loaded")
        sort_ready = sem("sort_ready")
        rows_zero, oh_made, mult_done, added = sem("rows_zero"), sem("oh_made"), sem("mult_done"), sem("added")
        gathered = [sem(f"gathered{i}") for i in range(TURN)]
        staged, squared, pool_turn = sem("staged"), sem("squared"), sem("pool_turn")
        deg_ready, mean_made, tr_done, tr_copied = sem("deg_ready"), sem("mean_made"), sem("tr_done"), sem("tr_copied")
        hmm_done, h_made, w_gnn = sem("hmm_done"), sem("h_made"), sem("w_gnn")
        h_stored = [sem(f"h_stored{i}") for i in range(TGRP)]
        h_all = sem("h_all")
        rows_clear = sem("rows_clear")
        w_ffn = sem("w_ffn")
        x_loaded, h_loaded, out_stored = sem("x_loaded"), sem("h_loaded"), sem("out_stored")
        h_free, x_free, grp_done = sem("h_free"), sem("x_free"), sem("grp_done")
        hd_ready, s1_ready, u_ready, th_ready = sem("hd_ready"), sem("s1_ready"), sem("u_ready"), sem("th_ready")
        uh_done, norm_step, scale_step = sem("uh_done"), sem("norm_step"), sem("scale_step")
        var_ready, sd_ready, x2_ready, x2_stored = sem("var_ready"), sem("sd_ready"), sem("x2_ready"), sem("x2_stored")
        xt_done, xt_copied, lg_done = sem("xt_done"), sem("xt_copied"), sem("lg_done")
        peak_step, share_step = sem("peak_step"), sem("share_step")
        lsub_ready, ex_ready = sem("lsub_ready"), sem("ex_ready")
        bias_loaded, pcounts_ready, ptotals_done = sem("bias_loaded"), sem("pcounts_ready"), sem("ptotals_done")
        ct_ready, ct_stored, ct_loaded = sem("ct_ready"), sem("ct_stored"), sem("ct_loaded")
        pk_ready, pk_done, picks_ready = sem("pk_ready"), sem("pk_done"), sem("picks_ready")
        pk_order = sem("pk_order")
        xstaged, ystaged = sem("xstaged"), sem("ystaged")
        xc_in = [sem(f"xc_in{i}") for i in range(EXP_TURN)]
        y_stored = [sem(f"y_stored{i}") for i in range(EXP_TURN)]
        yg_in = [sem(f"yg_in{i}") for i in range(2 * TBLK)]
        t1_done, xcT_ready, l1_done, hb_ready = sem("t1_done"), sem("xcT_ready"), sem("l1_done"), sem("hb_ready")
        gelu_done, t2_done, hidT_ready = sem("gelu_done"), sem("t2_done"), sem("hidT_ready")
        l2_done, y_ready, combined = sem("l2_done"), sem("y_ready"), sem("combined")

        block = ctx.enter_context(nc.Block())

        def blocked(ap):
            return ap.rearrange("(t p) d -> p t d", p=P)

        @block.sync
        def _(sp):
            full = EDGE_COLS * P
            for t, a in ((src_i, src), (dst_i, dst)):
                sp.dma_start(t[:, 0:EDGE_COLS], a[0:full].rearrange("(p n) -> p n", p=P)).then_inc(s_edges, 16)
            sp.wait_ge(pad_set, 4)
            zeros = zero_bf[:, :].bitcast(f32)
            sp.dma_start(pair_dram.rearrange("(p a c) w -> p a (c w)", p=P, a=8),
                         zeros.unsqueeze(1).to_broadcast([P, 8, HALF // 2])).then_inc(pairs_zero, 16)
            for t, a in ((src_i, src), (dst_i, dst)):
                with nc.allow_non_contiguous_dma(reason="ten single edges"):
                    sp.dma_start(t[0:EDGE_REST, EDGE_COLS:EDGE_COLS + 1],
                                 a[full:N_EDGES].rearrange("(p n) -> p n", n=1)).then_inc(s_edges, 16)
            sp.dma_start(rows[:, 0:BLOCKS - 1, 0:D], blocked(x[0:(BLOCKS - 1) * P, :])).then_inc(s_x, 16)
            sp.dma_start(rows[0:LAST_ROWS, BLOCKS - 1, 0:D], x[(BLOCKS - 1) * P:N_NODES, :]).then_inc(s_x, 16)
            sp.wait_ge(blk_ready, 1)
            with nc.allow_non_contiguous_dma(reason="small table"):
                sp.dma_start(blk_dram.rearrange("(q p) -> p q", p=P), blk_ci[:, :]).then_inc(blk_stored, 16)
            sp.wait_ge(blk_stored, 16)
            sp.wait_ge(pick_done, BLOCKS)
            sp.dma_start(blk_row[:, :], blk_dram.rearrange("(a n) -> a n", a=1)).then_inc(blk_loaded, 16)
            sp.wait_ge(xn_done, BLOCKS)
            sp.dma_start(blocked(xn_dram), rows[:, :, 0:D]).then_inc(xn_stored, 16)
            sp.wait_ge(xn_stored, 16)
            sp.wait_ge(blk_loaded, 16)
            for u in range(2 * GROUP):
                sp.wait_ge(scattered[u], 16 * (POOL_COLS // (2 * GROUP)))
            sp.dma_start(big[:, 0:2 * CHUNKS], pair_dram.rearrange("(p c) w -> p (c w)", p=P)).then_inc(pairs_loaded, 16)
            for k in range(2):
                sp.dma_start(wr_sb[:, k, :], w_root[k * P:(k + 1) * P, :]).then_inc(w_gnn, 16)
                sp.dma_start(wn_sb[:, k, :], w_neigh[k * P:(k + 1) * P, :]).then_inc(w_gnn, 16)
            sp.dma_start(gb_sb[:, :], gnn_b.rearrange("(a n) -> a n", a=1)).then_inc(w_gnn, 16)
            sp.wait_ge(sort_ready, 2)
            for k in range(2):
                sp.dma_start(w1_sb[:, :, k, :], w1[:, k * P:(k + 1) * P, :].rearrange("e p f -> p e f")).then_inc(w_ffn, 16)
                sp.dma_start(w2_sb[:, :, k, :], w2[:, k * P:(k + 1) * P, :].rearrange("e p f -> p e f")).then_inc(w_ffn, 16)
            with nc.allow_non_contiguous_dma(reason="small transposed weights"):
                for k in range(2):
                    sp.dma_start(rw_sb[:, k, :], router_w[:, k * P:(k + 1) * P].rearrange("e p -> p e")).then_inc(w_ffn, 16)
            for g in range(TGRP):
                sp.wait_ge(h_made, TBLK * (g + 1))
                sp.dma_start(blocked(h_dram[g * TBLK * P:(g + 1) * TBLK * P, :]),
                             rows[:, g * TBLK:(g + 1) * TBLK, 0:D]).then_inc(h_stored[g], 16)

            def load_h(g):
                sp.dma_start(hg, blocked(h_dram[ds(g * TBLK * P, TBLK * P), :])).then_inc(h_loaded, 16)

            def load_x(g):
                first = g * TBLK * P
                whole = (TBLK - 1) * P
                tail_rows = LAST_ROWS if g is TGRP - 1 else P
                sp.dma_start(xg[:, 0:TBLK - 1, :], blocked(x[ds(first, whole), :])).then_inc(x_loaded, 16)
                sp.dma_start(xg[0:tail_rows, TBLK - 1, :], x[ds(first + whole, tail_rows), :]).then_inc(x_loaded, 16)

            def store(g):
                first = g * TBLK * P
                whole = (TBLK - 1) * P
                tail_rows = LAST_ROWS if g is TGRP - 1 else P
                sp.dma_start(blocked(out[ds(first, whole), :]),
                             rows[:, ds(g * TBLK, TBLK - 1), 0:D]).then_inc(out_stored, 16)
                sp.dma_start(out[ds(first + whole, tail_rows), :],
                             rows[0:tail_rows, ds(g * TBLK + TBLK - 1, 1), 0:D].rearrange("p a d -> p (a d)"))\
                    .then_inc(out_stored, 16)

            def group_io(g, nxt):
                if nxt is not None:
                    sp.wait_ge(h_free, g + 1)
                    load_h(nxt)
                sp.wait_ge(x2_ready, g + 1)
                sp.dma_start(blocked(x2_dram[ds(g * TBLK * P, TBLK * P), :]), x2g).then_inc(x2_stored, 16)
                if nxt is not None:
                    sp.wait_ge(x_free, g + 1)
                    load_x(nxt)

            sp.wait_ge(added, 2 * CHUNKS)
            load_h(0)
            load_x(0)
            with sp.Fori(0, TGRP - 2) as g:
                group_io(g, g + 1)
            group_io(TGRP - 2, TGRP - 1)
            group_io(TGRP - 1, None)
            sp.wait_ge(u_ready, TGRP)
            for n, bias in enumerate((b1, b2)):
                for e in range(N_EXP):
                    sp.dma_start(rows[:, n * N_EXP + e, D:2 * D], bias[e, :].partition_broadcast(P)).then_inc(bias_loaded, 16)
            sp.wait_ge(ct_ready, 1)
            with nc.allow_non_contiguous_dma(reason="small table"):
                sp.dma_start(ct_dram.rearrange("(p n) -> p n", n=1), ct_i[:, :]).then_inc(ct_stored, 16)
            sp.wait_ge(ct_stored, 16)
            sp.dma_start(exp_row[:, EXP_TURN:EXP_TURN + P], ct_dram.rearrange("(a n) -> a n", a=1)).then_inc(ct_loaded, 16)

            def store_y(m, slot):
                sp.wait_ge(y_ready, m + 1)
                sp.dma_start(y_dram[ds(m * P, P), :], yc[:, slot, :]).then_inc(y_stored[slot], 16)

            with sp.Fori(0, EXP_CHUNKS // EXP_TURN) as i:
                for u in range(EXP_TURN):
                    store_y(EXP_TURN * i + u, u)
            with sp.Fori(0, TGRP - 1) as g:
                sp.wait_ge(grp_done, g + 1)
                store(g)
            sp.wait_ge(grp_done, TGRP)
            store(TGRP - 1)
            sp.wait_ge(out_stored, 32 * TGRP)

        @block.gpsimd
        def _(pool):
            n = [0]

            def step(ins):
                n[0] += 1
                ins.then_inc(pool_step, 1)
                pool.wait_ge(pool_step, n[0])

            step(pool.memset(ones[:, :], 1.0))
            pool.memset(rows[:, BLOCKS - 1, 0:D], 0.0).then_inc(pad_set, 1)
            step(pool.iota(iota_i[:, :], [[1, CHUNKS]], base=0, channel_multiplier=0))
            step(pool.iota(kpos_i[:, :], [[P, BLK_COLS // P]], base=0, channel_multiplier=1))
            step(pool.memset(eps_t[:, :], EPS))
            step(pool.affine_select(out=upper[:, :], in_=ones[:, :], compare_op=ALU.is_gt, fill=0.0, base=0,
                                    pattern=[[1, P]], channel_multiplier=-1))
            pool.affine_select(out=ident[:, :], in_=ones[:, :], compare_op=ALU.is_equal, fill=0.0, base=0,
                               pattern=[[1, P]], channel_multiplier=-1).then_inc(consts, 1)
            pool.wait_ge(pos_ready, 1)

            def add_places(b, par, first=False):
                if not first:
                    pool.wait_ge(pick_done, b)
                pool.wait_ge(placed, b + 1)
                pool.tensor_tensor(pos_f, pos_f, picked[:, par, :], ALU.add).then_inc(pick_done, 1)

            add_places(0, 0, True)
            with pool.Fori(0, BLOCKS // 2) as i:
                add_places(2 * i + 1, 1)
                add_places(2 * i + 2, 0)

            pool.wait_ge(pairs_zero, 16)

            def scatter(i):
                for h in range(2):
                    pool.wait_ge(pairs_staged, 2 * i + h + 1)
                    pool.sem_inc(pool_turn, 1)
                    for c in range(GROUP):
                        pool.indirect_dma_start(pair_dram, bass.IndirectOffsetOnAxis(ap=stage[:, h, c:c + 1], axis=0),
                                                pair_stage[:, h, c, :], None).then_inc(scattered[GROUP * h + c], 16)

            with pool.Fori(0, POOL_COLS // (2 * GROUP)) as i:
                scatter(i)
            pool.wait_ge(ssq_done, BLOCKS)
            pool.memset(rows[:, :, D:2 * D + 1], 0.0).then_inc(rows_zero, 1)

            def gather_turn(table, base, i, first):
                for h in range(2):
                    for_half = base + TURN * i + GROUP * h
                    pool.wait_ge(staged, 2 * (base // TURN) + 2 * i + h + 1)
                    if not first:
                        pool.wait_ge(mult_done, for_half - TURN + GROUP)
                    pool.sem_inc(pool_turn, 1)
                    for c in range(GROUP):
                        slot = GROUP * h + c
                        pool.indirect_dma_start(ring[:, slot, 0:D], None, table,
                                                bass.IndirectOffsetOnAxis(ap=stage[:, h, c:c + 1], axis=0))\
                            .then_inc(gathered[slot], 16)

            def gather_pass(table, base):
                gather_turn(table, base, 0, True)
                with pool.Fori(1, CHUNKS // TURN) as i:
                    gather_turn(table, base, i, False)

            pool.wait_ge(xn_stored, 16)
            gather_pass(xn_dram, 0)
            for g in range(TGRP):
                pool.wait_ge(h_stored[g], 16)
                pool.memset(rows[:, g * TBLK:(g + 1) * TBLK, 0:2 * D], 0.0).then_inc(rows_clear, 1)
            gather_pass(h_dram, CHUNKS)

            def sums_of(g):
                pool.wait_ge(s1_ready, g + 1)
                pool.tensor_tensor(ug, ug, hg, ALU.mult).then_inc(h_free, 1)
                pool.wait_ge(h_free, g + 1)
                pool.tensor_tensor(ug, ug, rows[:, ds(g * TBLK, TBLK), D:2 * D], ALU.add).then_inc(u_ready, 1)

            def start_of(g):
                pool.wait_ge(x2_ready, g + 1)
                pool.tensor_tensor(rows[:, ds(g * TBLK, TBLK), 0:D], xg, x2g, ALU.add).then_inc(x_free, 1)

            sums_of(0)
            with pool.Fori(0, TGRP - 1) as g:
                start_of(g)
                sums_of(g + 1)
            start_of(TGRP - 1)

            def gather(table, slot, index, arrived):
                pool.indirect_dma_start(slot, None, table, bass.IndirectOffsetOnAxis(ap=index, axis=0)).then_inc(arrived, 16)

            def gather_tokens(i, first):
                for h in range(2):
                    pool.wait_ge(xstaged, 2 * i + h + 1)
                    if not first:
                        pool.wait_ge(t1_done, EXP_TURN * (i - 1) + 2 * h + 2)
                    pool.sem_inc(pool_turn, 1)
                    for c in range(2):
                        gather(x2_dram, xc[:, 2 * h + c, :], stage[:, h, c:c + 1], xc_in[2 * h + c])

            pool.wait_ge(x2_stored, 16 * TGRP)
            pool.wait_ge(x_free, TGRP)
            gather_tokens(0, True)
            with pool.Fori(1, EXP_CHUNKS // EXP_TURN) as i:
                gather_tokens(i, False)

            def gather_results(g, first):
                for h in range(TOP_K):
                    pool.wait_ge(ystaged, 2 * g + h + 1)
                    if not first:
                        pool.wait_ge(combined, 2 * TBLK * (g - 1) + TBLK * (h + 1))
                    pool.sem_inc(pool_turn, 1)
                    for c in range(TBLK):
                        gather(y_dram, yg[:, TBLK * h + c, :], stage[:, h, c:c + 1], yg_in[TBLK * h + c])

            for u in range(EXP_TURN):
                pool.wait_ge(y_stored[u], 16 * (EXP_CHUNKS // EXP_TURN))
            gather_results(0, True)
            with pool.Fori(1, TGRP) as g:
                gather_results(g, False)

        @block.scalar
        def _(act):
            act.wait_ge(s_x, 32)

            def total(t):
                row = rows[:, ds(t, 1), 0:D].rearrange("p a d -> p (a d)")
                act.activation(row, row, ACT.Identity, accum_out=sums[:, ds(t, 1)]).then_inc(sums_done, 1)

            total(0)
            with act.Fori(1, BLOCKS) as t:
                total(t)
            act.wait_ge(sums_done, BLOCKS)
            act.mul(nmean[:, :], sums[:, :], -1.0 / D).then_inc(act_step, 1)
            act.wait_ge(act_step, 1)
            with act.Fori(0, BLOCKS) as t:
                act.activation(rows[:, ds(t, 1), D:2 * D].rearrange("p a d -> p (a d)"),
                               rows[:, ds(t, 1), 0:D].rearrange("p a d -> p (a d)"), ACT.Square,
                               bias=nmean[:, ds(t, 1)], accum_out=ssq[:, ds(t, 1)]).then_inc(ssq_done, 1)
            act.wait_ge(ssq_done, BLOCKS)
            act.wait_ge(consts, 1)
            act.activation(std[:, :], ssq[:, :], ACT.Sqrt, bias=eps_t[:, :], scale=1.0 / D).then_inc(std_done, 1)
            act.wait_ge(rstd_ready, 1)
            with act.Fori(0, BLOCKS) as t:
                row = rows[:, ds(t, 1), 0:D].rearrange("p a d -> p (a d)")
                act.activation(row, row, ACT.Identity, bias=nmr[:, ds(t, 1)], scale=rstd[:, ds(t, 1)]).then_inc(xn_done, 1)


            def put_pairs(i, h, first):
                if not first:
                    for c in range(GROUP):
                        act.wait_ge(scattered[GROUP * h + c], 16 * i)
                at = 2 * GROUP * i + GROUP * h
                act.copy(pair_stage[:, h, :, :], pair_f[:, ds(at, GROUP), :])
                act.copy(stage[:, h, :], place_i[:, ds(at, GROUP)]).then_inc(pairs_staged, 1)

            act.wait_ge(pairs_ready, 1)
            put_pairs(0, 0, True)
            put_pairs(0, 1, True)
            with act.Fori(1, POOL_COLS // (2 * GROUP)) as i:
                put_pairs(i, 0, False)
                put_pairs(i, 1, False)

            def put(i, h):
                act.copy(stage[:, h, :], idx_i[:, ds(TURN * i + GROUP * h, GROUP)]).then_inc(staged, 1)

            def stage_pass(base, squares):
                turns = base // TURN

                def half(i, h, last):
                    for c in range(GROUP):
                        slot = GROUP * h + c
                        act.wait_ge(gathered[slot], 16 * (turns + i + 1))
                        if squares:
                            act.activation(ring[:, slot, D:2 * D], ring[:, slot, 0:D], ACT.Square).then_inc(squared, 1)
                    if not last:
                        put(i + 1, h)

                put(0, 0)
                put(0, 1)
                with act.Fori(0, CHUNKS // TURN - 1) as i:
                    half(i, 0, False)
                    half(i, 1, False)
                half(CHUNKS // TURN - 1, 0, True)
                half(CHUNKS // TURN - 1, 1, True)

            act.wait_ge(sort_ready, 2)
            stage_pass(0, False)

            def copy_tr(t, par, early=False):
                act.wait_ge(tr_done, t + 1)
                if not early:
                    act.wait_ge(hmm_done, t - 1)
                act.copy(tr_sb[:, par, :, :].rearrange("p k r -> p (k r)"), bank[4 + par]).then_inc(tr_copied, 1)

            def relu(t, par):
                act.wait_ge(hmm_done, t + 1)
                act.activation(rows[:, ds(t, 1), 0:D].rearrange("p a d -> p (a d)"), bank[6 + par][:, 0:D],
                               ACT.Relu).then_inc(h_made, 1)

            copy_tr(0, 0, True)
            copy_tr(1, 1, True)
            relu(0, 0)
            with act.Fori(1, BLOCKS // 2) as i:
                copy_tr(2 * i, 0)
                relu(2 * i - 1, 1)
                copy_tr(2 * i + 1, 1)
                relu(2 * i, 0)
            copy_tr(BLOCKS - 1, 0)
            relu(BLOCKS - 2, 1)
            relu(BLOCKS - 1, 0)
            act.wait_ge(h_made, BLOCKS)
            stage_pass(CHUNKS, True)

            def scale_h(g, first=False):
                act.wait_ge(h_loaded, 16 * (g + 1))
                if not first:
                    act.wait_ge(norm_step, NORM_STEPS * (g - 1) + 1)
                for j in range(TBLK):
                    act.activation(ug[:, j, :], hg[:, j, :], ACT.Identity, scale=deg[:, ds(g * TBLK + j, 1)])\
                        .then_inc(hd_ready, 1)

            def tanhs(g):
                act.wait_ge(u_ready, g + 1)
                for j in range(TBLK):
                    act.activation(ug[:, j, :], ug[:, j, :], ACT.Tanh, scale=rden[:, ds(g * TBLK + j, 1)]).then_inc(th_ready, 1)

            def stds(g):
                act.wait_ge(var_ready, g + 1)
                act.activation(t7[:, 1, :], t7[:, 0, :], ACT.Sqrt).then_inc(sd_ready, 1)

            def copy_xt(g, first=False):
                if not first:
                    act.wait_ge(lg_done, g)
                for r in range(4):
                    n = 2 * TBLK * P - 512 * r if r == 3 else 512
                    act.wait_ge(xt_done, 4 * g + r + 1)
                    act.copy(xT_flat[:, 512 * r:512 * r + n], bank[4 + r % 2][:, 0:n]).then_inc(xt_copied, 1)

            def exps(g):
                act.wait_ge(lsub_ready, g + 1)
                act.activation(lg[:, 1, :, :], lg[:, 0, :, :], ACT.Exp).then_inc(ex_ready, 1)

            act.wait_ge(added, 2 * CHUNKS)
            scale_h(0, True)
            tanhs(0)
            scale_h(1)
            stds(0)
            copy_xt(0, True)
            tanhs(1)
            with act.Fori(1, TGRP - 1) as g:
                scale_h(g + 1)
                stds(g)
                exps(g - 1)
                copy_xt(g)
                tanhs(g + 1)
            stds(TGRP - 1)
            exps(TGRP - 2)
            copy_xt(TGRP - 1)
            exps(TGRP - 1)

            def put_tokens(i, h):
                act.copy(stage[:, h, 0:2], tok_sorted[:, ds(EXP_TURN * i + 2 * h, 2)]).then_inc(xstaged, 1)

            def expert_step(m, u, last_turn):
                par = u % 2
                if m is not None:
                    if u % 2 == 1 and not last_turn:
                        for c in (u - 1, u):
                            act.wait_ge(xc_in[c], 16 * (m_turn(m, u) + 1))
                        put_tokens(m_turn(m, u) + 1, u // 2)
                    act.wait_ge(t1_done, m + 1)
                    if not (isinstance(m, int) and m < 2):
                        act.wait_ge(l1_done, m - 1)
                    act.copy(xcT[:, par, :], bank[par][:, 0:D]).then_inc(xcT_ready, 1)

            def gelu_step(m, par):
                act.wait_ge(hb_ready, m + 1)
                act.activation(hid[:, par, :], hid[:, par, :], ACT.Gelu).then_inc(gelu_done, 1)

            def m_turn(m, u):
                return m // EXP_TURN if isinstance(m, int) else turn_now[0]

            turn_now = [None]

            act.wait_ge(picks_ready, 1)
            put_tokens(0, 0)
            put_tokens(0, 1)
            for u in range(EXP_TURN):
                expert_step(u, u, False)
                if u >= 1:
                    gelu_step(u - 1, (u - 1) % 2)
            with act.Fori(1, EXP_CHUNKS // EXP_TURN - 1) as i:
                turn_now[0] = i
                for u in range(EXP_TURN):
                    expert_step(EXP_TURN * i + u, u, False)
                    gelu_step(EXP_TURN * i + u - 1, (u - 1) % 2)
            for u in range(EXP_TURN):
                m = EXP_CHUNKS - EXP_TURN + u
                expert_step(m, u, True)
                gelu_step(m - 1, (m - 1) % 2)
            gelu_step(EXP_CHUNKS - 1, (EXP_CHUNKS - 1) % 2)

            def put_rows(g, h, first):
                if not first:
                    for c in range(TBLK):
                        act.wait_ge(yg_in[TBLK * h + c], 16 * g)
                act.copy(stage[:, h, 0:TBLK], pick_row[:, ds(h * BLOCKS + g * TBLK, TBLK)]).then_inc(ystaged, 1)

            for u in range(EXP_TURN):
                act.wait_ge(xc_in[u], 16 * (EXP_CHUNKS // EXP_TURN))
            put_rows(0, 0, True)
            put_rows(0, 1, True)
            with act.Fori(1, TGRP) as g:
                put_rows(g, 0, False)
                put_rows(g, 1, False)

        @block.vector
        def _(dve):
            n = [0]

            def step(ins):
                n[0] += 1
                ins.then_inc(dve_step, 1)
                dve.wait_ge(dve_step, n[0])

            v = nc.vector
            v.memset(src_i[:, EDGE_COLS:IN_COLS], BLOCKS * P).then_inc(pad_set, 1)
            v.memset(dst_i[:, EDGE_COLS:IN_COLS], 0).then_inc(pad_set, 1)
            step(v.memset(zero_bf[:, :], 0.0))
            v.sem_inc(pad_set, 1)
            dve.wait_ge(consts, 1)
            step(v.tensor_copy(iota_h[:, :], iota_i[:, :]))
            step(v.tensor_copy(kpos_f[:, :], kpos_i[:, :]))
            step(v.tensor_scalar(iota1_f[:, :], iota_i[:, 0:P], 1.0, None, ALU.add))
            step(v.tensor_copy(iota8_f[:, :], iota_i[:, 0:N_EXP]))
            dve.wait_ge(s_edges, 64)
            step(v.tensor_scalar(tmp_i, src_i, 7, None, ALU.arith_shift_right))
            step(v.tensor_scalar(blk_f, tmp_i, 1.0, None, ALU.add))
            step(v.tensor_scalar(tmp_i, src_i, P - 1, None, ALU.bitwise_and))
            step(v.tensor_scalar(rowlo_f, tmp_i, 1.0, None, ALU.add))
            step(v.tensor_scalar(tmp_i, dst_i, float(COL_BIAS), None, ALU.add))
            step(v.tensor_scalar(colbits.bitcast(i32), tmp_i, 16, None, ALU.logical_shift_left))
            step(v.tensor_scalar(pos_f, blk_f, float(BLOCKS), float(NOWHERE), ALU.is_gt, ALU.mult))
            v.sem_inc(pos_ready, 1)
            with dve.Fori(0, BLOCKS) as b:
                v.tensor_scalar(masks[:, ds(b, 1), :].rearrange("p a c -> p (a c)"), blk_f, iota1_f[:, ds(b, 1)],
                                0.0, ALU.is_equal, ALU.add, accum_out=counts[:, ds(b, 1)]).then_inc(mask_done, 1)
            dve.wait_ge(mask_done, BLOCKS)
            step(v.tensor_copy(off_f[:, :], counts[:, :]))
            v.sem_inc(counts_ready, 1)
            dve.wait_ge(totals_done, 1)
            step(v.tensor_scalar(tot_i[:, :], bank[1][:, 0:BLOCKS], float(P - 1), None, ALU.add))
            step(v.tensor_scalar(tot_i[:, :], tot_i[:, :], 7, None, ALU.arith_shift_right))
            step(v.tensor_copy(nch_f[:, :], tot_i[:, :]))
            step(v.memset(start_f[:, 0:1], 0.0))
            step(v.tensor_tensor_scan(start_f[:, 1:BLOCKS + 1], nch_f[:, :], nch_f[:, :], 0.0, ALU.add, ALU.max))
            step(v.scalar_tensor_tensor(off_f[:, :], start_f[:, 0:BLOCKS], float(P), bank[0][:, 0:BLOCKS],
                                        ALU.mult, ALU.add))
            q = BLK_COLS // P
            step(v.tensor_tensor(cmp_f[:, :, :], kpos_f[:, :].unsqueeze(2).to_broadcast([P, q, BLOCKS]),
                                 start_f[:, 0:BLOCKS].unsqueeze(1).to_broadcast([P, q, BLOCKS]), ALU.is_ge))
            step(v.tensor_reduce(blk_cf[:, :], cmp_f[:, :, :], AX.X, ALU.add))
            v.tensor_scalar(blk_ci[:, :], blk_cf[:, :], -1.0, float(BLOCKS - 1), ALU.add, ALU.min).then_inc(blk_ready, 1)
            def places(b, par, first):
                m = masks[:, ds(b, 1), :].rearrange("p a c -> p (a c)")
                running = ps[:, 1024 * (1 + par):1024 * (1 + par) + IN_COLS]
                if not first:
                    dve.wait_ge(pick_done, b - 1)
                v.tensor_tensor_scan(running, m, m, off_f[:, ds(b, 1)], ALU.add, ALU.max).then_inc(scan_done, 1)
                dve.wait_ge(scan_done, b + 1)
                v.tensor_tensor(picked[:, par, :], running, m, ALU.mult).then_inc(placed, 1)

            places(0, 0, True)
            places(1, 1, True)
            places(2, 0, False)
            with dve.Fori(1, BLOCKS // 4) as i:
                places(2 * i + 1, 1, False)
                places(2 * i + 2, 0, False)
            dve.wait_ge(std_done, 1)
            step(v.reciprocal(rstd[:, :], std[:, :]))
            v.tensor_tensor(nmr[:, :], nmean[:, :], rstd[:, :], ALU.mult).then_inc(rstd_ready, 1)
            with dve.Fori(BLOCKS // 4, BLOCKS // 2) as i:
                places(2 * i + 1, 1, False)
                places(2 * i + 2, 0, False)
            dve.wait_ge(pick_done, BLOCKS)
            step(v.tensor_scalar(tmp_i, pos_f, -1.0, None, ALU.add))
            step(v.tensor_scalar(src_i, tmp_i, 7, None, ALU.arith_shift_right))
            step(v.tensor_copy(hi_f, src_i))
            step(v.tensor_scalar(src_i, tmp_i, P - 1, None, ALU.bitwise_and))
            step(v.tensor_copy(lo_f, src_i))
            step(v.scalar_tensor_tensor(place_i, lo_f, float(CHUNKS), hi_f, ALU.mult, ALU.add))
            step(v.tensor_copy(pair_f[:, :, 0], dst_i[:, 0:POOL_COLS]))
            step(v.tensor_copy(pair_f[:, :, 1], rowlo_f[:, 0:POOL_COLS]))
            v.sem_inc(pairs_ready, 1)
            def one_hots(i, first):
                for u in range(IN_UNROLL):
                    j = POOL_COLS + i * IN_UNROLL + u
                    if not first:
                        dve.wait_ge(sorted_cols, (i - 1) * IN_UNROLL + u + 1)
                    v.tensor_scalar(hi_oh[:, u, :], iota_h[:, :], hi_f[:, ds(j, 1)], None, ALU.is_equal)
                    v.tensor_scalar(lo_col[:, u, :], iota_h[:, 0:P], lo_f[:, ds(j, 1)], colbits[:, ds(j, 1)],
                                    ALU.is_equal, ALU.mult)
                    v.tensor_scalar(lo_row[:, u, :], iota_h[:, 0:P], lo_f[:, ds(j, 1)], rowlo_f[:, ds(j, 1)],
                                    ALU.is_equal, ALU.mult).then_inc(oh_ready, 1)

            one_hots(0, True)
            with dve.Fori(1, (IN_COLS - POOL_COLS) // IN_UNROLL) as i:
                one_hots(i, False)
            dve.wait_ge(sorted_cols, IN_COLS - POOL_COLS + 1)
            bits = rflat[:, 0:CHUNKS]
            for half in range(2):
                v.tensor_copy(bits[:, half * HALF:(half + 1) * HALF], bank[half][:, 0:HALF])
                v.tensor_copy(erow[:, half * HALF:(half + 1) * HALF], bank[2 + half][:, 0:HALF])
            step(v.memset(erow[:, CHUNKS:CHUNKS + TURN], 0.0))
            step(v.tensor_scalar(bits.bitcast(i32), bits.bitcast(i32), 16, None, ALU.logical_shift_right))
            step(v.tensor_scalar(idx_i[:, :], bits.bitcast(i32), float(-COL_BIAS), 0.0, ALU.add, ALU.max))
            dve.wait_ge(pairs_loaded, 16)
            step(v.tensor_tensor(erow[:, 0:CHUNKS], erow[:, 0:CHUNKS], merged[:, :, 1], ALU.add))
            v.tensor_tensor(idx_i[:, :], merged[:, :, 0], idx_i[:, :], ALU.add).then_inc(sort_ready, 2)


            def make_one_hot(k, slot):
                v.tensor_scalar(onehot[:, slot // GROUP, slot % GROUP, :], iota1_f[:, :], erow[:, ds(k, 1)], None,
                                ALU.is_equal).then_inc(oh_made, 1)

            def add_half(i, h, base, lo, width, first):
                k0 = TURN * i + GROUP * h
                _, blocks = nc.values_load_multi_w_load_instructions(
                    blk_row[0:1, ds(k0, GROUP)], engines=[mybir.EngineType.DVE], min_val=0, max_val=BLOCKS - 1,
                    skip_runtime_bounds_check_because="the table is clamped to 0..BLOCKS-1 when it is made")
                for c in range(GROUP):
                    k = base + k0 + c
                    row = rows[:, ds(blocks[c], 1), lo:lo + width].rearrange("p a d -> p (a d)")
                    if not (first and c == 0):
                        dve.wait_ge(added, k)
                    dve.wait_ge(mult_done, k + 1)
                    v.tensor_tensor(row, row, bank[(GROUP * h + c) % ACC_BUFS][:, 0:width], ALU.add).then_inc(added, 1)
                    make_one_hot(k0 + c + TURN, GROUP * h + c)

            def add_pass(base, lo, width):
                for k in range(TURN):
                    make_one_hot(k, k)

                def turn(i, first):
                    add_half(i, 0, base, lo, width, first)
                    add_half(i, 1, base, lo, width, False)

                turn(0, base == 0)
                with dve.Fori(1, CHUNKS // TURN) as i:
                    turn(i, False)

            dve.wait_ge(sort_ready, 2)
            step(v.memset(ring[:, :, D:D + 1], 1.0))
            dve.wait_ge(blk_loaded, 16)
            dve.wait_ge(rows_zero, 1)
            add_pass(0, D, D + 1)

            dve.wait_ge(added, CHUNKS)
            step(v.tensor_copy(deg[:, :], rows[:, :, 2 * D]))
            step(v.tensor_scalar(rden[:, :], deg[:, :], 1.0, None, ALU.max))
            step(v.reciprocal(rden[:, :], rden[:, :]))

            def mean(t, par, early=False):
                if not early:
                    dve.wait_ge(tr_done, t - 1)
                v.tensor_copy(operand[:, par, 0:D], rows[:, ds(t, 1), 0:D].rearrange("p a d -> p (a d)"))
                v.tensor_scalar(operand[:, par, D:2 * D], rows[:, ds(t, 1), D:2 * D].rearrange("p a d -> p (a d)"),
                                rden[:, ds(t, 1)], None, ALU.mult).then_inc(mean_made, 1)

            mean(0, 0, True)
            mean(1, 1, True)
            with dve.Fori(1, BLOCKS // 2) as i:
                mean(2 * i, 0)
                mean(2 * i + 1, 1)
            mean(BLOCKS - 1, 0)

            dve.wait_ge(rows_clear, TGRP)
            add_pass(CHUNKS, 0, 2 * D)

            def chain(done, per):
                n = [0]

                def link(ins, g):
                    n[0] = n[0] % per + 1
                    ins.then_inc(done, 1)
                    dve.wait_ge(done, g * per + n[0])

                return link

            col7 = lambda r: t7[:, r, :]

            def sub_products(g):
                dve.wait_ge(hd_ready, TBLK * (g + 1))
                v.scalar_tensor_tensor(ug, rows[:, ds(g * TBLK, TBLK), 0:D], -2.0, ug, ALU.mult, ALU.add)\
                    .then_inc(s1_ready, 1)

            norm_link = chain(norm_step, NORM_STEPS)

            def norm(g):
                dve.wait_ge(x_loaded, 32 * (g + 1))
                dve.wait_ge(th_ready, TBLK * (g + 1))
                norm_link(v.tensor_tensor(xg, xg, ug, ALU.add), g)
                for j in range(TBLK):
                    last = v.bn_stats(bn6[:, j, :], xg[:, j, :])
                norm_link(last, g)
                v.sem_inc(tail_turn, 1)
                for j in range(TBLK):
                    last = v.bn_aggr(mv[:, j, :], bn6[:, j, :])
                norm_link(last, g)
                v.tensor_scalar(col7(0), mv[:, :, 1], EPS, None, ALU.add).then_inc(var_ready, 1)

            scale_link = chain(scale_step, 5)

            def scale(g, first=False):
                dve.wait_ge(sd_ready, g + 1)
                scale_link(v.reciprocal(col7(2), col7(1)), g)
                scale_link(v.tensor_tensor(col7(3), col7(2), col7(2), ALU.mult), g)
                scale_link(v.tensor_tensor(col7(3), col7(3), col7(0), ALU.mult), g)
                scale_link(v.tensor_scalar(col7(3), col7(3), -0.5, 1.5, ALU.mult, ALU.add), g)
                scale_link(v.tensor_tensor(col7(2), col7(2), col7(3), ALU.mult), g)
                if not first:
                    dve.wait_ge(x2_stored, 16 * g)
                    dve.wait_ge(x_free, g)
                    dve.wait_ge(xt_done, 4 * g)
                for j in range(TBLK):
                    last = v.tensor_scalar(x2g[:, j, :], xg[:, j, :], mv[:, j, 0:1], t7[:, 2, j:j + 1],
                                           ALU.subtract, ALU.mult)
                last.then_inc(x2_ready, 1)

            def wide(ap):
                return ap.unsqueeze(2).to_broadcast([P, TBLK, N_EXP])

            logits = bank[6][:, 0:TBLK * N_EXP].rearrange("p (j e) -> p j e", j=TBLK)
            peak_link = chain(peak_step, 1)

            def less_peak(g):
                dve.wait_ge(lg_done, g + 1)
                peak_link(v.tensor_reduce(col7(4), logits, AX.X, ALU.max), g)
                v.tensor_tensor(lg[:, 0, :, :], logits, wide(col7(4)), ALU.subtract).then_inc(lsub_ready, 1)

            share_link = chain(share_step, 9)

            def shares(g):
                dve.wait_ge(ex_ready, g + 1)
                ex = lg[:, 1, :, :]
                share_link(v.tensor_reduce(col7(4), ex, AX.X, ALU.add), g)
                share_link(v.reciprocal(col7(4), col7(4)), g)
                share_link(v.tensor_tensor(ex, ex, wide(col7(4)), ALU.mult), g)
                v.sem_inc(tail_turn, 1)
                for j in range(TBLK):
                    last = v.max(top8[:, j, :], lg[:, 1, j, :])
                share_link(last, g)
                v.sem_inc(tail_turn, 1)
                for j in range(TBLK):
                    last = v.max_index(idx8[:, j, :], top8[:, j, :], lg[:, 1, j, :])
                share_link(last, g)
                share_link(v.tensor_tensor(col7(5), top8[:, :, 0], top8[:, :, 1], ALU.add), g)
                share_link(v.tensor_scalar(col7(5), col7(5), 1e-12, None, ALU.max), g)
                share_link(v.reciprocal(col7(5), col7(5)), g)
                for r in range(TOP_K):
                    v.tensor_copy(expert_f[:, r, ds(g * TBLK, TBLK)], idx8[:, :, r])
                    last = v.tensor_tensor(share[:, r, ds(g * TBLK, TBLK)], top8[:, :, r], col7(5), ALU.mult)
                share_link(last, g)

            dve.wait_ge(added, 2 * CHUNKS)
            sub_products(0)
            norm(0)
            scale(0, True)
            sub_products(1)
            with dve.Fori(1, TGRP - 1) as g:
                norm(g)
                less_peak(g - 1)
                scale(g)
                sub_products(g + 1)
                shares(g - 1)
            norm(TGRP - 1)
            less_peak(TGRP - 2)
            scale(TGRP - 1)
            shares(TGRP - 2)
            less_peak(TGRP - 1)
            shares(TGRP - 1)

            chosen = expert_f[:, :, :].rearrange("p r t -> p (r t)")
            step(v.tensor_tensor(pmask, chosen.unsqueeze(1).to_broadcast([P, N_EXP, picks]),
                                 iota8_f[:, :].unsqueeze(2).to_broadcast([P, N_EXP, picks]), ALU.is_equal))
            v.tensor_reduce(c8[:, 0, 0:N_EXP], pmask, AX.X, ALU.add).then_inc(pcounts_ready, 1)
            dve.wait_ge(ptotals_done, 1)
            step(v.tensor_scalar(c8_i[:, :], bank[1][:, 0:N_EXP], float(P - 1), None, ALU.add))
            step(v.tensor_scalar(c8_i[:, :], c8_i[:, :], 7, None, ALU.arith_shift_right))
            step(v.tensor_copy(c8[:, 1, 0:N_EXP], c8_i[:, :]))
            step(v.memset(c8[:, 2, 0:1], 0.0))
            step(v.tensor_tensor_scan(c8[:, 2, 1:N_EXP + 1], c8[:, 1, 0:N_EXP], c8[:, 1, 0:N_EXP], 0.0, ALU.add, ALU.max))
            step(v.scalar_tensor_tensor(c8[:, 3, 0:N_EXP], c8[:, 2, 0:N_EXP], float(P), bank[0][:, 0:N_EXP],
                                        ALU.mult, ALU.add))
            step(v.tensor_tensor(c8[:, 0, 0:N_EXP], kpos_f[:, 0:1].to_broadcast([P, N_EXP]), c8[:, 2, 0:N_EXP], ALU.is_ge))
            step(v.tensor_reduce(ct_f[:, :], c8[:, 0, 0:N_EXP], AX.X, ALU.add))
            v.tensor_scalar(ct_i[:, :], ct_f[:, :], -1.0, float(N_EXP - 1), ALU.add, ALU.min).then_inc(ct_ready, 1)
            for e in range(N_EXP):
                last = v.tensor_tensor_scan(pscan[:, e, :], pmask[:, e, :], pmask[:, e, :], c8[:, 3, e:e + 1],
                                            ALU.add, ALU.max)
            step(last)
            step(v.tensor_tensor(pscan, pscan, pmask, ALU.mult))
            step(v.tensor_reduce(pick_pos[:, 0, :], pscan.rearrange("p e c -> p c e"), AX.X, ALU.add))
            step(v.tensor_scalar(pick_row, pick_pos[:, 0, :], -1.0, None, ALU.add))
            step(v.tensor_scalar(pick_tmp, pick_row, 7, None, ALU.arith_shift_right))
            step(v.tensor_copy(pick_pos[:, 1, :], pick_tmp))
            step(v.tensor_scalar(pick_tmp, pick_row, P - 1, None, ALU.bitwise_and))
            step(v.tensor_copy(pick_pos[:, 2, :], pick_tmp))
            step(v.memset(exp_row[:, 0:EXP_TURN], 0))
            v.sem_inc(pk_order, 1)
            step(v.tensor_scalar(tok_bits, iota_h[:, 0:BLOCKS], float(P), float(COL_BIAS), ALU.mult, ALU.add))
            step(v.tensor_scalar(tok_bits, tok_bits, kpos_f[:, 0:1], None, ALU.add))
            step(v.tensor_scalar(tok_bits, tok_bits, 16, None, ALU.logical_shift_left))

            def pick_one_hots(t, first):
                for r in range(TOP_K):
                    c = ds(r * BLOCKS + t, 1)
                    if not first:
                        dve.wait_ge(pk_done, 2 * t - 1 + r)
                    v.tensor_scalar(pk_hi[:, r, :], iota_h[:, 0:EXP_CHUNKS], pick_pos[:, 1, c], None, ALU.is_equal)
                    v.tensor_scalar(pk_lo[:, r, :], iota_h[:, 0:P], pick_pos[:, 2, c], tok_bits.bitcast(f32)[:, ds(t, 1)],
                                    ALU.is_equal, ALU.mult).then_inc(pk_ready, 1)

            pick_one_hots(0, True)
            with dve.Fori(1, BLOCKS) as t:
                pick_one_hots(t, False)
            dve.wait_ge(pk_done, PICKS + 1)
            step(v.tensor_copy(tok_sorted.bitcast(f32), bank[2][:, 0:EXP_CHUNKS]))
            step(v.tensor_scalar(tok_sorted, tok_sorted, 16, None, ALU.logical_shift_right))
            v.tensor_scalar(tok_sorted, tok_sorted, float(-COL_BIAS), 0.0, ALU.add, ALU.max).then_inc(picks_ready, 1)

            def add_b1(m, par, e):
                dve.wait_ge(l1_done, m + 1)
                if not (isinstance(m, int) and m < 2):
                    dve.wait_ge(t2_done, m - 1)
                v.tensor_tensor(hid[:, par, :], bank[2 + par][:, 0:D],
                                rows[:, ds(e, 1), D:2 * D].rearrange("p a d -> p (a d)"), ALU.add).then_inc(hb_ready, 1)

            def copy_hid(m, par):
                dve.wait_ge(t2_done, m + 1)
                if not (isinstance(m, int) and m < 2):
                    dve.wait_ge(l2_done, m - 1)
                v.tensor_copy(hidT[:, par, :], bank[4 + par][:, 0:D]).then_inc(hidT_ready, 1)

            def add_b2(m, slot, turn, e):
                dve.wait_ge(l2_done, m + 1)
                if turn is not None:
                    dve.wait_ge(y_stored[slot], 16 * turn)
                v.tensor_tensor(yc[:, slot, :], bank[6 + slot % 2][:, 0:D],
                                rows[:, ds(e + N_EXP, 1), D:2 * D].rearrange("p a d -> p (a d)"), ALU.add)\
                    .then_inc(y_ready, 1)

            def chunk_experts(i):
                _, e = nc.values_load_multi_w_load_instructions(
                    exp_row[0:1, ds(EXP_TURN * i, 2 * EXP_TURN)], engines=[mybir.EngineType.DVE],
                    min_val=0, max_val=N_EXP - 1,
                    skip_runtime_bounds_check_because="the table is clamped to 0..N_EXP-1 when it is made")
                return e

            def expert_turn(i, e, first, steps=EXP_TURN):
                for u in range(steps):
                    m = EXP_TURN * i + u
                    if (not first or u >= 1) and (steps == EXP_TURN or u < 1):
                        add_b1(m - 1, (u - 1) % 2, e[EXP_TURN + u - 1])
                    if (not first or u >= 2) and (steps == EXP_TURN or u < 2):
                        copy_hid(m - 2, u % 2)
                    if not first or u >= 3:
                        slot = (u - 3) % EXP_TURN
                        used = i if u >= 3 else i - 1
                        never = isinstance(used, int) and used == 0
                        add_b2(m - 3, slot, None if never else used, e[EXP_TURN + u - 3])

            dve.wait_ge(ct_loaded, 16)
            dve.wait_ge(bias_loaded, 16 * 2 * N_EXP)
            expert_turn(0, chunk_experts(0), True)
            expert_turn(1, chunk_experts(1), False)
            with dve.Fori(2, EXP_CHUNKS // EXP_TURN) as i:
                expert_turn(i, chunk_experts(i), False)
            expert_turn(EXP_CHUNKS // EXP_TURN, chunk_experts(EXP_CHUNKS // EXP_TURN), False, steps=3)

            def combine(g):
                for r in range(TOP_K):
                    for j in range(TBLK):
                        t = g * TBLK + j
                        if r:
                            dve.wait_ge(combined, 2 * TBLK * g + j + 1)
                        dve.wait_ge(yg_in[TBLK * r + j], 16 * (g + 1))
                        row = rows[:, ds(t, 1), 0:D].rearrange("p a d -> p (a d)")
                        v.scalar_tensor_tensor(row, yg[:, TBLK * r + j, :], share[:, r, ds(t, 1)], row,
                                               ALU.mult, ALU.add).then_inc(combined, 1)
                dve.wait_ge(combined, 2 * TBLK * (g + 1))
                v.sem_inc(grp_done, 1)

            with dve.Fori(0, TGRP) as g:
                combine(g)

        @block.tensor
        def _(pe):
            mm = nc.tensor.matmul
            pe.wait_ge(consts, 1)
            pe.wait_ge(counts_ready, 1)
            mm(bank[0][:, 0:BLOCKS], upper[:, :], counts[:, :], start=True, stop=True)
            mm(bank[1][:, 0:BLOCKS], ones[:, :], counts[:, :], start=True, stop=True).then_inc(totals_done, 1)
            pe.wait_ge(pairs_ready, 1)

            def zero(start):
                for b in range(4):
                    last = mm(bank[b][:, 0:HALF], zero_bf[:, 0:P], zero_bf[:, :], start=start, stop=not start)
                return last

            zero(True)

            def sort(i):
                for u in range(IN_UNROLL):
                    pe.wait_ge(oh_ready, i * IN_UNROLL + u + 1)
                    for n, lo in enumerate((lo_col, lo_row)):
                        for half in range(2):
                            last = mm(bank[2 * n + half][:, 0:HALF], lo[:, u, :],
                                      hi_oh[:, u, half * HALF:(half + 1) * HALF], start=False, stop=False)
                    last.then_inc(sorted_cols, 1)

            sort(0)
            with pe.Fori(1, (IN_COLS - POOL_COLS) // IN_UNROLL) as i:
                sort(i)
            zero(False).then_inc(sorted_cols, 1)

            def multiply_turn(i, base, width, ready, first):
                for s in range(TURN):
                    k = base + TURN * i + s
                    pe.wait_ge(oh_made, made[0] + TURN * i + s + 1)
                    if not (first and s < ACC_BUFS):
                        pe.wait_ge(added, k - ACC_BUFS + 1)
                    if ready is None:
                        pe.wait_ge(gathered[s], 16 * (i + 1))
                    else:
                        pe.wait_ge(squared, TURN * i + s + 1)
                    mm(bank[s % ACC_BUFS][:, 0:width], onehot[:, s // GROUP, s % GROUP, :], ring[:, s, 0:width],
                       start=True, stop=True).then_inc(mult_done, 1)

            made = [0]

            def multiply_pass(base, width, ready):
                multiply_turn(0, base, width, ready, base == 0)
                with pe.Fori(1, CHUNKS // TURN) as i:
                    multiply_turn(i, base, width, ready, False)

            multiply_pass(0, D + 1, None)

            def transposes(t, par, early=False):
                pe.wait_ge(mean_made, t + 1)
                if not early:
                    pe.wait_ge(tr_copied, t - 1)
                for k in range(4):
                    last = nc.tensor.transpose(bank[4 + par][:, k * P:(k + 1) * P],
                                               operand[:, par, k * P:(k + 1) * P], ident[:, :])
                last.then_inc(tr_done, 1)

            def hidden(t, par, early=False):
                pe.wait_ge(tr_copied, t + 1)
                if not early:
                    pe.wait_ge(h_made, t - 1)
                o = bank[6 + par][:, 0:D]
                for k in range(4):
                    mm(o, tr_sb[:, par, k, :], (wr_sb if k < 2 else wn_sb)[:, k % 2, :], start=(k == 0), stop=False)
                mm(o, ones[0:1, :], gb_sb[:, :], start=False, stop=True).then_inc(hmm_done, 1)

            pe.wait_ge(w_gnn, 16 * 5)
            transposes(0, 0, True)
            transposes(1, 1, True)
            hidden(0, 0, True)
            hidden(1, 1, True)
            transposes(2, 0)
            with pe.Fori(1, BLOCKS // 2) as i:
                transposes(2 * i + 1, 1)
                hidden(2 * i, 0)
                transposes(2 * i + 2, 0)
                hidden(2 * i + 1, 1)
            hidden(BLOCKS - 1, 0)

            made[0] = CHUNKS + TURN
            multiply_pass(CHUNKS, 2 * D, squared)

            def transpose_x2(g, first=False):
                pe.wait_ge(x2_ready, g + 1)
                for r in range(4):
                    if not (first and r < 2):
                        pe.wait_ge(xt_copied, 4 * g + r - 1)
                    for n in range(4 * r, min(4 * r + 4, 2 * TBLK)):
                        k, j = n // TBLK, n % TBLK
                        last = nc.tensor.transpose(bank[4 + r % 2][:, (n % 4) * P:(n % 4 + 1) * P],
                                                   x2g[:, j, k * P:(k + 1) * P], ident[:, :])
                    last.then_inc(xt_done, 1)

            def route(g, first=False):
                pe.wait_ge(xt_copied, 4 * (g + 1))
                if not first:
                    pe.wait_ge(lsub_ready, g)
                for j in range(TBLK):
                    for k in range(2):
                        last = mm(bank[6][:, j * N_EXP:(j + 1) * N_EXP], xT[:, k, j * P:(j + 1) * P], rw_sb[:, k, :],
                                  start=(k == 0), stop=(k == 1))
                last.then_inc(lg_done, 1)

            pe.wait_ge(w_ffn, 16 * 6)
            transpose_x2(0, True)
            route(0, True)
            with pe.Fori(1, TGRP) as g:
                transpose_x2(g)
                route(g)
            pe.wait_ge(pcounts_ready, 1)
            mm(bank[0][:, 0:N_EXP], upper[:, :], c8[:, 0, 0:N_EXP], start=True, stop=True)
            mm(bank[1][:, 0:N_EXP], ones[:, :], c8[:, 0, 0:N_EXP], start=True, stop=True).then_inc(ptotals_done, 1)
            mm(bank[2][:, 0:EXP_CHUNKS], zero_bf[:, 0:P], zero_bf[:, 0:EXP_CHUNKS], start=True, stop=False)
            with pe.Fori(0, BLOCKS) as t:
                for r in range(TOP_K):
                    pe.wait_ge(pk_ready, TOP_K * t + r + 1)
                    mm(bank[2][:, 0:EXP_CHUNKS], pk_lo[:, r, :], pk_hi[:, r, :], start=False, stop=False)\
                        .then_inc(pk_done, 1)
            mm(bank[2][:, 0:EXP_CHUNKS], zero_bf[:, 0:P], zero_bf[:, 0:EXP_CHUNKS], start=False, stop=True)\
                .then_inc(pk_done, 1)

            def flip(m, out, rows2, ready, value, free, done):
                pe.wait_ge(ready, value)
                if not (isinstance(m, int) and m < 2):
                    pe.wait_ge(free, m - 1)
                for k in range(2):
                    last = nc.tensor.transpose(out[:, k * P:(k + 1) * P], rows2[:, k * P:(k + 1) * P], ident[:, :])
                last.then_inc(done, 1)

            def layer(m, out, left, w, e, ready, free, done):
                pe.wait_ge(ready, m + 1)
                if not (isinstance(m, int) and m < 2):
                    pe.wait_ge(free, m - 1)
                for k in range(2):
                    last = mm(out[:, 0:D], left[:, k * P:(k + 1) * P],
                              w[:, ds(e, 1), k, :].rearrange("p a d -> p (a d)"), start=(k == 0), stop=(k == 1))
                last.then_inc(done, 1)

            def expert_turn(i, first, steps=EXP_TURN):
                _, e = nc.values_load_multi_w_load_instructions(
                    exp_row[0:1, ds(EXP_TURN * i, 2 * EXP_TURN)], engines=[mybir.EngineType.PE],
                    min_val=0, max_val=N_EXP - 1,
                    skip_runtime_bounds_check_because="the table is clamped to 0..N_EXP-1 when it is made")
                for u in range(steps):
                    m = EXP_TURN * i + u
                    if steps == EXP_TURN:
                        flip(m, bank[u % 2], xc[:, u, :], xc_in[u], 16 * (i + 1), xcT_ready, t1_done)
                    if (not first or u >= 1) and (steps == EXP_TURN or u < 1):
                        par = (u - 1) % 2
                        layer(m - 1, bank[2 + par], xcT[:, par, :], w1_sb, e[EXP_TURN + u - 1], xcT_ready, hb_ready, l1_done)
                    if (not first or u >= 2) and (steps == EXP_TURN or u < 2):
                        par = u % 2
                        flip(m - 2, bank[4 + par], hid[:, par, :], gelu_done, m - 1, hidT_ready, t2_done)
                    if not first or u >= 3:
                        par = (u - 3) % 2
                        layer(m - 3, bank[6 + par], hidT[:, par, :], w2_sb, e[EXP_TURN + u - 3], hidT_ready, y_ready, l2_done)

            pe.wait_ge(ct_loaded, 16)
            pe.wait_ge(pk_order, 1)
            expert_turn(0, True)
            expert_turn(1, False)
            with pe.Fori(2, EXP_CHUNKS // EXP_TURN) as i:
                expert_turn(i, False)
            expert_turn(EXP_CHUNKS // EXP_TURN, False, steps=3)


_INS = ['x', 'src', 'dst', 'L0_gnn_W_root', 'L0_gnn_W_neigh', 'L0_gnn_b', 'L0_ffn_router_w', 'L0_ffn_w1',
        'L0_ffn_b1', 'L0_ffn_w2', 'L0_ffn_b2']


def kernel(**inputs):
    import numpy as _np
    import concourse.bacc as _bacc
    from concourse import mybir as _mybir
    from concourse.bass_utils import run_bass_kernel_spmd as _run

    nc = _bacc.Bacc("TRN2", target_bir_lowering=False, num_devices=1)
    arrays, args = {}, []
    for name in _INS:
        a = _np.ascontiguousarray(inputs[name])
        arrays[f"in_{name}"] = a
        args.append(nc.dram_tensor(f"in_{name}", a.shape, _mybir.dt.from_np(a.dtype), kind="ExternalInput").ap())
    args.append(nc.dram_tensor("out_0", (N_NODES, D), _mybir.dt.float32, kind="ExternalOutput").ap())
    gnn_moe(nc, *args)
    r = _run(nc, [arrays], core_ids=[0])
    return r.results[0]["out_0"]
```

```python
import concourse.bass as bass
from concourse import mybir
from concourse.alu_op_type import AluOpType as ALU
from contextlib import ExitStack

P = 128
N_NODES = 6250
D = 256
N_EDGES = 106250
N_EXP = 8
EPS = 1e-5
BLOCKS = -(-N_NODES // P)
LAST_ROWS = N_NODES - (BLOCKS - 1) * P
EDGE_COLS = N_EDGES // P
EDGE_REST = N_EDGES - EDGE_COLS * P
IN_UNROLL = 4
IN_COLS = -(-(EDGE_COLS + 1) // IN_UNROLL) * IN_UNROLL
POOL_COLS = 352
GROUP = 8
MAX_CHUNKS = -(-N_EDGES // P) + BLOCKS - 1
NORM_STEPS = 3
NORM_AT = 5
PLACE_UNROLL = 4
TURN = 2 * GROUP
CHUNKS = -(-MAX_CHUNKS // TURN) * TURN
HALF = CHUNKS // 2
NOWHERE = 1 << 18
COL_BIAS = 0x3000
BLK_COLS = -(-(CHUNKS + GROUP) // P) * P
TBLK = 7
TGRP = BLOCKS // TBLK
TOP_K = 2
PICKS = TOP_K * BLOCKS
EXP_TURN = 4
EXP_CHUNKS = -(-(PICKS + N_EXP - 1) // EXP_TURN) * EXP_TURN
ACC_BUFS = 4
assert BLOCKS < CHUNKS // TURN
assert BLOCKS % TBLK == 0 and HALF <= 512 and EXP_CHUNKS <= P - EXP_TURN


def gnn_moe(nc, x, src, dst, w_root, w_neigh, gnn_b, router_w, w1, b1, w2, b2, out):
    f32, i32, u8 = mybir.dt.float32, mybir.dt.int32, mybir.dt.uint8
    bf16, f16, u32 = mybir.dt.bfloat16, mybir.dt.float16, mybir.dt.uint32
    ACT, AX = mybir.ActivationFunctionType, mybir.AxisListType
    ds = bass.ds

    ctx = ExitStack()
    with ctx:
        def sb(name, shape, dt):
            return ctx.enter_context(nc.sbuf_tensor(name, shape, dt))

        def pb(name, shape, dt):
            return ctx.enter_context(nc.psum_tensor(name, shape, dt))

        def sem(name):
            return ctx.enter_context(nc.semaphore(name))

        xw_dram = nc.dram_tensor("xw_rows", (BLOCKS * P, D), f32).ap()
        h_dram = nc.dram_tensor("h_rows", (BLOCKS * P, D), f32).ap()
        pair_dram = nc.dram_tensor("sorted_pairs", (P * CHUNKS, 2), f32).ap()
        x2_dram = nc.dram_tensor("x2_rows", (BLOCKS * P, D), f32).ap()
        y_dram = nc.dram_tensor("pick_rows", ((PICKS + EXP_CHUNKS) * P, D), f32).ap()
        ct_dram = nc.dram_tensor("chunk_expert", (P,), i32).ap()
        blk_dram = nc.dram_tensor("chunk_block", (BLK_COLS,), i32).ap()

        rows = sb("rows", [P, BLOCKS, 2 * D + 1], f32)
        big = sb("big", [P, BLOCKS * IN_COLS // 4], f32)
        masks = big[:, :].bitcast(u8).rearrange("p (b c) -> p b c", b=BLOCKS)
        wsize = N_EXP * 2 * D
        w1_sb = big[:, 0:wsize].rearrange("p (e k f) -> p e k f", e=N_EXP, k=2)
        w2_sb = big[:, wsize:2 * wsize].rearrange("p (e k f) -> p e k f", e=N_EXP, k=2)
        wrn_sb = sb("wrn_sb", [P, 2, 2 * D], f32)
        rw_sb = sb("rw_sb", [P, 2, N_EXP], f32)

        iota_h = sb("iota_h", [P, CHUNKS], f16)
        iota1_f = sb("iota1_f", [P, P], f32)
        iota8_f = sb("iota8_f", [P, N_EXP], f32)
        kpos_i = sb("kpos_i", [P, BLK_COLS // P], i32)
        kpos_f = sb("kpos_f", [P, BLK_COLS // P], f32)
        ident = sb("ident", [P, P], f32)
        upper = sb("upper", [P, P], f32)
        ones = sb("ones", [P, P], f32)
        zero_bf = sb("zero_bf", [P, HALF], bf16)
        eps_t = sb("eps_t", [P, 1], f32)
        zero_col = sb("zero_col", [P, TBLK], f32)

        ring = sb("ring", [P, TURN, 2 * D], f32)
        rflat = ring[:, :, :].rearrange("p a b -> p (a b)")
        o = 0
        dst_i = rflat[:, o:o + IN_COLS].bitcast(i32); o += IN_COLS
        hi_f = rflat[:, o:o + IN_COLS]; o += IN_COLS
        lo_f = rflat[:, o:o + IN_COLS]; o += IN_COLS
        payload = rflat[:, o:o + 2 * IN_COLS].rearrange("p (w c) -> p w c", w=2)
        rowlo_f = rflat[:, o:o + IN_COLS]; o += IN_COLS
        colbits = rflat[:, o:o + IN_COLS]; o += IN_COLS
        pos_f = rflat[:, o:o + IN_COLS]; o += IN_COLS
        tmp_i = rflat[:, o:o + IN_COLS].bitcast(i32); o += IN_COLS
        pair_f = rflat[:, o:o + 2 * POOL_COLS].rearrange("p (c w) -> p c w", w=2)
        src_i = rflat[:, o:o + IN_COLS].bitcast(i32); o += IN_COLS
        blk_f = rflat[:, o:o + IN_COLS]; o += IN_COLS
        place_i = tmp_i
        assert o <= TURN * 2 * D
        onehot = sb("onehot", [P, 2, GROUP, P], f32)
        oflat = onehot[:, :, :, :].rearrange("p a b c -> p (a b c)").bitcast(bf16)
        hflat = sb("hi_room", [P, TBLK * D], f32)
        hi_oh = hflat[:, 0:IN_UNROLL * CHUNKS // 2].bitcast(bf16).rearrange("p (a c) -> p a c", a=IN_UNROLL)
        lo_pay = oflat[:, 0:2 * IN_UNROLL * P].rearrange("p (a w b) -> p a w b", a=IN_UNROLL, w=2)

        idx_i = sb("idx_i", [P, CHUNKS], i32)
        erow = sb("erow", [P, CHUNKS + TURN], f32)
        blk_row = big[0:1, 2 * wsize:2 * wsize + BLK_COLS].bitcast(i32)
        stage = sb("stage", [P, 2, GROUP], i32)
        pair_stage = sb("pair_stage", [P, 2, GROUP, 2], f32)
        merged = big[:, 0:2 * CHUNKS].rearrange("p (c w) -> p c w", w=2)

        iota_i = idx_i
        qb = BLK_COLS // P * BLOCKS
        cmp_f = hflat[:, D:D + qb].rearrange("p (q b) -> p q b", b=BLOCKS)
        picked = onehot[:, :, :, :].rearrange("p a b c -> p (a b c)")[:, 0:2 * IN_COLS].rearrange("p (a c) -> p a c", a=2)
        at = D + qb
        xn = hflat[:, at:at + 2 * D].rearrange("p (a d) -> p a d", a=2)
        xnT = hflat[:, at + 2 * D:at + 4 * D].rearrange("p (a d) -> p a d", a=2)
        assert at + 4 * D <= IN_UNROLL * CHUNKS // 2
        gb_sb = hflat[:, 0:D]
        counts = sb("counts", [P, BLOCKS], f32)
        tot_i = sb("tot_i", [P, BLOCKS], i32)
        nch_f = sb("nch_f", [P, BLOCKS], f32)
        start_f = sb("start_f", [P, BLOCKS + 1], f32)
        off_f = sb("off_f", [P, BLOCKS], f32)
        blk_cf = sb("blk_cf", [P, BLK_COLS // P], f32)
        blk_ci = sb("blk_ci", [P, BLK_COLS // P], i32)

        G7 = TBLK * D
        xg0, xg1, hg, x2g = [rflat[:, n * G7:(n + 1) * G7].rearrange("p (j d) -> p j d", j=TBLK) for n in range(4)]
        xg = (xg0, xg1)
        hg_first = hflat[:, :].rearrange("p (j d) -> p j d", j=TBLK)
        oh_flat = onehot[:, :, :, :].rearrange("p a b c -> p (a b c)")
        xT_flat = oh_flat[:, 0:G7]
        xT = xT_flat.rearrange("p (k t) -> p k t", k=2)
        spare = [2 * wsize + BLK_COLS]

        def small(*shape):
            n = 1
            for a in shape:
                n *= a
            flat = big[:, spare[0]:spare[0] + n]
            spare[0] += n
            assert spare[0] <= BLOCKS * IN_COLS // 4
            if len(shape) == 3:
                return flat.rearrange("p (a b c) -> p a b c", a=shape[0], b=shape[1])
            return flat.rearrange("p (a b) -> p a b", a=shape[0]) if len(shape) == 2 else flat

        bn6 = small(TBLK, 6)
        mv = sb("mv", [P, TBLK, 2], f32)
        t7 = sb("t7", [P, 6, TBLK], f32)
        lg = small(2, TBLK, N_EXP)
        top8 = small(TBLK, 8)
        idx8 = small(TBLK, 8).bitcast(u32)
        share = sb("share", [P, TOP_K, BLOCKS], f32)
        expert_f = sb("expert_f", [P, TOP_K, BLOCKS], f32)
        pmask = oh_flat[:, 0:N_EXP * PICKS].rearrange("p (e c) -> p e c", e=N_EXP)
        pscan = hflat[:, 0:N_EXP * PICKS].rearrange("p (e c) -> p e c", e=N_EXP)
        c8 = small(4, N_EXP + 1)
        c8_i = small(N_EXP).bitcast(i32)
        pick_pos = small(3, PICKS)
        pick_row = idx_i[:, 0:PICKS]
        pick_tmp = idx_i[:, PICKS:2 * PICKS]
        at = 3 * PICKS
        pick_bits = idx_i[:, 2 * PICKS:at]
        tok_sorted = idx_i[:, at:at + EXP_CHUNKS]
        pad_place = idx_i[:, at + EXP_CHUNKS:at + 2 * EXP_CHUNKS].bitcast(f32)
        place_sorted = idx_i[:, at + 2 * EXP_CHUNKS:at + 3 * EXP_CHUNKS]
        assert 2 * EXP_CHUNKS <= 3 * PICKS
        pk_small = pick_pos.rearrange("p a c -> p (a c)")
        id_f, id_t = pk_small[:, 0:EXP_CHUNKS], pk_small[:, EXP_CHUNKS:2 * EXP_CHUNKS]
        ct_f = sb("ct_f", [P, 1], f32)
        ct_i = sb("ct_i", [P, 1], i32)
        exp_row = erow[0:1, 0:EXP_TURN + P].bitcast(i32)
        slots = TOP_K * TBLK
        pk_flat = rflat[:, 2 * G7:3 * G7].bitcast(bf16)
        pk_hi = pk_flat[:, 0:slots * EXP_CHUNKS].rearrange("p (a c) -> p a c", a=slots)
        pk_lo = pk_flat[:, slots * EXP_CHUNKS:slots * (EXP_CHUNKS + P)].rearrange("p (a c) -> p a c", a=slots)
        xc = rflat[:, 0:4 * D].rearrange("p (a d) -> p a d", a=4)
        xcT = rflat[:, 4 * D:6 * D].rearrange("p (a d) -> p a d", a=2)
        hidT = rflat[:, 6 * D:8 * D].rearrange("p (a d) -> p a d", a=2)
        w1_cur = rflat[:, 8 * D:12 * D].rearrange("p (a d) -> p a d", a=2)
        b1_all = small(N_EXP, 2)
        b1_cur = small(2, 2)
        yc = rflat[:, 12 * D:16 * D].rearrange("p (a d) -> p a d", a=4)
        yg = [rflat[:, n * 2 * G7:(n + 1) * 2 * G7].rearrange("p (r j d) -> p r j d", r=TOP_K, j=TBLK) for n in range(2)]

        sums = sb("sums", [P, BLOCKS], f32)
        nmean = sb("nmean", [P, BLOCKS], f32)
        ssq = sb("ssq", [P, BLOCKS], f32)
        std = sb("std", [P, BLOCKS], f32)
        rstd = sb("rstd", [P, BLOCKS], f32)
        nmr = sb("nmr", [P, BLOCKS], f32)
        deg = sb("deg", [P, BLOCKS], f32)
        neg_half = counts
        rden = sb("rden", [P, BLOCKS], f32)

        ps = pb("ps", [P, 8 * 512], f32)
        bank = [ps[:, 512 * i:512 * (i + 1)] for i in range(8)]

        pairs_zero, pairs_ready, pairs_staged = sem("pairs_zero"), sem("pairs_ready"), sem("pairs_staged")
        pairs_loaded = sem("pairs_loaded")
        scattered = [sem(f"scattered{i}") for i in range(2)]
        tail_turn = sem("tail_turn")
        placed, pos_ready = sem("placed"), sem("pos_ready")
        pad_set = sem("pad_set")
        s_edges = sem("s_edges")
        s_x = [sem(f"s_x{g}") for g in range(TGRP)]
        pool_step, consts = sem("pool_step"), sem("consts")
        dve_step = sem("dve_step")
        sums_done, ssq_done, std_done = sem("sums_done"), sem("ssq_done"), sem("std_done")
        rstd_ready, xn_done, xw_stored = sem("rstd_ready"), sem("xn_done"), sem("xw_stored")
        act_step = sem("act_step")
        mask_done, scan_done, pick_done = sem("mask_done"), sem("scan_done"), sem("pick_done")
        counts_ready, totals_done = sem("counts_ready"), sem("totals_done")
        oh_ready, sorted_cols = sem("oh_ready"), sem("sorted_cols")
        blk_ready, blk_stored, blk_loaded = sem("blk_ready"), sem("blk_stored"), sem("blk_loaded")
        sort_ready = sem("sort_ready")
        rows_zero, oh_made, mult_done, added = sem("rows_zero"), sem("oh_made"), sem("mult_done"), sem("added")
        gathered = [sem(f"gathered{i}") for i in range(TURN)]
        staged, squared, pool_turn = sem("staged"), sem("squared"), sem("pool_turn")
        tr_done, tr_copied, xw_done, xw_made = sem("tr_done"), sem("tr_copied"), sem("xw_done"), sem("xw_made")
        h_sum, h_made, w_gnn = sem("h_sum"), sem("h_made"), sem("w_gnn")
        gb_loaded, biased = sem("gb_loaded"), sem("biased")
        h_stored = [sem(f"h_stored{i}") for i in range(TGRP)]
        rows_clear = sem("rows_clear")
        w_ffn = sem("w_ffn")
        h_loaded, h_first_loaded, out_stored = sem("h_loaded"), sem("h_first_loaded"), sem("out_stored")
        x_loaded = [sem(f"x_loaded{n}") for n in range(2)]
        h_free, x_free, grp_done = sem("h_free"), sem("x_free"), sem("grp_done")
        s1_ready, u_ready, th_ready = sem("s1_ready"), sem("u_ready"), sem("th_ready")
        norm_step, scale_step, coef_ready = sem("norm_step"), sem("scale_step"), sem("coef_ready")
        var_ready, sd_ready, x2_ready, x2_stored = sem("var_ready"), sem("sd_ready"), sem("x2_ready"), sem("x2_stored")
        xt_done, xt_copied, lg_done = sem("xt_done"), sem("xt_copied"), sem("lg_done")
        peak_step, share_step = sem("peak_step"), sem("share_step")
        lsub_ready, ex_ready = sem("lsub_ready"), sem("ex_ready")
        bias_loaded, pcounts_ready, ptotals_done = sem("bias_loaded"), sem("pcounts_ready"), sem("ptotals_done")
        ct_ready, ct_stored, ct_loaded = sem("ct_ready"), sem("ct_stored"), sem("ct_loaded")
        pk_ready, pk_done, picks_ready = sem("pk_ready"), sem("pk_done"), sem("picks_ready")
        pk_order, places_ready = sem("pk_order"), sem("places_ready")
        xstaged, ystaged = sem("xstaged"), sem("ystaged")
        xc_in = [sem(f"xc_in{i}") for i in range(EXP_TURN)]
        y_stored = [sem(f"y_stored{i}") for i in range(EXP_TURN)]
        yg_in = [[sem(f"yg_in{n}_{r}") for r in range(TOP_K)] for n in range(2)]
        t1_done, xcT_ready, w1_ready, l1_done = sem("t1_done"), sem("xcT_ready"), sem("w1_ready"), sem("l1_done")
        gelu_done = sem("gelu_done")
        l2_done, y_ready, combined = sem("l2_done"), sem("y_ready"), sem("combined")

        block = ctx.enter_context(nc.Block())

        def blocked(ap):
            return ap.rearrange("(t p) d -> p t d", p=P)

        @block.sync
        def _(sp):
            full = EDGE_COLS * P
            for t, a in ((src_i, src), (dst_i, dst)):
                sp.dma_start(t[:, 0:EDGE_COLS], a[0:full].rearrange("(p n) -> p n", p=P)).then_inc(s_edges, 16)
            sp.wait_ge(pad_set, 4)
            zeros = zero_bf[:, :].bitcast(f32)
            sp.dma_start(pair_dram.rearrange("(p a c) w -> p a (c w)", p=P, a=8),
                         zeros.unsqueeze(1).to_broadcast([P, 8, HALF // 2])).then_inc(pairs_zero, 16)
            for t, a in ((src_i, src), (dst_i, dst)):
                with nc.allow_non_contiguous_dma(reason="ten single edges"):
                    sp.dma_start(t[0:EDGE_REST, EDGE_COLS:EDGE_COLS + 1],
                                 a[full:N_EDGES].rearrange("(p n) -> p n", n=1)).then_inc(s_edges, 16)
            for g in range(TGRP):
                last = min((g + 1) * TBLK, BLOCKS - 1)
                sp.dma_start(rows[:, g * TBLK:last, 0:D], blocked(x[g * TBLK * P:last * P, :])).then_inc(s_x[g], 16)
            sp.dma_start(rows[0:LAST_ROWS, BLOCKS - 1, 0:D], x[(BLOCKS - 1) * P:N_NODES, :]).then_inc(s_x[TGRP - 1], 16)
            for k in range(2):
                sp.dma_start(wrn_sb[:, k, 0:D], w_root[k * P:(k + 1) * P, :]).then_inc(w_gnn, 16)
                sp.dma_start(wrn_sb[:, k, D:2 * D], w_neigh[k * P:(k + 1) * P, :]).then_inc(w_gnn, 16)
            sp.wait_ge(blk_ready, 1)
            with nc.allow_non_contiguous_dma(reason="small table"):
                sp.dma_start(blk_dram.rearrange("(q p) -> p q", p=P), blk_ci[:, :]).then_inc(blk_stored, 16)
            sp.wait_ge(blk_stored, 16)
            sp.wait_ge(pick_done, BLOCKS)
            sp.dma_start(blk_row[:, :], blk_dram.rearrange("(a n) -> a n", a=1)).then_inc(blk_loaded, 16)
            sp.wait_ge(xw_made, BLOCKS)
            sp.dma_start(blocked(xw_dram), rows[:, :, D:2 * D]).then_inc(xw_stored, 16)
            sp.wait_ge(blk_loaded, 16)
            for h in range(2):
                sp.wait_ge(scattered[h], 16 * POOL_COLS // 2)
            sp.dma_start(big[:, 0:2 * CHUNKS], pair_dram.rearrange("(p c) w -> p (c w)", p=P)).then_inc(pairs_loaded, 16)
            sp.wait_ge(sort_ready, 2)
            sp.dma_start(gb_sb, gnn_b.partition_broadcast(P)).then_inc(gb_loaded, 16)
            for k in range(2):
                sp.dma_start(w1_sb[:, :, k, :], w1[:, k * P:(k + 1) * P, :].rearrange("e p f -> p e f")).then_inc(w_ffn, 16)
                sp.dma_start(w2_sb[:, :, k, :], w2[:, k * P:(k + 1) * P, :].rearrange("e p f -> p e f")).then_inc(w_ffn, 16)
            with nc.allow_non_contiguous_dma(reason="small transposed weights"):
                for k in range(2):
                    sp.dma_start(rw_sb[:, k, :], router_w[:, k * P:(k + 1) * P].rearrange("e p -> p e")).then_inc(w_ffn, 16)
                    sp.dma_start(b1_all[:, :, k], b1[:, k * P:(k + 1) * P].rearrange("e p -> p e")).then_inc(w_ffn, 16)
            for g in range(TGRP):
                sp.wait_ge(h_made, g + 1)
                sp.dma_start(blocked(h_dram[g * TBLK * P:(g + 1) * TBLK * P, :]),
                             rows[:, g * TBLK:(g + 1) * TBLK, 0:D]).then_inc(h_stored[g], 16)

            def load_h(g):
                sp.dma_start(hg_first if g == 0 else hg, blocked(h_dram[ds(g * TBLK * P, TBLK * P), :]))\
                    .then_inc(h_first_loaded if g == 0 else h_loaded, 16)

            def load_x(g, par):
                first = g * TBLK * P
                whole = (TBLK - 1) * P
                tail_rows = LAST_ROWS if g == TGRP - 1 else P
                sp.dma_start(xg[par][:, 0:TBLK - 1, :], blocked(x[ds(first, whole), :])).then_inc(x_loaded[par], 16)
                sp.dma_start(xg[par][0:tail_rows, TBLK - 1, :], x[ds(first + whole, tail_rows), :]).then_inc(x_loaded[par], 16)

            def store(g):
                first = g * TBLK * P
                whole = (TBLK - 1) * P
                tail_rows = LAST_ROWS if g is TGRP - 1 else P
                sp.dma_start(blocked(out[ds(first, whole), :]),
                             rows[:, ds(g * TBLK, TBLK - 1), 0:D]).then_inc(out_stored, 16)
                sp.dma_start(out[ds(first + whole, tail_rows), :],
                             rows[0:tail_rows, ds(g * TBLK + TBLK - 1, 1), 0:D].rearrange("p a d -> p (a d)"))\
                    .then_inc(out_stored, 16)

            def next_h(g):
                sp.wait_ge(h_free, g + 1)
                load_h(g + 1)

            def group_io(g):
                if g + 2 < TGRP:
                    next_h(g + 1)
                sp.wait_ge(x2_ready, TBLK * (g + 1))
                sp.dma_start(blocked(x2_dram[ds(g * TBLK * P, TBLK * P), :]), x2g).then_inc(x2_stored, 16)

            def x_io(g, par):
                sp.wait_ge(x_free, g + 1)
                load_x(g + 2, par)

            for g in range(TGRP):
                sp.wait_ge(h_stored[g], 16)
            load_h(0)
            sp.wait_ge(added, 2 * CHUNKS)
            load_h(1)
            load_x(0, 0)
            load_x(1, 1)
            for g in range(TGRP):
                group_io(g)
                if g + 2 < TGRP:
                    x_io(g, g % 2)
            sp.wait_ge(u_ready, TGRP)
            for e in range(N_EXP):
                sp.dma_start(rows[:, e, D:2 * D], b2[e, :].partition_broadcast(P)).then_inc(bias_loaded, 16)
            sp.wait_ge(ct_ready, 1)
            with nc.allow_non_contiguous_dma(reason="small table"):
                sp.dma_start(ct_dram.rearrange("(p n) -> p n", n=1), ct_i[:, :]).then_inc(ct_stored, 16)
            sp.wait_ge(ct_stored, 16)
            sp.dma_start(exp_row[:, EXP_TURN:EXP_TURN + P], ct_dram.rearrange("(a n) -> a n", a=1)).then_inc(ct_loaded, 16)

            def load_y(g, r):
                first = (r * BLOCKS + g * TBLK) * P
                sp.dma_start(yg[g % 2][:, r, :, :], blocked(y_dram[first:first + TBLK * P, :])).then_inc(yg_in[g % 2][r], 16)

            for u in range(EXP_TURN):
                sp.wait_ge(y_stored[u], 16 * (EXP_CHUNKS // EXP_TURN))
            for g in range(2):
                for r in range(TOP_K):
                    load_y(g, r)
            for g in range(TGRP):
                if g + 2 < TGRP:
                    for r in range(TOP_K):
                        sp.wait_ge(combined, TBLK * (TOP_K * g + r + 1))
                        load_y(g + 2, r)
                sp.wait_ge(grp_done, g + 1)
                store(g)
            sp.wait_ge(out_stored, 32 * TGRP)

        @block.gpsimd
        def _(pool):
            n = [0]

            def step(ins):
                n[0] += 1
                ins.then_inc(pool_step, 1)
                pool.wait_ge(pool_step, n[0])

            step(pool.memset(ones[:, :], 1.0))
            pool.memset(rows[:, BLOCKS - 1, 0:D], 0.0).then_inc(pad_set, 1)
            step(pool.iota(iota_i[:, :], [[1, CHUNKS]], base=0, channel_multiplier=0))
            step(pool.iota(kpos_i[:, :], [[P, BLK_COLS // P]], base=0, channel_multiplier=1))
            step(pool.memset(eps_t[:, :], EPS))
            step(pool.memset(zero_col[:, :], 0.0))
            step(pool.affine_select(out=upper[:, :], in_=ones[:, :], compare_op=ALU.is_gt, fill=0.0, base=0,
                                    pattern=[[1, P]], channel_multiplier=-1))
            pool.affine_select(out=ident[:, :], in_=ones[:, :], compare_op=ALU.is_equal, fill=0.0, base=0,
                               pattern=[[1, P]], channel_multiplier=-1).then_inc(consts, 1)
            pool.wait_ge(pos_ready, 1)

            def add_places(b, par, first=False):
                if not first:
                    pool.wait_ge(pick_done, b)
                pool.wait_ge(placed, b + 1)
                pool.tensor_tensor(pos_f, pos_f, picked[:, par, :], ALU.add).then_inc(pick_done, 1)

            add_places(0, 0, True)
            with pool.Fori(0, BLOCKS // 4) as i:
                for u in range(4):
                    add_places(4 * i + 1 + u, (1 + u) % 2)

            pool.wait_ge(pairs_zero, 16)

            def scatter(i):
                for h in range(2):
                    pool.wait_ge(pairs_staged, 2 * i + h + 1)
                    pool.sem_inc(pool_turn, 1)
                    for c in range(GROUP):
                        pool.indirect_dma_start(pair_dram, bass.IndirectOffsetOnAxis(ap=stage[:, h, c:c + 1], axis=0),
                                                pair_stage[:, h, c, :], None).then_inc(scattered[h], 16)

            with pool.Fori(0, POOL_COLS // (2 * GROUP)) as i:
                scatter(i)

            def gather_turn(table, base, i, first):
                for h in range(2):
                    for_half = base + TURN * i + GROUP * h
                    pool.wait_ge(staged, 2 * (base // TURN) + 2 * i + h + 1)
                    if not first:
                        pool.wait_ge(mult_done, for_half - TURN + GROUP)
                    pool.sem_inc(pool_turn, 1)
                    for c in range(GROUP):
                        slot = GROUP * h + c
                        pool.indirect_dma_start(ring[:, slot, 0:D], None, table,
                                                bass.IndirectOffsetOnAxis(ap=stage[:, h, c:c + 1], axis=0))\
                            .then_inc(gathered[slot], 16)

            def gather_pass(table, base):
                gather_turn(table, base, 0, True)
                with pool.Fori(1, CHUNKS // TURN) as i:
                    gather_turn(table, base, i, False)

            gather_pass(xw_dram, 0)
            for g in range(TGRP):
                pool.wait_ge(h_sum, TBLK * (g + 1))
                pool.memset(rows[:, g * TBLK:(g + 1) * TBLK, D:2 * D], 0.0).then_inc(rows_clear, 1)
            for g in range(TGRP):
                pool.wait_ge(h_stored[g], 16)
            gather_pass(h_dram, CHUNKS)

            def group_rows(g):
                return rows[:, ds(g * TBLK, TBLK), 0:D]

            def products_of(g):
                pool.wait_ge(s1_ready, TBLK * (g + 1))
                pool.sem_inc(pool_turn, 1)
                pool.tensor_tensor(group_rows(g), group_rows(g), hg_first if isinstance(g, int) and g == 0 else hg, ALU.mult).then_inc(h_free, 1)

            def start_of(g, par):
                pool.wait_ge(x2_ready, TBLK * (g + 1))
                pool.sem_inc(pool_turn, 1)
                pool.tensor_tensor(group_rows(g), xg[par], x2g, ALU.add).then_inc(x_free, 1)

            products_of(0)
            products_of(1)
            products_of(2)
            start_of(0, 0)
            with pool.Fori(0, (TGRP - 3) // 2) as i:
                for u in (1, 2):
                    products_of(2 * i + u + 2)
                    start_of(2 * i + u, u % 2)
            start_of(TGRP - 2, (TGRP - 2) % 2)
            start_of(TGRP - 1, (TGRP - 1) % 2)

            def gather(table, slot, index, arrived):
                pool.indirect_dma_start(slot, None, table, bass.IndirectOffsetOnAxis(ap=index, axis=0)).then_inc(arrived, 16)

            def gather_tokens(i, h):
                pool.wait_ge(xstaged, 2 * i + h + 1)
                if not (isinstance(i, int) and i == 0):
                    pool.wait_ge(t1_done, EXP_TURN * (i - 1) + 2 * h + 2)
                pool.sem_inc(pool_turn, 1)
                for c in range(2):
                    gather(x2_dram, xc[:, 2 * h + c, :], stage[:, h, c:c + 1], xc_in[2 * h + c])

            def scatter_results(i, h):
                pool.wait_ge(ystaged, 2 * i + h + 1)
                for c in range(2):
                    slot = 2 * h + c
                    pool.wait_ge(y_ready, EXP_TURN * i + slot + 1)
                    pool.sem_inc(pool_turn, 1)
                    pool.indirect_dma_start(y_dram, bass.IndirectOffsetOnAxis(ap=stage[:, h, 4 + c:5 + c], axis=0),
                                            yc[:, slot, :], None).then_inc(y_stored[slot], 16)

            pool.wait_ge(x2_stored, 16 * TGRP)
            pool.wait_ge(x_free, TGRP)
            turns = EXP_CHUNKS // EXP_TURN
            for i in range(2):
                for h in range(2):
                    gather_tokens(i, h)
            with pool.Fori(2, turns) as i:
                for h in range(2):
                    scatter_results(i - 2, h)
                    gather_tokens(i, h)
            for i in (turns - 2, turns - 1):
                for h in range(2):
                    scatter_results(i, h)

        @block.scalar
        def _(act):
            def total(t):
                row = rows[:, ds(t, 1), 0:D].rearrange("p a d -> p (a d)")
                act.activation(row, row, ACT.Identity, accum_out=sums[:, ds(t, 1)]).then_inc(sums_done, 1)

            act.wait_ge(s_x[0], 16)
            total(0)
            for g in range(TGRP):
                act.wait_ge(s_x[g], 32 if g == TGRP - 1 else 16)
                for t in range(max(g * TBLK, 1), (g + 1) * TBLK):
                    total(t)
            act.wait_ge(sums_done, BLOCKS)
            act.mul(nmean[:, :], sums[:, :], -1.0 / D).then_inc(act_step, 1)
            act.wait_ge(act_step, 1)
            with act.Fori(0, TGRP) as g:
                for j in range(TBLK):
                    t = g * TBLK + j
                    act.activation(rows[:, ds(t, 1), D:2 * D].rearrange("p a d -> p (a d)"),
                                   rows[:, ds(t, 1), 0:D].rearrange("p a d -> p (a d)"), ACT.Square,
                                   bias=nmean[:, ds(t, 1)], accum_out=ssq[:, ds(t, 1)]).then_inc(ssq_done, 1)
            act.wait_ge(ssq_done, BLOCKS)
            act.wait_ge(consts, 1)
            act.activation(std[:, :], ssq[:, :], ACT.Sqrt, bias=eps_t[:, :], scale=1.0 / D).then_inc(std_done, 1)
            act.wait_ge(rstd_ready, 1)

            def normed(t, par, early=False):
                if not early:
                    act.wait_ge(tr_done, t - 1)
                act.activation(xn[:, par, :], rows[:, ds(t, 1), 0:D].rearrange("p a d -> p (a d)"), ACT.Identity,
                               bias=nmr[:, ds(t, 1)], scale=rstd[:, ds(t, 1)]).then_inc(xn_done, 1)

            def copy_tr(t, par, early=False):
                act.wait_ge(tr_done, t + 1)
                if not early:
                    act.wait_ge(xw_done, t - 1)
                act.copy(xnT[:, par, :], bank[6 + par][:, 0:D]).then_inc(tr_copied, 1)

            def products(t, par):
                act.wait_ge(xw_done, t + 1)
                act.copy(rows[:, ds(t, 1), 0:2 * D].rearrange("p a d -> p (a d)"), bank[par]).then_inc(xw_made, 1)

            normed(0, 0, True)
            normed(1, 1, True)
            copy_tr(0, 0, True)
            normed(2, 0)
            copy_tr(1, 1, True)
            products(0, 0)
            with act.Fori(1, BLOCKS // 2) as i:
                normed(2 * i + 1, 1)
                copy_tr(2 * i, 0)
                products(2 * i - 1, 1)
                normed(2 * i + 2, 0)
                copy_tr(2 * i + 1, 1)
                products(2 * i, 0)
            copy_tr(BLOCKS - 1, 0)
            products(BLOCKS - 2, 1)
            products(BLOCKS - 1, 0)

            def put_pairs(i, h, first):
                if not first:
                    act.wait_ge(scattered[h], 16 * GROUP * i)
                at = 2 * GROUP * i + GROUP * h
                act.copy(pair_stage[:, h, :, :], pair_f[:, ds(at, GROUP), :])
                act.copy(stage[:, h, :], place_i[:, ds(at, GROUP)]).then_inc(pairs_staged, 1)

            act.wait_ge(pairs_ready, 1)
            put_pairs(0, 0, True)
            put_pairs(0, 1, True)
            put_pairs(1, 0, False)
            put_pairs(1, 1, False)
            act.wait_ge(xw_stored, 16)
            for g in range(TGRP):
                act.copy(rows[:, g * TBLK:(g + 1) * TBLK, D:2 * D + 1],
                         zero_col[:, :].unsqueeze(2).to_broadcast([P, TBLK, D + 1])).then_inc(rows_zero, 1)
            with act.Fori(2, POOL_COLS // (2 * GROUP)) as i:
                put_pairs(i, 0, False)
                put_pairs(i, 1, False)

            def put(i, h):
                act.copy(stage[:, h, :], idx_i[:, ds(TURN * i + GROUP * h, GROUP)]).then_inc(staged, 1)

            def stage_pass(base, squares):
                turns = base // TURN

                def half(i, h, last):
                    for c in range(GROUP):
                        slot = GROUP * h + c
                        act.wait_ge(gathered[slot], 16 * (turns + i + 1))
                        if squares:
                            act.activation(ring[:, slot, D:2 * D], ring[:, slot, 0:D], ACT.Square).then_inc(squared, 1)
                    if not last:
                        put(i + 1, h)

                put(0, 0)
                put(0, 1)
                with act.Fori(0, CHUNKS // TURN - 1) as i:
                    half(i, 0, False)
                    half(i, 1, False)
                half(CHUNKS // TURN - 1, 0, True)
                half(CHUNKS // TURN - 1, 1, True)

            act.wait_ge(sort_ready, 1)
            stage_pass(0, False)

            for g in range(TGRP):
                act.wait_ge(h_sum, TBLK * (g + 1))
                block_rows = rows[:, g * TBLK:(g + 1) * TBLK, 0:D]
                act.activation(block_rows, block_rows, ACT.Relu).then_inc(h_made, 1)
            stage_pass(CHUNKS, True)

            def tanhs(g):
                act.wait_ge(u_ready, g + 1)
                for j in range(TBLK):
                    t = g * TBLK + j
                    row = rows[:, ds(t, 1), 0:D].rearrange("p a d -> p (a d)")
                    act.activation(row, row, ACT.Tanh, scale=rden[:, ds(t, 1)]).then_inc(th_ready, 1)

            def norms(g, par, first=False):
                act.wait_ge(coef_ready, g + 1)
                if not first:
                    act.wait_ge(x2_stored, 16 * g)
                    act.wait_ge(x_free, g)
                    act.wait_ge(xt_done, 4 * g)
                for j in range(TBLK):
                    act.activation(x2g[:, j, :], xg[par][:, j, :], ACT.Identity, bias=t7[:, 3, j:j + 1],
                                   scale=t7[:, 2, j:j + 1]).then_inc(x2_ready, 1)

            def stds(g):
                act.wait_ge(var_ready, g + 1)
                act.activation(t7[:, 1, :], t7[:, 0, :], ACT.Sqrt).then_inc(sd_ready, 1)

            def copy_xt(g, first=False):
                if not first:
                    act.wait_ge(lg_done, g)
                for r in range(4):
                    n = 2 * TBLK * P - 512 * r if r == 3 else 512
                    act.wait_ge(xt_done, 4 * g + r + 1)
                    act.copy(xT_flat[:, 512 * r:512 * r + n], bank[4 + r % 2][:, 0:n]).then_inc(xt_copied, 1)

            def exps(g):
                act.wait_ge(lsub_ready, g + 1)
                act.activation(lg[:, 1, :, :], lg[:, 0, :, :], ACT.Exp).then_inc(ex_ready, 1)

            tanhs(0)
            stds(0)
            tanhs(1)
            norms(0, 0, True)
            copy_xt(0, True)
            with act.Fori(0, (TGRP - 3) // 2) as i:
                for u in (1, 2):
                    g = 2 * i + u
                    stds(g)
                    tanhs(g + 1)
                    exps(g - 1)
                    norms(g, u % 2)
                    copy_xt(g)
            stds(TGRP - 2)
            tanhs(TGRP - 1)
            exps(TGRP - 3)
            norms(TGRP - 2, (TGRP - 2) % 2)
            copy_xt(TGRP - 2)
            stds(TGRP - 1)
            norms(TGRP - 1, (TGRP - 1) % 2)
            exps(TGRP - 2)
            copy_xt(TGRP - 1)
            exps(TGRP - 1)

            def put_tokens(i, h):
                act.copy(stage[:, h, 0:2], tok_sorted[:, ds(EXP_TURN * i + 2 * h, 2)]).then_inc(xstaged, 1)

            def next_tokens(i, u):
                if u % 2 == 1:
                    for c in (u - 1, u):
                        act.wait_ge(xc_in[c], 16 * (i + 1))
                    put_tokens(i + 1, u // 2)

            def gelu_of(m, par, early=False):
                act.wait_ge(l1_done, m + 1)
                if not early:
                    act.wait_ge(l2_done, m - 1)
                for f in range(2):
                    act.activation(hidT[:, par, f * P:(f + 1) * P], bank[2 + par][:, f * P:(f + 1) * P], ACT.Gelu,
                                   bias=b1_cur[:, par, f:f + 1]).then_inc(gelu_done, 1)

            def put_places(i, h):
                if not (isinstance(i, int) and i == 0):
                    for c in (2 * h, 2 * h + 1):
                        act.wait_ge(y_stored[c], 16 * i)
                act.copy(stage[:, h, 4:6], place_sorted[:, ds(EXP_TURN * i + 2 * h, 2)]).then_inc(ystaged, 1)

            def expert_turn(i, first=False, last=False):
                for u in range(EXP_TURN):
                    if not first and u % 2 == 0:
                        put_places(i - 1, u // 2)
                    if not last:
                        next_tokens(i, u)
                    if not (first and u == 0):
                        gelu_of(EXP_TURN * i + u - 1, (u - 1) % 2, early=first and u < 3)

            act.wait_ge(picks_ready, 1)
            put_tokens(0, 0)
            put_tokens(0, 1)
            expert_turn(0, first=True)
            act.wait_ge(places_ready, 1)
            expert_turn(1)
            turns = EXP_CHUNKS // EXP_TURN
            with act.Fori(2, turns - 1) as i:
                expert_turn(i)
            expert_turn(turns - 1, last=True)
            gelu_of(EXP_CHUNKS - 1, (EXP_CHUNKS - 1) % 2)
            put_places(turns - 1, 0)
            put_places(turns - 1, 1)

        @block.vector
        def _(dve):
            n = [0]

            def step(ins):
                n[0] += 1
                ins.then_inc(dve_step, 1)
                dve.wait_ge(dve_step, n[0])

            v = nc.vector
            v.memset(src_i[:, EDGE_COLS:IN_COLS], BLOCKS * P).then_inc(pad_set, 1)
            v.memset(dst_i[:, EDGE_COLS:IN_COLS], 0).then_inc(pad_set, 1)
            step(v.memset(zero_bf[:, :], 0.0))
            v.sem_inc(pad_set, 1)
            dve.wait_ge(consts, 1)
            step(v.tensor_copy(iota_h[:, :], iota_i[:, :]))
            step(v.tensor_copy(kpos_f[:, :], kpos_i[:, :]))
            step(v.tensor_scalar(iota1_f[:, :], iota_i[:, 0:P], 1.0, None, ALU.add))
            step(v.tensor_copy(iota8_f[:, :], iota_i[:, 0:N_EXP]))
            dve.wait_ge(s_edges, 64)
            step(v.tensor_scalar(tmp_i, src_i, 7, None, ALU.arith_shift_right))
            step(v.tensor_scalar(blk_f, tmp_i, 1.0, None, ALU.add))
            step(v.tensor_scalar(tmp_i, src_i, P - 1, None, ALU.bitwise_and))
            step(v.tensor_scalar(rowlo_f, tmp_i, 1.0, None, ALU.add))
            step(v.tensor_scalar(tmp_i, dst_i, float(COL_BIAS), None, ALU.add))
            step(v.tensor_scalar(colbits.bitcast(i32), tmp_i, 16, None, ALU.logical_shift_left))
            step(v.tensor_scalar(pos_f, blk_f, float(BLOCKS), float(NOWHERE), ALU.is_gt, ALU.mult))
            v.sem_inc(pos_ready, 1)
            with dve.Fori(0, TGRP) as g:
                for j in range(TBLK):
                    b = g * TBLK + j
                    v.tensor_scalar(masks[:, ds(b, 1), :].rearrange("p a c -> p (a c)"), blk_f, iota1_f[:, ds(b, 1)],
                                    0.0, ALU.is_equal, ALU.add, accum_out=counts[:, ds(b, 1)]).then_inc(mask_done, 1)
            dve.wait_ge(mask_done, BLOCKS)
            step(v.tensor_copy(off_f[:, :], counts[:, :]))
            v.sem_inc(counts_ready, 1)
            dve.wait_ge(totals_done, 1)
            step(v.tensor_scalar(tot_i[:, :], bank[1][:, 0:BLOCKS], float(P - 1), None, ALU.add))
            step(v.tensor_scalar(tot_i[:, :], tot_i[:, :], 7, None, ALU.arith_shift_right))
            step(v.tensor_copy(nch_f[:, :], tot_i[:, :]))
            step(v.memset(start_f[:, 0:1], 0.0))
            step(v.tensor_tensor_scan(start_f[:, 1:BLOCKS + 1], nch_f[:, :], nch_f[:, :], 0.0, ALU.add, ALU.max))
            step(v.scalar_tensor_tensor(off_f[:, :], start_f[:, 0:BLOCKS], float(P), bank[0][:, 0:BLOCKS],
                                        ALU.mult, ALU.add))
            q = BLK_COLS // P
            step(v.tensor_tensor(cmp_f[:, :, :], kpos_f[:, :].unsqueeze(2).to_broadcast([P, q, BLOCKS]),
                                 start_f[:, 0:BLOCKS].unsqueeze(1).to_broadcast([P, q, BLOCKS]), ALU.is_ge))
            step(v.tensor_reduce(blk_cf[:, :], cmp_f[:, :, :], AX.X, ALU.add))
            v.tensor_scalar(blk_ci[:, :], blk_cf[:, :], -1.0, float(BLOCKS - 1), ALU.add, ALU.min).then_inc(blk_ready, 1)
            def places(b, par, first):
                m = masks[:, ds(b, 1), :].rearrange("p a c -> p (a c)")
                running = ps[:, 1024 * (1 + par):1024 * (1 + par) + IN_COLS]
                if not first:
                    dve.wait_ge(pick_done, b - 1)
                v.tensor_tensor_scan(running, m, m, off_f[:, ds(b, 1)], ALU.add, ALU.max).then_inc(scan_done, 1)
                dve.wait_ge(scan_done, b + 1)
                v.tensor_tensor(picked[:, par, :], running, m, ALU.mult).then_inc(placed, 1)

            for b in range(NORM_AT):
                places(b, b % 2, b < 2)
            dve.wait_ge(std_done, 1)
            step(v.reciprocal(rstd[:, :], std[:, :]))
            v.tensor_tensor(nmr[:, :], nmean[:, :], rstd[:, :], ALU.mult).then_inc(rstd_ready, 1)
            with dve.Fori(0, (BLOCKS - NORM_AT) // PLACE_UNROLL) as i:
                for u in range(PLACE_UNROLL):
                    places(PLACE_UNROLL * i + NORM_AT + u, (NORM_AT + u) % 2, False)
            dve.wait_ge(pick_done, BLOCKS)
            step(v.tensor_scalar(tmp_i, pos_f, -1.0, None, ALU.add))
            step(v.tensor_scalar(src_i, tmp_i, 7, None, ALU.arith_shift_right))
            step(v.tensor_copy(hi_f, src_i))
            step(v.tensor_scalar(src_i, tmp_i, P - 1, None, ALU.bitwise_and))
            step(v.tensor_copy(lo_f, src_i))
            step(v.scalar_tensor_tensor(place_i, lo_f, float(CHUNKS), hi_f, ALU.mult, ALU.add))
            step(v.tensor_copy(pair_f[:, :, 0], dst_i[:, 0:POOL_COLS]))
            step(v.tensor_copy(pair_f[:, :, 1], rowlo_f[:, 0:POOL_COLS]))
            v.sem_inc(pairs_ready, 1)
            def one_hots(i, first):
                for u in range(IN_UNROLL):
                    j = POOL_COLS + i * IN_UNROLL + u
                    if not first:
                        dve.wait_ge(sorted_cols, (i - 1) * IN_UNROLL + u + 1)
                    v.tensor_scalar(hi_oh[:, u, :], iota_h[:, :], hi_f[:, ds(j, 1)], None, ALU.is_equal)
                    v.scalar_tensor_tensor(lo_pay[:, u, :, :], iota_h[:, 0:P].unsqueeze(1).to_broadcast([P, 2, P]),
                                           lo_f[:, ds(j, 1)], payload[:, :, ds(j, 1)].to_broadcast([P, 2, P]),
                                           ALU.is_equal, ALU.mult).then_inc(oh_ready, 1)

            dve.wait_ge(xw_done, BLOCKS)
            one_hots(0, True)
            with dve.Fori(1, (IN_COLS - POOL_COLS) // IN_UNROLL) as i:
                one_hots(i, False)
            dve.wait_ge(sorted_cols, IN_COLS - POOL_COLS + 1)
            bits = rflat[:, 0:CHUNKS]
            for half in range(2):
                v.tensor_copy(erow[:, half * HALF:(half + 1) * HALF], bank[half][:, 0:HALF])
                v.tensor_copy(bits[:, half * HALF:(half + 1) * HALF], bank[2 + half][:, 0:HALF])
            step(v.memset(erow[:, CHUNKS:CHUNKS + TURN], 0.0))
            step(v.tensor_scalar(bits.bitcast(i32), bits.bitcast(i32), 16, None, ALU.logical_shift_right))
            step(v.tensor_scalar(idx_i[:, :], bits.bitcast(i32), float(-COL_BIAS), 0.0, ALU.add, ALU.max))
            dve.wait_ge(pairs_loaded, 16)
            v.tensor_tensor(idx_i[:, :], merged[:, :, 0], idx_i[:, :], ALU.add).then_inc(sort_ready, 1)
            v.tensor_tensor(erow[:, 0:CHUNKS], erow[:, 0:CHUNKS], merged[:, :, 1], ALU.add).then_inc(sort_ready, 1)

            def make_one_hot(k, slot):
                v.tensor_scalar(onehot[:, slot // GROUP, slot % GROUP, :], iota1_f[:, :], erow[:, ds(k, 1)], None,
                                ALU.is_equal).then_inc(oh_made, 1)

            def add_half(i, h, base, lo, width, first):
                k0 = TURN * i + GROUP * h
                _, blocks = nc.values_load_multi_w_load_instructions(
                    blk_row[0:1, ds(k0, GROUP)], engines=[mybir.EngineType.DVE], min_val=0, max_val=BLOCKS - 1,
                    skip_runtime_bounds_check_because="the table is clamped to 0..BLOCKS-1 when it is made")
                for c in range(GROUP):
                    k = base + k0 + c
                    row = rows[:, ds(blocks[c], 1), lo:lo + width].rearrange("p a d -> p (a d)")
                    if not (first and c == 0):
                        dve.wait_ge(added, k)
                    dve.wait_ge(mult_done, k + 1)
                    v.tensor_tensor(row, row, bank[(GROUP * h + c) % ACC_BUFS][:, 0:width], ALU.add).then_inc(added, 1)
                    make_one_hot(k0 + c + TURN, GROUP * h + c)

            def add_pass(base, lo, width):
                for k in range(TURN):
                    make_one_hot(k, k)

                def turn(i, first):
                    add_half(i, 0, base, lo, width, first)
                    add_half(i, 1, base, lo, width, False)

                turn(0, base == 0)
                first_of_loop = 1
                if base == 0:
                    dve.wait_ge(gb_loaded, 16)
                    first_of_loop = BLOCKS + 1
                    with dve.Fori(1, first_of_loop) as i:
                        turn(i, False)
                        own = rows[:, ds(i - 1, 1), 0:D].rearrange("p a d -> p (a d)")
                        v.tensor_tensor(own, own, gb_sb, ALU.add).then_inc(biased, 1)
                with dve.Fori(first_of_loop, CHUNKS // TURN) as i:
                    turn(i, False)

            dve.wait_ge(sort_ready, 2)
            step(v.memset(ring[:, :, D:D + 1], 1.0))
            dve.wait_ge(blk_loaded, 16)
            dve.wait_ge(rows_zero, TGRP)
            add_pass(0, D, D + 1)

            dve.wait_ge(added, CHUNKS)
            step(v.tensor_copy(deg[:, :], rows[:, :, 2 * D]))
            step(v.tensor_scalar(rden[:, :], deg[:, :], 1.0, None, ALU.max))
            step(v.reciprocal(rden[:, :], rden[:, :]))
            step(v.tensor_scalar(neg_half[:, :], deg[:, :], -0.5, None, ALU.mult))

            dve.wait_ge(biased, BLOCKS)
            with dve.Fori(0, TGRP) as g:
                for j in range(TBLK):
                    t = g * TBLK + j
                    own = rows[:, ds(t, 1), 0:D].rearrange("p a d -> p (a d)")
                    v.scalar_tensor_tensor(own, rows[:, ds(t, 1), D:2 * D].rearrange("p a d -> p (a d)"),
                                           rden[:, ds(t, 1)], own, ALU.mult, ALU.add).then_inc(h_sum, 1)
            for g in range(TGRP):
                dve.wait_ge(h_stored[g], 16)
                v.memset(rows[:, g * TBLK:(g + 1) * TBLK, 0:D], 0.0).then_inc(rows_clear, 1)
            dve.wait_ge(rows_clear, 2 * TGRP)
            add_pass(CHUNKS, 0, 2 * D)

            def chain(done, per):
                n = [0]

                def link(ins, g):
                    n[0] = n[0] % per + 1
                    ins.then_inc(done, 1)
                    dve.wait_ge(done, g * per + n[0])

                return link

            col7 = lambda r: t7[:, r, :]

            def half_diffs(g):
                first = isinstance(g, int) and g == 0
                h_rows = hg_first if first else hg
                if first:
                    dve.wait_ge(h_first_loaded, 16)
                else:
                    dve.wait_ge(h_loaded, 16 * g)
                for j in range(TBLK):
                    t = g * TBLK + j
                    row = rows[:, ds(t, 1), 0:D].rearrange("p a d -> p (a d)")
                    v.scalar_tensor_tensor(row, h_rows[:, j, :], neg_half[:, ds(t, 1)], row, ALU.mult, ALU.add)\
                        .then_inc(s1_ready, 1)

            def diffs(g):
                dve.wait_ge(h_free, g + 1)
                row = rows[:, ds(g * TBLK, TBLK), 0:D]
                v.scalar_tensor_tensor(row, row, -2.0, rows[:, ds(g * TBLK, TBLK), D:2 * D], ALU.mult, ALU.add)\
                    .then_inc(u_ready, 1)

            norm_link = chain(norm_step, NORM_STEPS)

            def norm(g, par, turn):
                dve.wait_ge(x_loaded[par], 32 * (turn + 1))
                dve.wait_ge(th_ready, TBLK * (g + 1))
                norm_link(v.tensor_tensor(xg[par], xg[par], rows[:, ds(g * TBLK, TBLK), 0:D], ALU.add), g)
                for j in range(TBLK):
                    last = v.bn_stats(bn6[:, j, :], xg[par][:, j, :])
                norm_link(last, g)
                v.sem_inc(tail_turn, 1)
                for j in range(TBLK):
                    last = v.bn_aggr(mv[:, j, :], bn6[:, j, :])
                norm_link(last, g)
                if not (isinstance(g, int) and g == 0):
                    dve.wait_ge(sd_ready, g)
                v.tensor_scalar(col7(0), mv[:, :, 1], EPS, None, ALU.add).then_inc(var_ready, 1)

            scale_link = chain(scale_step, 5)

            def scale(g, first=False):
                dve.wait_ge(sd_ready, g + 1)
                if not first:
                    dve.wait_ge(x2_ready, TBLK * g)
                scale_link(v.reciprocal(col7(2), col7(1)), g)
                scale_link(v.tensor_tensor(col7(3), col7(2), col7(2), ALU.mult), g)
                scale_link(v.tensor_tensor(col7(3), col7(3), col7(0), ALU.mult), g)
                scale_link(v.tensor_scalar(col7(3), col7(3), -0.5, 1.5, ALU.mult, ALU.add), g)
                scale_link(v.tensor_tensor(col7(2), col7(2), col7(3), ALU.mult), g)
                v.scalar_tensor_tensor(col7(3), mv[:, :, 0], -1.0, col7(2), ALU.mult, ALU.mult).then_inc(coef_ready, 1)

            def wide(ap):
                return ap.unsqueeze(2).to_broadcast([P, TBLK, N_EXP])

            logits = bank[6][:, 0:TBLK * N_EXP].rearrange("p (j e) -> p j e", j=TBLK)
            peak_link = chain(peak_step, 1)

            def less_peak(g):
                dve.wait_ge(lg_done, g + 1)
                peak_link(v.tensor_reduce(col7(4), logits, AX.X, ALU.max), g)
                v.tensor_tensor(lg[:, 0, :, :], logits, wide(col7(4)), ALU.subtract).then_inc(lsub_ready, 1)

            share_link = chain(share_step, 9)

            def shares(g):
                dve.wait_ge(ex_ready, g + 1)
                ex = lg[:, 1, :, :]
                share_link(v.tensor_reduce(col7(4), ex, AX.X, ALU.add), g)
                share_link(v.reciprocal(col7(4), col7(4)), g)
                share_link(v.tensor_tensor(ex, ex, wide(col7(4)), ALU.mult), g)
                v.sem_inc(tail_turn, 1)
                for j in range(TBLK):
                    last = v.max(top8[:, j, :], lg[:, 1, j, :])
                share_link(last, g)
                v.sem_inc(tail_turn, 1)
                for j in range(TBLK):
                    last = v.max_index(idx8[:, j, :], top8[:, j, :], lg[:, 1, j, :])
                share_link(last, g)
                share_link(v.tensor_tensor(col7(5), top8[:, :, 0], top8[:, :, 1], ALU.add), g)
                share_link(v.tensor_scalar(col7(5), col7(5), 1e-12, None, ALU.max), g)
                share_link(v.reciprocal(col7(5), col7(5)), g)
                for r in range(TOP_K):
                    v.tensor_copy(expert_f[:, r, ds(g * TBLK, TBLK)], idx8[:, :, r])
                    last = v.tensor_tensor(share[:, r, ds(g * TBLK, TBLK)], top8[:, :, r], col7(5), ALU.mult)
                share_link(last, g)

            dve.wait_ge(added, 2 * CHUNKS)
            half_diffs(0)
            diffs(0)
            half_diffs(1)
            norm(0, 0, 0)
            diffs(1)
            scale(0, True)
            half_diffs(2)
            with dve.Fori(0, (TGRP - 3) // 2) as i:
                for u in (1, 2):
                    g = 2 * i + u
                    norm(g, u % 2, i + u // 2)
                    diffs(g + 1)
                    scale(g)
                    less_peak(g - 1)
                    half_diffs(g + 2)
                    shares(g - 1)
            norm(TGRP - 2, (TGRP - 2) % 2, (TGRP - 2) // 2)
            diffs(TGRP - 1)
            scale(TGRP - 2)
            less_peak(TGRP - 3)
            shares(TGRP - 3)
            norm(TGRP - 1, (TGRP - 1) % 2, (TGRP - 1) // 2)
            scale(TGRP - 1)
            less_peak(TGRP - 2)
            shares(TGRP - 2)
            less_peak(TGRP - 1)
            shares(TGRP - 1)

            chosen = expert_f[:, :, :].rearrange("p r t -> p (r t)")
            step(v.tensor_tensor(pmask, chosen.unsqueeze(1).to_broadcast([P, N_EXP, PICKS]),
                                 iota8_f[:, :].unsqueeze(2).to_broadcast([P, N_EXP, PICKS]), ALU.is_equal))
            v.tensor_reduce(c8[:, 0, 0:N_EXP], pmask, AX.X, ALU.add).then_inc(pcounts_ready, 1)
            dve.wait_ge(ptotals_done, 1)
            step(v.tensor_scalar(c8_i[:, :], bank[1][:, 0:N_EXP], float(P - 1), None, ALU.add))
            step(v.tensor_scalar(c8_i[:, :], c8_i[:, :], 7, None, ALU.arith_shift_right))
            step(v.tensor_copy(c8[:, 1, 0:N_EXP], c8_i[:, :]))
            step(v.memset(c8[:, 2, 0:1], 0.0))
            step(v.tensor_tensor_scan(c8[:, 2, 1:N_EXP + 1], c8[:, 1, 0:N_EXP], c8[:, 1, 0:N_EXP], 0.0, ALU.add, ALU.max))
            step(v.scalar_tensor_tensor(c8[:, 3, 0:N_EXP], c8[:, 2, 0:N_EXP], float(P), bank[0][:, 0:N_EXP],
                                        ALU.mult, ALU.add))
            step(v.tensor_tensor(c8[:, 0, 0:N_EXP], kpos_f[:, 0:1].to_broadcast([P, N_EXP]), c8[:, 2, 0:N_EXP], ALU.is_ge))
            step(v.tensor_reduce(ct_f[:, :], c8[:, 0, 0:N_EXP], AX.X, ALU.add))
            v.tensor_scalar(ct_i[:, :], ct_f[:, :], -1.0, float(N_EXP - 1), ALU.add, ALU.min).then_inc(ct_ready, 1)
            for e in range(N_EXP):
                last = v.tensor_tensor_scan(pscan[:, e, :], pmask[:, e, :], pmask[:, e, :], c8[:, 3, e:e + 1],
                                            ALU.add, ALU.max)
            step(last)
            step(v.tensor_tensor(pscan, pscan, pmask, ALU.mult))
            step(v.tensor_reduce(pick_pos[:, 0, :], pscan.rearrange("p e c -> p c e"), AX.X, ALU.add))
            step(v.tensor_scalar(pick_row, pick_pos[:, 0, :], -1.0, None, ALU.add))
            step(v.tensor_scalar(pick_tmp, pick_row, 7, None, ALU.arith_shift_right))
            step(v.tensor_copy(pick_pos[:, 1, :], pick_tmp))
            step(v.tensor_scalar(pick_tmp, pick_row, P - 1, None, ALU.bitwise_and))
            step(v.tensor_copy(pick_pos[:, 2, :], pick_tmp))
            step(v.memset(exp_row[:, 0:EXP_TURN], 0))
            v.sem_inc(pk_order, 1)
            step(v.tensor_scalar(pick_bits, iota_h[:, 0:PICKS], float(P), float(COL_BIAS), ALU.mult, ALU.add))
            step(v.tensor_scalar(pick_bits, pick_bits, kpos_f[:, 0:1], None, ALU.add))
            step(v.tensor_scalar(pick_bits, pick_bits, 16, None, ALU.logical_shift_left))
            step(v.tensor_scalar(pad_place, iota_h[:, 0:EXP_CHUNKS], float(P), float(PICKS * P + COL_BIAS), ALU.mult, ALU.add))
            step(v.tensor_scalar(pad_place, pad_place, kpos_f[:, 0:1], None, ALU.add))

            def pick_one_hots(g, first):
                for s in range(slots):
                    j, r = s // TOP_K, s % TOP_K
                    t = g * TBLK + j
                    c = ds(r * BLOCKS + t, 1)
                    if not first:
                        dve.wait_ge(pk_done, slots * (g - 1) + s + 1)
                    v.tensor_scalar(pk_hi[:, s, :], iota_h[:, 0:EXP_CHUNKS], pick_pos[:, 1, c], None, ALU.is_equal)
                    v.tensor_scalar(pk_lo[:, s, :], iota_h[:, 0:P], pick_pos[:, 2, c], pick_bits.bitcast(f32)[:, c],
                                    ALU.is_equal, ALU.mult).then_inc(pk_ready, 1)

            pick_one_hots(0, True)
            with dve.Fori(1, TGRP) as g:
                pick_one_hots(g, False)
            dve.wait_ge(pk_done, PICKS + 1)
            step(v.tensor_copy(tok_sorted.bitcast(f32), bank[2][:, 0:EXP_CHUNKS]))
            step(v.tensor_scalar(tok_sorted, tok_sorted, 16, None, ALU.logical_shift_right))
            step(v.tensor_scalar(id_f, tok_sorted, float(-COL_BIAS), None, ALU.add))
            step(v.tensor_scalar(id_t, id_f, float(BLOCKS * P), float(-BLOCKS * P), ALU.is_ge, ALU.mult))
            step(v.tensor_tensor(id_t, id_t, id_f, ALU.add))
            step(v.tensor_scalar(tok_sorted, id_t, 0.0, None, ALU.max))
            v.sem_inc(picks_ready, 1)
            step(v.scalar_tensor_tensor(id_t, id_f, 0.0, pad_place, ALU.is_lt, ALU.mult))
            v.tensor_tensor(place_sorted, id_t, id_f, ALU.add).then_inc(places_ready, 1)

            def prepare(m, par, e):
                if not (isinstance(m, int) and m < 2):
                    dve.wait_ge(l1_done, m - 1)
                    dve.wait_ge(gelu_done, 2 * (m - 1))
                v.tensor_copy(b1_cur[:, par, :], b1_all[:, ds(e, 1), :].rearrange("p a k -> p (a k)"))
                v.tensor_copy(w1_cur[:, par, :], w1_sb[:, ds(e, 1), :, :].rearrange("p a k f -> p (a k f)"))\
                    .then_inc(w1_ready, 1)
                dve.wait_ge(t1_done, m + 1)
                v.tensor_copy(xcT[:, par, :], bank[par][:, 0:D]).then_inc(xcT_ready, 1)

            def add_b2(m, slot, turn, e):
                dve.wait_ge(l2_done, m + 1)
                if turn is not None:
                    dve.wait_ge(y_stored[slot], 16 * turn)
                v.tensor_tensor(yc[:, slot, :], bank[6 + slot % 2][:, 0:D],
                                rows[:, ds(e, 1), D:2 * D].rearrange("p a d -> p (a d)"), ALU.add).then_inc(y_ready, 1)

            def chunk_experts(i):
                _, e = nc.values_load_multi_w_load_instructions(
                    exp_row[0:1, ds(EXP_TURN * i, 2 * EXP_TURN)], engines=[mybir.EngineType.DVE],
                    min_val=0, max_val=N_EXP - 1,
                    skip_runtime_bounds_check_because="the table is clamped to 0..N_EXP-1 when it is made")
                return e

            def expert_turn(i, e, first, steps=EXP_TURN):
                for u in range(steps):
                    m = EXP_TURN * i + u
                    if steps == EXP_TURN:
                        prepare(m, u % 2, e[EXP_TURN + u])
                    if not first or u >= 3:
                        slot = (u - 3) % EXP_TURN
                        used = i if u >= 3 else i - 1
                        never = isinstance(used, int) and used == 0
                        add_b2(m - 3, slot, None if never else used, e[EXP_TURN + u - 3])

            dve.wait_ge(ct_loaded, 16)
            dve.wait_ge(bias_loaded, 16 * N_EXP)
            expert_turn(0, chunk_experts(0), True)
            expert_turn(1, chunk_experts(1), False)
            with dve.Fori(2, EXP_CHUNKS // EXP_TURN) as i:
                expert_turn(i, chunk_experts(i), False)
            expert_turn(EXP_CHUNKS // EXP_TURN, chunk_experts(EXP_CHUNKS // EXP_TURN), False, steps=3)

            def combine(g, par, turn):
                for r in range(TOP_K):
                    dve.wait_ge(yg_in[par][r], 16 * (turn + 1))
                    for j in range(TBLK):
                        t = g * TBLK + j
                        if r:
                            dve.wait_ge(combined, 2 * TBLK * g + j + 1)
                        row = rows[:, ds(t, 1), 0:D].rearrange("p a d -> p (a d)")
                        v.scalar_tensor_tensor(row, yg[par][:, r, j, :], share[:, r, ds(t, 1)], row,
                                               ALU.mult, ALU.add).then_inc(combined, 1)
                dve.wait_ge(combined, 2 * TBLK * (g + 1))
                v.sem_inc(grp_done, 1)

            with dve.Fori(0, TGRP // 2) as i:
                for par in range(2):
                    combine(2 * i + par, par, i)
            combine(TGRP - 1, 0, TGRP // 2)

        @block.tensor
        def _(pe):
            mm = nc.tensor.matmul
            pe.wait_ge(consts, 1)
            pe.wait_ge(counts_ready, 1)
            mm(bank[0][:, 0:BLOCKS], upper[:, :], counts[:, :], start=True, stop=True)
            mm(bank[1][:, 0:BLOCKS], ones[:, :], counts[:, :], start=True, stop=True).then_inc(totals_done, 1)

            def transposes(t, par, early=False):
                pe.wait_ge(xn_done, t + 1)
                if not early:
                    pe.wait_ge(tr_copied, t - 1)
                for k in range(2):
                    last = nc.tensor.transpose(bank[6 + par][:, k * P:(k + 1) * P], xn[:, par, k * P:(k + 1) * P],
                                               ident[:, :])
                last.then_inc(tr_done, 1)

            def multiply_xn(t, par, early=False):
                pe.wait_ge(tr_copied, t + 1)
                if not early:
                    pe.wait_ge(xw_made, t - 1)
                left = xnT[:, par, :].rearrange("p (k r) -> p k r", k=2)
                mm(bank[par], left[:, 0, :], wrn_sb[:, 0, :], start=True, stop=False)
                mm(bank[par], left[:, 1, :], wrn_sb[:, 1, :], start=False, stop=True).then_inc(xw_done, 1)

            pe.wait_ge(w_gnn, 16 * 4)
            pe.wait_ge(blk_ready, 1)
            transposes(0, 0, True)
            transposes(1, 1, True)
            multiply_xn(0, 0, True)
            transposes(2, 0)
            multiply_xn(1, 1, True)
            with pe.Fori(1, BLOCKS // 2) as i:
                transposes(2 * i + 1, 1)
                multiply_xn(2 * i, 0)
                transposes(2 * i + 2, 0)
                multiply_xn(2 * i + 1, 1)
            multiply_xn(BLOCKS - 1, 0)
            pe.wait_ge(xw_made, BLOCKS)
            pe.wait_ge(pairs_ready, 1)

            def zero(start):
                for b in range(4):
                    last = mm(bank[b][:, 0:HALF], zero_bf[:, 0:P], zero_bf[:, :], start=start, stop=not start)
                return last

            zero(True)

            def sort(i):
                for u in range(IN_UNROLL):
                    pe.wait_ge(oh_ready, i * IN_UNROLL + u + 1)
                    for n in range(2):
                        for half in range(2):
                            last = mm(bank[2 * n + half][:, 0:HALF], lo_pay[:, u, n, :],
                                      hi_oh[:, u, half * HALF:(half + 1) * HALF], start=False, stop=False)
                    last.then_inc(sorted_cols, 1)

            sort(0)
            with pe.Fori(1, (IN_COLS - POOL_COLS) // IN_UNROLL) as i:
                sort(i)
            zero(False).then_inc(sorted_cols, 1)

            def multiply_turn(i, base, width, ready, first):
                for s in range(TURN):
                    k = base + TURN * i + s
                    pe.wait_ge(oh_made, made[0] + TURN * i + s + 1)
                    if not (first and s < ACC_BUFS):
                        pe.wait_ge(added, k - ACC_BUFS + 1)
                    if ready is None:
                        pe.wait_ge(gathered[s], 16 * (i + 1))
                    else:
                        pe.wait_ge(squared, TURN * i + s + 1)
                    mm(bank[s % ACC_BUFS][:, 0:width], onehot[:, s // GROUP, s % GROUP, :], ring[:, s, 0:width],
                       start=True, stop=True).then_inc(mult_done, 1)

            made = [0]

            def multiply_pass(base, width, ready):
                multiply_turn(0, base, width, ready, base == 0)
                with pe.Fori(1, CHUNKS // TURN) as i:
                    multiply_turn(i, base, width, ready, False)

            multiply_pass(0, D + 1, None)

            made[0] = CHUNKS + TURN
            multiply_pass(CHUNKS, 2 * D, squared)

            def transpose_x2(g, first=False):
                pe.wait_ge(x2_ready, TBLK * (g + 1))
                for r in range(4):
                    if not (first and r < 2):
                        pe.wait_ge(xt_copied, 4 * g + r - 1)
                    for n in range(4 * r, min(4 * r + 4, 2 * TBLK)):
                        k, j = n // TBLK, n % TBLK
                        last = nc.tensor.transpose(bank[4 + r % 2][:, (n % 4) * P:(n % 4 + 1) * P],
                                                   x2g[:, j, k * P:(k + 1) * P], ident[:, :])
                    last.then_inc(xt_done, 1)

            def route(g, first=False):
                pe.wait_ge(xt_copied, 4 * (g + 1))
                if not first:
                    pe.wait_ge(lsub_ready, g)
                for j in range(TBLK):
                    for k in range(2):
                        last = mm(bank[6][:, j * N_EXP:(j + 1) * N_EXP], xT[:, k, j * P:(j + 1) * P], rw_sb[:, k, :],
                                  start=(k == 0), stop=(k == 1))
                last.then_inc(lg_done, 1)

            pe.wait_ge(w_ffn, 16 * 8)
            transpose_x2(0, True)
            route(0, True)
            with pe.Fori(1, TGRP) as g:
                transpose_x2(g)
                route(g)
            pe.wait_ge(pcounts_ready, 1)
            mm(bank[0][:, 0:N_EXP], upper[:, :], c8[:, 0, 0:N_EXP], start=True, stop=True)
            mm(bank[1][:, 0:N_EXP], ones[:, :], c8[:, 0, 0:N_EXP], start=True, stop=True).then_inc(ptotals_done, 1)
            mm(bank[2][:, 0:EXP_CHUNKS], zero_bf[:, 0:P], zero_bf[:, 0:EXP_CHUNKS], start=True, stop=False)
            with pe.Fori(0, TGRP) as g:
                for s in range(slots):
                    pe.wait_ge(pk_ready, slots * g + s + 1)
                    mm(bank[2][:, 0:EXP_CHUNKS], pk_lo[:, s, :], pk_hi[:, s, :], start=False, stop=False)\
                        .then_inc(pk_done, 1)
            mm(bank[2][:, 0:EXP_CHUNKS], zero_bf[:, 0:P], zero_bf[:, 0:EXP_CHUNKS], start=False, stop=True)\
                .then_inc(pk_done, 1)

            def flip(m, u, i):
                pe.wait_ge(xc_in[u], 16 * (i + 1))
                if not (isinstance(m, int) and m < 2):
                    pe.wait_ge(xcT_ready, m - 1)
                for k in range(2):
                    last = nc.tensor.transpose(bank[u % 2][:, k * P:(k + 1) * P], xc[:, u, k * P:(k + 1) * P], ident[:, :])
                last.then_inc(t1_done, 1)

            def first_layer(m, par):
                pe.wait_ge(w1_ready, m + 1)
                pe.wait_ge(xcT_ready, m + 1)
                if not (isinstance(m, int) and m < 2):
                    pe.wait_ge(gelu_done, 2 * (m - 1))
                for f in range(2):
                    for k in range(2):
                        last = mm(bank[2 + par][:, f * P:(f + 1) * P], w1_cur[:, par, k * D + f * P:k * D + (f + 1) * P],
                                  xcT[:, par, k * P:(k + 1) * P], start=(k == 0), stop=(k == 1))
                last.then_inc(l1_done, 1)

            def second_layer(m, par, e):
                pe.wait_ge(gelu_done, 2 * (m + 1))
                if not (isinstance(m, int) and m < 2):
                    pe.wait_ge(y_ready, m - 1)
                for k in range(2):
                    last = mm(bank[6 + par][:, 0:D], hidT[:, par, k * P:(k + 1) * P],
                              w2_sb[:, ds(e, 1), k, :].rearrange("p a d -> p (a d)"), start=(k == 0), stop=(k == 1))
                last.then_inc(l2_done, 1)

            def expert_turn(i, first, steps=EXP_TURN):
                _, e = nc.values_load_multi_w_load_instructions(
                    exp_row[0:1, ds(EXP_TURN * i, 2 * EXP_TURN)], engines=[mybir.EngineType.PE],
                    min_val=0, max_val=N_EXP - 1,
                    skip_runtime_bounds_check_because="the table is clamped to 0..N_EXP-1 when it is made")
                for u in range(steps):
                    m = EXP_TURN * i + u
                    if steps == EXP_TURN:
                        flip(m, u, i)
                    if (not first or u >= 1) and (steps == EXP_TURN or u < 1):
                        first_layer(m - 1, (u - 1) % 2)
                    if not first or u >= 2:
                        second_layer(m - 2, u % 2, e[EXP_TURN + u - 2])

            pe.wait_ge(ct_loaded, 16)
            pe.wait_ge(pk_order, 1)
            expert_turn(0, True)
            with pe.Fori(1, EXP_CHUNKS // EXP_TURN) as i:
                expert_turn(i, False)
            expert_turn(EXP_CHUNKS // EXP_TURN, False, steps=2)


_INS = ['x', 'src', 'dst', 'L0_gnn_W_root', 'L0_gnn_W_neigh', 'L0_gnn_b', 'L0_ffn_router_w', 'L0_ffn_w1',
        'L0_ffn_b1', 'L0_ffn_w2', 'L0_ffn_b2']


def kernel(**inputs):
    import numpy as _np
    import concourse.bacc as _bacc
    from concourse import mybir as _mybir
    from concourse.bass_utils import run_bass_kernel_spmd as _run

    nc = _bacc.Bacc("TRN2", target_bir_lowering=False, num_devices=1)
    arrays, args = {}, []
    for name in _INS:
        a = _np.ascontiguousarray(inputs[name])
        arrays[f"in_{name}"] = a
        args.append(nc.dram_tensor(f"in_{name}", a.shape, _mybir.dt.from_np(a.dtype), kind="ExternalInput").ap())
    args.append(nc.dram_tensor("out_0", (N_NODES, D), _mybir.dt.float32, kind="ExternalOutput").ap())
    gnn_moe(nc, *args)
    r = _run(nc, [arrays], core_ids=[0])
    return r.results[0]["out_0"]
```
